# Optimizing a Trainium2 kernel written in Bass

```python
import numpy as np
import jax
import jax.numpy as jnp

def _softmax(x, axis=-1):
    return jax.nn.softmax(x, axis=axis)

def _gelu(x):
    return jax.nn.gelu(x, approximate=True)

def _silu(x):
    return jax.nn.silu(x)

def _sigmoid(x):
    return jax.nn.sigmoid(x)

def _layernorm(x, axis=-1, eps=1e-05):
    m = jnp.mean(x, axis=axis, keepdims=True)
    v = jnp.var(x, axis=axis, keepdims=True)
    return (x - m) / jnp.sqrt(v + eps)

def _scatter_add(tgt, idx, src, axis=0):
    return tgt.at[idx].add(src)

def _segment_sum(src, seg, n):
    return jax.ops.segment_sum(src, seg, n)
kernel_name = 'mk_adaln_ffn_d2_seqx_r4_14c0d7'

def setup_inputs(seed: int=0):
    np.random.seed(seed)
    _w = jnp.asarray

    def _rec_inputs():
        import jax
        import jax.numpy as jnp
        _rk = jax.random.key(seed)
        x = -0.0002071 + 1 * jax.random.normal(jax.random.fold_in(_rk, 1), (8, 256, 256), jnp.float32)
        _lenS = 256 - jax.random.randint(jax.random.fold_in(_rk, 7), (8,), 0, max(1, 256 // 4) + 1, jnp.int32)
        _lenS2 = 256 - jax.random.randint(jax.random.fold_in(_rk, 8), (8,), 0, max(1, 256 // 4) + 1, jnp.int32)
        cond_8 = jax.random.uniform(jax.random.fold_in(_rk, 11), (8, 8), jnp.float32, 0.0, 0.983423)
        return (x, cond_8)
    x, cond_8 = _rec_inputs()

    def _L0_cond_setup():
        import jax, jax.numpy as jnp
        import numpy as np
        R = 16
        ALPHA = 32.0
        SCALING = ALPHA / R
        key = jax.random.key(seed)
        ks = jax.random.split(key, 6)
        B, T, C, O, E = (16, 375, 256, 256, 8)
        x = jax.random.normal(ks[0], (B, T, C), dtype=jnp.float32)
        w = jax.random.uniform(ks[1], (B, E), dtype=jnp.float32)
        W_base = jax.random.normal(ks[2], (O, C), dtype=jnp.float32) * 0.02
        b_base = jax.random.normal(ks[3], (O,), dtype=jnp.float32) * 0.02
        As = jax.random.normal(ks[4], (E, R, C), dtype=jnp.float32) * 0.02
        Bs = jax.random.normal(ks[5], (E, O, R), dtype=jnp.float32) * 0.02
        return {'x': x, 'w': w, 'W_base': W_base, 'b_base': b_base, 'As': As, 'Bs': Bs}
    _L0_cond_all = _L0_cond_setup()
    _L0_cond_in = {k: v for k, v in _L0_cond_all.items() if k in ('W_base', 'b_base', 'As', 'Bs')}
    del _L0_cond_all

    def _L0_ffn_setup():
        import jax, jax.numpy as jnp
        import numpy as np
        from jax.scipy.linalg import expm
        D = 256
        E = 6
        K = 2
        H = 2 * D
        A4 = 4 * D
        NROT = 4
        LN_EPS = 1e-05

        def _xavier(key, shape):
            fan_in, fan_out = (shape[-2], shape[-1])
            lim = np.sqrt(6.0 / (fan_in + fan_out))
            return jax.random.uniform(key, shape, jnp.float32, -lim, lim)

        def _layernorm(x, g, b):
            mu = jnp.mean(x, axis=-1, keepdims=True)
            var = jnp.var(x, axis=-1, keepdims=True)
            return (x - mu) * jax.lax.rsqrt(var + LN_EPS) * g + b

        def _moe(xn, gate_w, gate_b, ew1, eb1, ew2, eb2):
            logits = xn @ gate_w + gate_b
            tw, ti = jax.lax.top_k(logits, K)
            tw = jax.nn.softmax(tw, axis=-1)
            w_full = jnp.sum(tw[..., None] * jax.nn.one_hot(ti, E, dtype=tw.dtype), axis=-2)
            h = jax.nn.gelu(jnp.einsum('bsd,edh->besh', xn, ew1) + eb1[None, :, None, :], approximate=False)
            eo = jnp.einsum('besh,ehd->besd', h, ew2) + eb2[None, :, None, :]
            return jnp.einsum('bse,besd->bsd', w_full, eo)

        def _rotate(x, gens):
            for i in range(NROT):
                x = x @ expm(gens[i])
            return x
        key = jax.random.key(seed)
        ks = jax.random.split(key, 16)
        x = jax.random.normal(ks[0], (4, 512, D), jnp.float32)
        gens_raw = _xavier(ks[1], (NROT, D, D))
        gens = 0.5 * (gens_raw - jnp.swapaxes(gens_raw, -1, -2))
        return {'x': x, 'ln_g': jnp.ones((D,), jnp.float32), 'ln_b': jnp.zeros((D,), jnp.float32), 'aw1': _xavier(ks[2], (D, A4)), 'ab1': jnp.zeros((A4,), jnp.float32), 'aw2': _xavier(ks[3], (A4, D)), 'ab2': jnp.zeros((D,), jnp.float32), 'gate_w': _xavier(ks[4], (D, E)), 'gate_b': jnp.zeros((E,), jnp.float32), 'ew1': _xavier(ks[5], (E, D, H)), 'eb1': jnp.zeros((E, H), jnp.float32), 'ew2': _xavier(ks[6], (E, H, D)), 'eb2': jnp.zeros((E, D), jnp.float32), 'gens': gens, 'gc_w': _xavier(ks[7], (2 * D, 1)), 'gc_b': jnp.zeros((1,), jnp.float32)}
    _L0_ffn_all = _L0_ffn_setup()
    _L0_ffn_in = {k: v for k, v in _L0_ffn_all.items() if k in ('ln_g', 'ln_b', 'aw1', 'ab1', 'aw2', 'ab2', 'gate_w', 'gate_b', 'ew1', 'eb1', 'ew2', 'eb2', 'gens', 'gc_w', 'gc_b')}
    del _L0_ffn_all

    def _L1_cond_setup():
        import jax, jax.numpy as jnp
        import numpy as np
        key = jax.random.key(seed)
        k1, k2, k3, k4, k5 = jax.random.split(key, 5)
        B, N, T, O, G = (32, 64, 256, 256, 8)
        x = jax.random.normal(k1, (B, N, T), dtype=jnp.float32)
        y = jax.random.uniform(k2, (B, G), dtype=jnp.float32)
        weight = jax.random.normal(k3, (G, O, T), dtype=jnp.float32) * (1.0 / np.sqrt(T))
        mask = jax.random.uniform(k4, (O, T), dtype=jnp.float32)
        bias = jax.random.normal(k5, (O,), dtype=jnp.float32)
        return {'x': x, 'y': y, 'weight': weight, 'mask': mask, 'bias': bias}
    _L1_cond_all = _L1_cond_setup()
    _L1_cond_in = {k: v for k, v in _L1_cond_all.items() if k in ('weight', 'mask', 'bias')}
    del _L1_cond_all

    def _L1_ffn_setup():
        import jax, jax.numpy as jnp
        import numpy as np
        D_MODEL = 256
        HIDDEN = 512
        E_ROUTED = 14
        E_SHARED = 2
        TOP_K = 2
        EPS = 1e-09
        RMS_EPS = 1.1920929e-07

        def _ffn(xn, rw, W1, W2):
            ms = jnp.mean(xn * xn, axis=-1, keepdims=True)
            h = xn * jax.lax.rsqrt(ms + RMS_EPS) * rw
            return jax.nn.silu(h @ W1) @ W2
        key = jax.random.key(seed)
        ks = jax.random.split(key, 9)
        B, T = (2, 256)
        x = jax.random.normal(ks[0], (B, T, D_MODEL), dtype=jnp.float32)
        router_w = jax.random.normal(ks[1], (D_MODEL, E_ROUTED), dtype=jnp.float32) * 0.006
        rms_w = jnp.ones((E_ROUTED, D_MODEL), dtype=jnp.float32)
        w1 = jax.random.normal(ks[2], (E_ROUTED, D_MODEL, HIDDEN), dtype=jnp.float32) * 0.02
        w2 = jax.random.normal(ks[3], (E_ROUTED, HIDDEN, D_MODEL), dtype=jnp.float32) * 0.02
        rms_w_s = jnp.ones((E_SHARED, D_MODEL), dtype=jnp.float32)
        w1_s = jax.random.normal(ks[4], (E_SHARED, D_MODEL, HIDDEN), dtype=jnp.float32) * 0.02
        w2_s = jax.random.normal(ks[5], (E_SHARED, HIDDEN, D_MODEL), dtype=jnp.float32) * 0.02
        return {'x': x, 'router_w': router_w, 'rms_w': rms_w, 'w1': w1, 'w2': w2, 'rms_w_s': rms_w_s, 'w1_s': w1_s, 'w2_s': w2_s}
    _L1_ffn_all = _L1_ffn_setup()
    _L1_ffn_in = {k: v for k, v in _L1_ffn_all.items() if k in ('router_w', 'rms_w', 'w1', 'w2', 'rms_w_s', 'w1_s', 'w2_s')}
    del _L1_ffn_all
    return {'x': x, 'cond_8': cond_8, 'L0_cond_W_base': _L0_cond_in['W_base'], 'L0_cond_b_base': _L0_cond_in['b_base'], 'L0_cond_As': _L0_cond_in['As'], 'L0_cond_Bs': _L0_cond_in['Bs'], 'L0_ffn_ln_g': _L0_ffn_in['ln_g'], 'L0_ffn_ln_b': _L0_ffn_in['ln_b'], 'L0_ffn_aw1': _L0_ffn_in['aw1'], 'L0_ffn_ab1': _L0_ffn_in['ab1'], 'L0_ffn_aw2': _L0_ffn_in['aw2'], 'L0_ffn_ab2': _L0_ffn_in['ab2'], 'L0_ffn_gate_w': _L0_ffn_in['gate_w'], 'L0_ffn_gate_b': _L0_ffn_in['gate_b'], 'L0_ffn_ew1': _L0_ffn_in['ew1'], 'L0_ffn_eb1': _L0_ffn_in['eb1'], 'L0_ffn_ew2': _L0_ffn_in['ew2'], 'L0_ffn_eb2': _L0_ffn_in['eb2'], 'L0_ffn_gens': _L0_ffn_in['gens'], 'L0_ffn_gc_w': _L0_ffn_in['gc_w'], 'L0_ffn_gc_b': _L0_ffn_in['gc_b'], 'L1_cond_weight': _L1_cond_in['weight'], 'L1_cond_mask': _L1_cond_in['mask'], 'L1_cond_bias': _L1_cond_in['bias'], 'L1_ffn_router_w': _L1_ffn_in['router_w'], 'L1_ffn_rms_w': _L1_ffn_in['rms_w'], 'L1_ffn_w1': _L1_ffn_in['w1'], 'L1_ffn_w2': _L1_ffn_in['w2'], 'L1_ffn_rms_w_s': _L1_ffn_in['rms_w_s'], 'L1_ffn_w1_s': _L1_ffn_in['w1_s'], 'L1_ffn_w2_s': _L1_ffn_in['w2_s']}

def reference(x, cond_8, L0_cond_W_base, L0_cond_b_base, L0_cond_As, L0_cond_Bs, L0_ffn_ln_g, L0_ffn_ln_b, L0_ffn_aw1, L0_ffn_ab1, L0_ffn_aw2, L0_ffn_ab2, L0_ffn_gate_w, L0_ffn_gate_b, L0_ffn_ew1, L0_ffn_eb1, L0_ffn_ew2, L0_ffn_eb2, L0_ffn_gens, L0_ffn_gc_w, L0_ffn_gc_b, L1_cond_weight, L1_cond_mask, L1_cond_bias, L1_ffn_router_w, L1_ffn_rms_w, L1_ffn_w1, L1_ffn_w2, L1_ffn_rms_w_s, L1_ffn_w1_s, L1_ffn_w2_s):
    import jax
    import jax.numpy as jnp

    def _L0_cond_ref(x, w, W_base, b_base, As, Bs):
        import jax, jax.numpy as jnp
        import numpy as np
        R = 16
        ALPHA = 32.0
        SCALING = ALPHA / R
        out = jnp.einsum('btc,oc->bto', x, W_base) + b_base
        h = jnp.einsum('btc,erc->bter', x, As)
        lora = jnp.einsum('bter,eor,be->bto', h, Bs, w)
        return out + lora * SCALING

    def _L0_ffn_ref(x, ln_g, ln_b, aw1, ab1, aw2, ab2, gate_w, gate_b, ew1, eb1, ew2, eb2, gens, gc_w, gc_b):
        import jax, jax.numpy as jnp
        import numpy as np
        from jax.scipy.linalg import expm
        D = 256
        E = 6
        K = 2
        H = 2 * D
        A4 = 4 * D
        NROT = 4
        LN_EPS = 1e-05

        def _xavier(key, shape):
            fan_in, fan_out = (shape[-2], shape[-1])
            lim = np.sqrt(6.0 / (fan_in + fan_out))
            return jax.random.uniform(key, shape, jnp.float32, -lim, lim)

        def _layernorm(x, g, b):
            mu = jnp.mean(x, axis=-1, keepdims=True)
            var = jnp.var(x, axis=-1, keepdims=True)
            return (x - mu) * jax.lax.rsqrt(var + LN_EPS) * g + b

        def _moe(xn, gate_w, gate_b, ew1, eb1, ew2, eb2):
            logits = xn @ gate_w + gate_b
            tw, ti = jax.lax.top_k(logits, K)
            tw = jax.nn.softmax(tw, axis=-1)
            w_full = jnp.sum(tw[..., None] * jax.nn.one_hot(ti, E, dtype=tw.dtype), axis=-2)
            h = jax.nn.gelu(jnp.einsum('bsd,edh->besh', xn, ew1) + eb1[None, :, None, :], approximate=False)
            eo = jnp.einsum('besh,ehd->besd', h, ew2) + eb2[None, :, None, :]
            return jnp.einsum('bse,besd->bsd', w_full, eo)

        def _rotate(x, gens):
            for i in range(NROT):
                x = x @ expm(gens[i])
            return x
        residual = x
        xn = _layernorm(x, ln_g, ln_b)
        abel = jax.nn.gelu(xn @ aw1 + ab1, approximate=False) @ aw2 + ab2
        nonabel = _rotate(_moe(xn, gate_w, gate_b, ew1, eb1, ew2, eb2), gens)
        combined = jnp.concatenate([abel, nonabel], axis=-1)
        gate = jax.nn.sigmoid(combined @ gc_w + gc_b)
        mixed = abel * (1.0 - gate) + nonabel * gate
        return residual + mixed

    def _L1_cond_ref(x, y, weight, mask, bias):
        import jax, jax.numpy as jnp
        import numpy as np
        masked_w = weight * mask[None, :, :]
        w_bot = jnp.einsum('bg,got->bot', y, masked_w)
        return jnp.einsum('bnt,bot->bno', x, w_bot) + bias

    def _L1_ffn_ref(x, router_w, rms_w, w1, w2, rms_w_s, w1_s, w2_s):
        import jax, jax.numpy as jnp
        import numpy as np
        D_MODEL = 256
        HIDDEN = 512
        E_ROUTED = 14
        E_SHARED = 2
        TOP_K = 2
        EPS = 1e-09
        RMS_EPS = 1.1920929e-07

        def _ffn(xn, rw, W1, W2):
            ms = jnp.mean(xn * xn, axis=-1, keepdims=True)
            h = xn * jax.lax.rsqrt(ms + RMS_EPS) * rw
            return jax.nn.silu(h @ W1) @ W2
        B, T, D = x.shape
        N = B * T
        xf = x.reshape(N, D)
        gates = jax.nn.softmax(xf @ router_w, axis=-1)
        top_v, top_i = jax.lax.top_k(gates, TOP_K)
        masked = jnp.zeros_like(gates).at[jnp.arange(N)[:, None], top_i].set(top_v)
        masked = masked / (masked.sum(axis=-1, keepdims=True) + EPS)
        routed = jax.vmap(lambda rw_, W1_, W2_: _ffn(xf, rw_, W1_, W2_))(rms_w, w1, w2)
        routed_out = jnp.einsum('end,ne->nd', routed, masked)
        shared = jax.vmap(lambda rw_, W1_, W2_: _ffn(xf, rw_, W1_, W2_))(rms_w_s, w1_s, w2_s).sum(0)
        return (routed_out + shared).reshape(B, T, D)
    x = x + _L0_ffn_ref(_L0_cond_ref(x, cond_8, L0_cond_W_base, L0_cond_b_base, L0_cond_As, L0_cond_Bs), L0_ffn_ln_g, L0_ffn_ln_b, L0_ffn_aw1, L0_ffn_ab1, L0_ffn_aw2, L0_ffn_ab2, L0_ffn_gate_w, L0_ffn_gate_b, L0_ffn_ew1, L0_ffn_eb1, L0_ffn_ew2, L0_ffn_eb2, L0_ffn_gens, L0_ffn_gc_w, L0_ffn_gc_b)
    x = x + _L1_ffn_ref(_L1_cond_ref(x, cond_8, L1_cond_weight, L1_cond_mask, L1_cond_bias), L1_ffn_router_w, L1_ffn_rms_w, L1_ffn_w1, L1_ffn_w2, L1_ffn_rms_w_s, L1_ffn_w1_s, L1_ffn_w2_s)
    return x

_drawn_inputs = setup_inputs


def setup_inputs(seed=0):
    import zlib

    import numpy as np

    out = dict(_drawn_inputs(seed))
    spreads = {'L0_ffn_ln_g': (1.0, 0.2),
     'L0_ffn_ln_b': (0.0, 0.1),
     'L0_ffn_ab1': (0.0, 0.1),
     'L0_ffn_ab2': (0.0, 0.1),
     'L0_ffn_gate_b': (0.0, 0.1),
     'L0_ffn_eb1': (0.0, 0.1),
     'L0_ffn_eb2': (0.0, 0.1),
     'L1_ffn_rms_w': (1.0, 0.6),
     'L1_ffn_rms_w_s': (1.0, 0.6)}
    factors = {}
    for name, (base, spread) in spreads.items():
        noise = np.random.default_rng([zlib.crc32(name.encode()), seed]).standard_normal(out[name].shape)
        drawn = base * np.exp(spread * noise) if base else spread * noise
        out[name] = jnp.asarray(drawn.astype(out[name].dtype))
    for name, factor in factors.items():
        out[name] = (out[name] * factor).astype(out[name].dtype)
    return out
```

```python
import math
from contextlib import ExitStack

import concourse.bass as bass
import numpy as np
from concourse import mybir

F32 = mybir.dt.float32
I32 = mybir.dt.int32
U32 = mybir.dt.uint32
ALU = mybir.AluOpType
ACT = mybir.ActivationFunctionType
AX = mybir.AxisListType
RMAX = bass.bass_isa.ReduceOp.max

P = 128
B, TOK, D = 8, 256, 256
T = B * TOK
NT = T // P
PER_BATCH = TOK // P
KC = D // P
HID = 512
HC = HID // P
UNIT = KC * HID + HC * D
W2_AT = KC * HID
SLOTS = 16
TOPK = 2
BLK = 512
NBLK = T // BLK
GENS = 4
LANES = 16
TBLOCKS = D // LANES
WCHUNK = 1024
RWIDE = NT * 14
NWCHUNK = TBLOCKS * D // WCHUNK

EXPERTS = (6, 14)
DENSE_SLOT = (8, 0)
EXPERT_SLOT = (10, 2)


def routed_tiles(n_experts):
    n = (TOPK * T + n_experts * (P - 1)) // P
    return n + n % 2


TILES = tuple(routed_tiles(e) for e in EXPERTS)

_Q = math.sqrt(177.0)
X3 = 2.0 / 3.0
X1 = X3 * (1 + _Q) / 88
X2 = X3 * (1 + _Q) / 352
X4 = (-271 + 29 * _Q) / (315 * X3)
X5 = 11 * (-1 + _Q) / (1260 * X3)
X6 = 11 * (-9 + _Q) / (5040 * X3)
X7 = (89 - _Q) / (5040 * X3 * X3)
Y2 = (857 - 58 * _Q) / 630

ROWS = {}
for _name, _n in (("b_base", D), ("ab2", D), ("gate_abel", D), ("gate_nonabel", D), ("bias1", D),
                  ("gate_b", 8), ("gate_c", 8)):
    _at = sum(n for _, n in ROWS.values())
    ROWS[_name] = (_at, _n)
NROWS = sum(n for _, n in ROWS.values())

COLS = {}
for _name, _n in (("ln_g", KC), ("ln_b", KC), ("ab1", 2 * HC), ("gate_w", KC * EXPERTS[0]),
                  ("router_w", KC * EXPERTS[1]), ("rms", SLOTS * KC)):
    _at = sum(n for _, n in COLS.values())
    COLS[_name] = (_at, _n)
NCOLS = sum(n for _, n in COLS.values())


class Step:

    def __init__(self, n, k, i=None):
        self.n, self.k, self.i = n, k, i

    def has(self, lag):
        return self.i is not None or 0 <= self.k - lag < self.n

    def tile(self, lag):
        return self.k - lag + (0 if self.i is None else self.i * 2)

    def slot(self, lag):
        return (self.k - lag) % 2

    def turn(self, lag):
        return (self.k - lag) // 2 + (0 if self.i is None else self.i)


def pipeline(eng, n, lags, step):
    lead = lags + 2 + lags % 2
    for k in range(lead):
        step(Step(n, k))
    with eng.Fori(0, (n - lead) // 2) as i:
        for k in range(2):
            step(Step(n, lead + k, i))
    for k in range(n, n + lags):
        step(Step(n, k))


class Chain:

    def __init__(self, eng, sem, per):
        self.eng, self.sem, self.per = eng, sem, per
        self.base, self.k = 0, 0

    def start(self, item):
        self.base, self.k = item * self.per, 0

    def did(self, instruction):
        self.k += 1
        assert self.k <= self.per
        instruction.then_inc(self.sem, 1)

    def wait(self):
        self.eng.wait_ge(self.sem, self.base + self.k)

    def then(self, instruction):
        self.did(instruction)
        self.wait()


def after(eng, sem, step, lag, back, per=1):
    if step.i is None and step.k - lag - back < 0:
        return
    eng.wait_ge(sem, (step.tile(lag) - back + 1) * per)


def two_layers(nc, x_rows, x_cols, cond, wbase, as_t, bs_t, rows, cols, units0, units1, eb1, eb2,
               gens, gens_t, w1c, mask1c, consts, identity2, out):
    ctx = ExitStack()
    with ctx:
        def sb(name, shape, dt=F32):
            return ctx.enter_context(nc.sbuf_tensor(name, shape, dt))

        def sem(name):
            return ctx.enter_context(nc.semaphore(name))

        queue = [nc.dram_tensor(f"queue{l}", (TILES[l] * P, D), F32, kind="Internal").ap() for l in range(2)]
        answer = [nc.dram_tensor(f"answer{l}", (TILES[l] * P, D), F32, kind="Internal").ap() for l in range(2)]
        wbot_dram = nc.dram_tensor("wbot", (B, D, D), F32, kind="Internal").ap()

        units = sb("units", [P, SLOTS, UNIT])
        z_all = sb("z_all", [P, NT, D])
        znt = sb("znt", [P, KC, T])
        res = sb("res", [P, NT, D])
        rot = sb("rot", [P, KC, D])
        con = sb("con", [P, 3, P])
        lane_mask = sb("lane_mask", [P, LANES])
        iota_e = sb("iota_e", [P, 16])
        iota_t = sb("iota_t", [P, max(TILES)])
        scan_on = sb("scan_on", [P, max(EXPERTS), NT])
        row = sb("row", [P, NROWS])
        col = sb("col", [P, NCOLS])
        crep = sb("crep", [P, B])
        c2 = sb("c2", [P, B])
        ring = sb("ring", [P, 4096])
        half = sb("half", [P, 1])
        logits = sb("logits", [P, NT, 16])
        top = sb("top", [P, NT, 8])
        top_i = sb("top_i", [P, NT, 8], U32)
        gate_w8 = sb("gate_w8", [P, TOPK, NT])
        pos_i = sb("pos_i", [P, TOPK, NT], I32)
        table = sb("table", [P, 2, max(TILES)], I32)
        small = sb("small", [P, 32])
        small_i = sb("small_i", [P, 4], I32)
        stats = sb("stats", [P, 2, 3])
        var = sb("var", [P, 2])
        rstd = sb("rstd", [P, 2])
        inv = sb("inv", [P, 2])
        gdot = sb("gdot", [P, 2, 4])

        ident = con[:, 0, :]
        upper = con[:, 1, :]
        ones = con[:, 2, :]

        def r(name):
            at, n = ROWS[name]
            return row[:, at:at + n]

        def cl(name):
            at, n = COLS[name]
            return col[:, at:at + n]

        ln_g, ln_b, ab1 = cl("ln_g"), cl("ln_b"), cl("ab1")
        router = [cl("gate_w").rearrange("p (k e) -> p k e", k=KC),
                  cl("router_w").rearrange("p (k e) -> p k e", k=KC)]
        rms = cl("rms").rearrange("p (s k) -> p s k", k=KC)

        def cut(at, n):
            return ring[:, at:at + n], at + n

        at = 0
        v, at = cut(at, 2 * D)
        x_t = v.rearrange("p (s k t) -> p s k t", s=2, k=KC)
        v, at = cut(at, 2 * D)
        x_in = v.rearrange("p (s d) -> p s d", s=2)
        v, at = cut(at, 2 * D)
        c_row = v.rearrange("p (s d) -> p s d", s=2)
        v, at = cut(at, 2 * D)
        z_row = v.rearrange("p (s d) -> p s d", s=2)
        v, at = cut(at, 2 * D)
        z_col = v.rearrange("p (s k t) -> p s k t", s=2, k=KC)
        v, at = cut(at, 2 * D)
        m_row = v.rearrange("p (s d) -> p s d", s=2)
        v, at = cut(at, 2 * D)
        m_col = v.rearrange("p (s k t) -> p s k t", s=2, k=KC)
        v, at = cut(at, 2 * D)
        work = v.rearrange("p (s d) -> p s d", s=2)
        hid_col = ring[:, :].rearrange("p (c t) -> p c t", c=2 * HC)
        at = 0
        v, at = cut(at, 2 * D)
        q_row = v.rearrange("p (s d) -> p s d", s=2)
        v, at = cut(at, 2 * D)
        q_col = v.rearrange("p (s k t) -> p s k t", s=2, k=KC)
        v, at = cut(at, 2 * HID)
        q_hid = v.rearrange("p (s h) -> p s h", s=2)
        v, at = cut(at, 2 * HID)
        q_hidc = v.rearrange("p (s c t) -> p s c t", s=2, c=HC)
        v, at = cut(at, 2 * D)
        q_out = v.rearrange("p (s d) -> p s d", s=2)
        assert at <= 4096

        flat = units[:, :, :].rearrange("p s n -> p (s n)")

        def mats(slot):
            return units[:, slot, :].rearrange("p (g k c) -> p g k c", g=GENS, k=KC)

        A_, AT_, A2_, TR_, PR_, U_ = (mats(s) for s in range(6))
        weff = units[:, 6:8, :].rearrange("p s n -> p (s n)").rearrange("p (b k o) -> p b k o", b=B, k=KC)
        eb1_sb = units[:, 6:8, :].rearrange("p s n -> p (s n)")[:, 0:EXPERTS[0] * HID]
        eb2_sb = z_all[:, 0:EXPERTS[0], :].rearrange("p e d -> p (e d)")
        wbot = units[:, 14:16, :].rearrange("p s n -> p (s n)").rearrange("p (b k o) -> p b k o", b=B, k=KC)
        cond_w = [weff, wbot]
        abel = units[:, 12:14, :].rearrange("p s n -> p (s n)").rearrange("p (t d) -> p t d", t=NT)
        second0 = units[:, 10:12, :].rearrange("p s n -> p (s n)").rearrange("p (t d) -> p t d", t=NT)
        second1 = znt[:, :, :].rearrange("p k t -> p (k t)").rearrange("p (t d) -> p t d", t=NT)
        second = [second0, second1]
        setup = units[:, 4, :]
        asT = setup[:, 0:D]
        bsT = setup[:, D:2 * D]
        wbaseT = setup[:, 2 * D:4 * D]
        bsw = units[:, 5, :].rearrange("p (b o) -> p b o", b=B)
        masks = units[:, 0:2, :].rearrange("p s n -> p (s n)")
        wfull = units[:, 2:4, :].rearrange("p s n -> p (s n)")
        wch = [wfull[:, q * WCHUNK:(q + 1) * WCHUNK] for q in range(NWCHUNK)]
        mch = [masks[:, q * WCHUNK:(q + 1) * WCHUNK] for q in range(NWCHUNK)]
        kron = units[:, 5, 0:P]
        ident2 = ring[:, 0:KC * D]
        zeros = m_row[:, 0, :]
        junk = m_row[:, 1, :]
        onehot = rot[:, :, :]
        scratch = [units[:, (5, 15)[l], 0:4 * RWIDE].rearrange("p (a n) -> p a n", a=4) for l in range(2)]
        picked = sb("picked", [P, NT, TOPK])
        small_e = sb("small_e", [P, 4, 16])

        ps = [ctx.enter_context(nc.psum_tensor(f"ps{i}", [P, 512], F32)) for i in range(8)]

        s_small = sem("small_loaded")
        s_cond = sem("cond_loaded")
        s_gens = sem("gens_loaded")
        s_units0 = sem("units0_loaded")
        s_eb = sem("expert_biases_loaded")
        s_zero = sem("zeros_made")
        s_qzero = sem("queues_zeroed")
        s_xt = [sem(f"x_cols_loaded{i}") for i in range(2)]
        s_x = [sem(f"x_rows_loaded{i}") for i in range(2)]
        s_unit1 = [sem(f"unit1_{i}_loaded") for i in range(SLOTS)]
        s_wc = sem("masked_weights_loaded")
        s_wst = sem("wbot_stored")
        s_id2 = sem("identity2_loaded")
        s_wbot = sem("wbot_loaded")
        s_out = [sem(f"out_stored{i}") for i in range(2)]
        s_prep = sem("prep_steps")
        s_bsw = sem("lora_b_scaled")
        s_weffmm = sem("weff_product")
        s_weff = sem("weff_added")
        s_norm = sem("norm_steps")
        s_allmax = sem("norm_maximum")
        s_scaled = sem("gens_scaled")
        s_prod = sem("exp_products")
        s_tr = sem("exp_transposes")
        s_poly = sem("exp_polynomial_steps")
        s_trc = sem("exp_transposes_copied")
        s_sqp = sem("square_products")
        s_sqc = sem("square_copied")
        s_sqt = sem("square_transposes")
        s_sqtc = sem("square_transposes_copied")
        s_rp = sem("rotation_products")
        s_rc = sem("rotation_copied")
        s_kron = sem("kron_made")
        s_wmul = sem("chunk_masked")
        s_wmm = sem("chunk_product")
        s_wev = sem("chunk_copied")
        s_rms = sem("unit_scaled")

        class Layer:
            pass

        L = []
        for l in range(2):
            y = Layer()
            y.cond_mm = sem(f"cond_product{l}")
            y.stat = sem(f"stat_steps{l}")
            y.pow = sem(f"rstd_made{l}")
            y.norm = sem(f"normalise_steps{l}")
            y.zt = sem(f"z_transposed{l}")
            y.ztc = sem(f"z_transpose_copied{l}")
            y.rescopy = sem(f"residual_started{l}")
            y.zcopy = sem(f"z_row_kept{l}")
            y.ztcopy = sem(f"z_col_kept{l}")
            y.lg = sem(f"logits_product{l}")
            y.lgc = sem(f"logits_copied{l}")
            y.route = sem(f"route_steps{l}")
            y.expd = sem(f"route_exp{l}")
            y.rank = sem(f"rank_products{l}")
            y.scat = sem(f"rows_scattered{l}")
            y.qload = [sem(f"queue_tile_loaded{l}_{i}") for i in range(2)]
            y.qt = sem(f"queue_transposed{l}")
            y.qtc = sem(f"queue_transpose_copied{l}")
            y.h = sem(f"hidden_product{l}")
            y.hb = sem(f"hidden_biased{l}")
            y.ha = sem(f"hidden_activated{l}")
            y.ht = sem(f"hidden_transposed{l}")
            y.htc = sem(f"hidden_transpose_copied{l}")
            y.o = sem(f"answer_product{l}")
            y.oc = sem(f"answer_copied{l}")
            y.ostore = [sem(f"answer_stored{l}_{i}") for i in range(2)]
            y.gather = sem(f"answers_gathered{l}")
            y.dh = sem(f"dense_hidden_product{l}")
            y.da = sem(f"dense_hidden_activated{l}")
            y.do = sem(f"dense_product{l}")
            y.doc = sem(f"dense_copied{l}")
            L.append(y)
        s_mix = sem("mix_steps")
        s_mt = sem("mix_transposed")
        s_mtc = sem("mix_transpose_copied")
        s_rot = sem("rotated")
        s_dot = sem("gate_dot_steps")
        s_sig = sem("gate_made")
        s_x1 = sem("x1_steps")
        s_xtr = sem("x1_transposed")
        s_xtc = sem("x1_transpose_copied")
        s_fin = sem("final_steps")

        MIX_STEPS, DOT_STEPS, X1_STEPS, FINAL_STEPS = 2, 4, 4, 2
        STAT_STEPS = (5, 3)
        NORM_STEPS = (1, 2)
        ZTC_STEPS = (KC, 1)
        ENTRY_LAG = (0, 5)
        ROUTE_STEPS = (32, 37)
        BOTH_STEP = 7

        block = ctx.enter_context(nc.Block())

        @block.sync
        def _(sp):
            for e in range(B):
                sp.dma_start(crep[e * LANES:(e + 1) * LANES, :], cond[e:e + 1, :].broadcast_to([LANES, B])).then_inc(s_cond, 16)
            sp.dma_start(asT, as_t).then_inc(s_cond, 16)
            sp.dma_start(bsT, bs_t).then_inc(s_cond, 16)
            sp.dma_start(wbaseT, wbase).then_inc(s_cond, 16)
            sp.dma_start(con[:, :, :], consts[:, 0:3 * P].rearrange("p (a b) -> p a b", a=3)).then_inc(s_small, 16)
            sp.dma_start(lane_mask[:, :], consts[:, 3 * P:3 * P + LANES]).then_inc(s_small, 16)
            sp.dma_start(col[:, :], cols).then_inc(s_small, 16)
            sp.dma_start(row[:, :], rows.broadcast_to([P, NROWS])).then_inc(s_small, 16)
            sp.dma_start(iota_e[:, :], consts[:, 400:416]).then_inc(s_small, 16)
            sp.dma_start(iota_t[:, :], consts[:, 416:416 + max(TILES)]).then_inc(s_small, 16)

            def load_x(st):
                if not st.has(0):
                    return
                s, t = st.slot(0), st.tile(0)
                after(sp, L[0].cond_mm, st, 0, 2)
                sp.dma_start(x_t[:, s, :, :], x_cols[bass.ds(t, 1), :, :, :].rearrange("a p k t -> (a p) k t")
                             ).then_inc(s_xt[s], 16)
                after(sp, L[0].rescopy, st, 0, 2)
                sp.dma_start(x_in[:, s, :], x_rows[bass.ds(t * P, P), :]).then_inc(s_x[s], 16)

            pipeline(sp, NT, 0, load_x)

            def routed(l):
                y = L[l]
                sp.wait_ge(y.scat, 16 * TOPK * NT)
                if l == 1:
                    sp.wait_ge(y.do, NT)
                if l == 0:
                    sp.wait_ge(y.cond_mm, NT)
                    sp.dma_start(eb1_sb, eb1.broadcast_to([P, EXPERTS[0] * HID])).then_inc(s_eb, 16)
                    sp.dma_start(eb2_sb, eb2.broadcast_to([P, EXPERTS[0] * D])).then_inc(s_eb, 16)

                def step(st):
                    if st.has(0):
                        s, t = st.slot(0), st.tile(0)
                        after(sp, y.qt, st, 0, 2)
                        sp.dma_start(q_row[:, s, :], queue[l][bass.ds(t * P, P), :]).then_inc(y.qload[s], 16)
                    if st.has(4):
                        s, t = st.slot(4), st.tile(4)
                        sp.wait_ge(y.oc, t + 1)
                        sp.dma_start(answer[l][bass.ds(t * P, P), :], q_out[:, s, :]).then_inc(y.ostore[s], 16)

                pipeline(sp, TILES[l], 4, step)

            sp.wait_ge(L[0].cond_mm, NT)
            sp.dma_start(ident2, identity2).then_inc(s_id2, 16)
            sp.wait_ge(s_rc, 3)
            sp.dma_start(wfull, w1c).then_inc(s_wc, 16)
            for g in range(B):
                sp.dma_start(masks[g * LANES:(g + 1) * LANES, :], mask1c).then_inc(s_wc, 16)
            routed(0)
            tb = WCHUNK // D
            for q in range(NWCHUNK):
                sp.wait_ge(s_wev, 2 * q + 2)
                for b in range(B):
                    sp.dma_start(
                        wbot_dram[b].rearrange("(tb tl) o -> tl tb o", tl=LANES)[:, q * tb:(q + 1) * tb, :],
                        mch[q][b * LANES:(b + 1) * LANES, :].rearrange("p (tb o) -> p tb o", tb=tb)
                    ).then_inc(s_wst, 16)

            sp.wait_ge(L[0].o, TILES[0])
            sp.wait_ge(L[0].oc, TILES[0])
            sp.wait_ge(s_wst, 16 * B * NWCHUNK)
            for s in range(8):
                sp.dma_start(units[:, s, :], units1[s]).then_inc(s_unit1[s], 16)
                if s == 1:
                    for b in range(B):
                        sp.dma_start(wbot[:, b, :, :], wbot_dram[b].rearrange("(k p) o -> p k o", p=P)).then_inc(s_wbot, 16)
            sp.wait_ge(L[0].do, NT)
            for s in (8, 9):
                sp.dma_start(units[:, s, :], units1[s]).then_inc(s_unit1[s], 16)
            sp.wait_ge(s_mix, NT * MIX_STEPS)
            sp.wait_ge(s_x1, NT * X1_STEPS)
            sp.wait_ge(L[1].cond_mm, NT)
            for s in range(10, SLOTS):
                if s == SLOTS - 1:
                    sp.wait_ge(L[1].route, ROUTE_STEPS[1])
                sp.dma_start(units[:, s, :], units1[s]).then_inc(s_unit1[s], 16)
            routed(1)
            out_v = out.rearrange("(n p) d -> n p d", p=P)

            def store(st):
                if st.has(0):
                    s, t = st.slot(0), st.tile(0)
                    sp.wait_ge(s_fin, (t + 1) * FINAL_STEPS)
                    sp.dma_start(out_v[bass.ds(t, 1), :, :].rearrange("a p d -> (a p) d"),
                                 res[:, bass.ds(t, 1), :].rearrange("p a d -> p (a d)")).then_inc(s_out[s], 16)

            pipeline(sp, NT, 0, store)
            for s in range(2):
                sp.wait_ge(s_out[s], 16 * NT // 2)

        @block.gpsimd
        def _(pool):
            nc.gpsimd.memset(half[:, :], -0.5).then_inc(s_zero, 1)
            pool.wait_ge(s_zero, 2)

            def entry(l):
                y, q = L[l], ENTRY_LAG[l]
                shift = q

                def step(st):
                    if st.has(q + 2):
                        s, t = st.slot(q + 2), st.tile(q + 2)
                        pool.wait_ge(y.ztc, (t + 1) * ZTC_STEPS[l])
                        nc.gpsimd.tensor_copy(znt[:, :, bass.ds(t * P, P)], z_col[:, s, :, :]).then_inc(y.ztcopy, 1)
                    if st.has(q + 1):
                        s, t = st.slot(q + 1), st.tile(q + 1)
                        pool.wait_ge(y.norm, (t + 1) * NORM_STEPS[l])
                        nc.gpsimd.tensor_copy(z_all[:, bass.ds(t, 1), :].rearrange("p a d -> p (a d)"),
                                              z_row[:, s, :]).then_inc(y.zcopy, 1)
                    if st.has(q):
                        s, t = st.slot(q), st.tile(q)
                        pool.wait_ge(y.stat, (t + 1) * STAT_STEPS[l])
                        after(pool, y.norm, st, q, 2, NORM_STEPS[l])
                        nc.gpsimd.tensor_tensor(rstd[:, s:s + 1], var[:, s:s + 1], half[:, :], ALU.pow).then_inc(y.pow, 1)
                        if l == 0:
                            pool.wait_ge(s_x[s], 16 * (st.turn(q) + 1))
                            nc.gpsimd.tensor_tensor(res[:, bass.ds(t, 1), :].rearrange("p a d -> p (a d)"),
                                                    c_row[:, s, :], x_in[:, s, :], ALU.add).then_inc(y.rescopy, 1)

                pipeline(pool, NT, q + 2, step)

            def scatter(l):
                y = L[l]
                pool.wait_ge(y.route, ROUTE_STEPS[l])
                pool.wait_ge(y.zcopy, NT)
                pool.wait_ge(s_qzero, 32)
                for t in range(NT):
                    for k in range(TOPK):
                        nc.gpsimd.indirect_dma_start(
                            queue[l], bass.IndirectOffsetOnAxis(pos_i[:, k, t:t + 1].bitcast(U32), 0),
                            z_all[:, t, :], None).then_inc(y.scat, 16)

            def gather(l):
                y = L[l]
                for s in range(2):
                    pool.wait_ge(y.ostore[s], 16 * TILES[l] // 2)
                if l == 0:
                    pool.wait_ge(y.oc, TILES[0])
                if l == 1:
                    pool.wait_ge(y.scat, 16 * TOPK * NT)
                for t in range(NT):
                    for k in range(TOPK):
                        to = z_all[:, t, :] if k == 0 else second[l][:, t, :]
                        nc.gpsimd.indirect_dma_start(
                            to, None, answer[l],
                            bass.IndirectOffsetOnAxis(pos_i[:, k, t:t + 1].bitcast(U32), 0)).then_inc(y.gather, 16)

            entry(0)
            pool.wait_ge(s_norm, 2)
            nc.gpsimd.partition_all_reduce(small[:, 1:2], small[:, 0:1], P, RMAX).then_inc(s_allmax, 1)
            scatter(0)
            gather(0)
            entry(1)
            scatter(1)
            gather(1)

        @block.scalar
        def _(act):
            act.wait_ge(s_zero, 2)
            for l in range(2):
                act.dma_start(queue[l].rearrange("(n p) d -> p n d", p=P),
                              zeros.unsqueeze(1).broadcast_to([P, TILES[l], D])).then_inc(s_qzero, 16)
                if l == 0:
                    act.dma_start(A_, gens).then_inc(s_gens, 16)
                    act.dma_start(AT_, gens_t).then_inc(s_gens, 16)
                    for s in range(8):
                        act.dma_start(units[:, 8 + s, :], units0[s]).then_inc(s_units0, 16)

            def entry(l):
                y, q = L[l], ENTRY_LAG[l]

                def step(st):
                    if st.has(q + 2):
                        s, t = st.slot(q + 2), st.tile(q + 2)
                        act.wait_ge(y.zt, t + 1)
                        after(act, y.lg, st, q + 2, 2)
                        after(act, y.ztcopy, st, q + 2, 2)
                        if l == 0:
                            for k in range(KC):
                                nc.scalar.activation(z_col[:, s, k, :], ps[5][:, k * P:(k + 1) * P], ACT.Identity,
                                                     scale=ln_g[:, k:k + 1], bias=ln_b[:, k:k + 1]).then_inc(y.ztc, 1)
                        else:
                            nc.scalar.copy(z_col[:, s, :, :].rearrange("p k t -> p (k t)"), ps[5][:, 0:D]).then_inc(y.ztc, 1)
                    if l == 1 and st.has(4):
                        s, t = st.slot(4), st.tile(4)
                        act.wait_ge(s_xtr, t + 1)
                        after(act, y.cond_mm, st, 4, 2)
                        nc.scalar.copy(x_t[:, s, :, :].rearrange("p k t -> p (k t)"), ps[2][:, 0:D]).then_inc(s_xtc, 1)
                    if l == 1 and st.has(2):
                        s, t = st.slot(2), st.tile(2)
                        act.wait_ge(s_dot, (t + 1) * DOT_STEPS)
                        after(act, s_x1, st, 2, 2, X1_STEPS)
                        nc.scalar.activation(gdot[:, s, 3:4], gdot[:, s, 2:3], ACT.Sigmoid).then_inc(s_sig, 1)
                    if l == 1 and st.has(1):
                        s, t = st.slot(1), st.tile(1)
                        act.wait_ge(s_mt, t + 1)
                        after(act, s_rot, st, 1, 2)
                        nc.scalar.copy(m_col[:, s, :, :].rearrange("p k t -> p (k t)"), ps[0][:, 0:D]).then_inc(s_mtc, 1)

                pipeline(act, NT, q + 2, step)

            def route_exp(l):
                y = L[l]
                act.wait_ge(y.route, 3)
                e2 = scratch[l][:, 2, 0:NT]
                nc.scalar.activation(e2, e2, ACT.Exp).then_inc(y.expd, 1)
                if l == 1:
                    e = scratch[l][:, 1, 0:NT * EXPERTS[1]]
                    nc.scalar.activation(e, e, ACT.Exp).then_inc(y.expd, 1)

            def exponentials():
                for stage in range(3):
                    dst, done = ((TR_, s_trc), (TR_, s_trc), (AT_, s_sqtc))[stage]
                    for g in range(GENS):
                        act.wait_ge(s_tr, stage * GENS + g + 1)
                        if stage == 1:
                            act.wait_ge(s_prod, GENS + g + 1)
                        nc.scalar.copy(dst[:, g, :, :].rearrange("p k c -> p (k c)"), ps[4 + g][:, :]).then_inc(done, 1)
                turns = act.value_load(small_i[0:1, 1:2], min_val=1, max_val=100)
                with act.Fori(0, turns) as i:
                    for g in range(GENS):
                        act.wait_ge(s_sqt, GENS * i + g + 1)
                        nc.scalar.copy(AT_[:, g, :, :].rearrange("p k c -> p (k c)"), ps[4 + g][:, :]).then_inc(s_sqtc, 1)

            def routed(l):
                y = L[l]

                def step(st):
                    if not st.has(1):
                        return
                    s, t = st.slot(1), st.tile(1)
                    if l == 0:
                        act.wait_ge(y.hb, t + 1)
                        nc.scalar.activation(q_hid[:, s, :], q_hid[:, s, :], ACT.Gelu).then_inc(y.ha, 1)
                    else:
                        act.wait_ge(y.h, t + 1)
                        after(act, y.ht, st, 1, 2)
                        nc.scalar.activation(q_hid[:, s, :], ps[2 + s][:, :], ACT.Silu).then_inc(y.ha, 1)

                pipeline(act, TILES[l], 4, step)

            def dense(l):
                y = L[l]
                if l == 0:
                    for s in range(2):
                        act.wait_ge(y.ostore[s], 16 * TILES[0] // 2)
                act.wait_ge(y.zcopy, NT)
                with act.Fori(0, NBLK) as i:
                    for c in range(2 * HC):
                        act.wait_ge(y.dh, 2 * HC * i + c + 1)
                        if l == 0:
                            nc.scalar.activation(hid_col[:, c, :], ps[2 + c % 4][:, :], ACT.Gelu,
                                                 bias=ab1[:, c:c + 1]).then_inc(y.da, 1)
                        else:
                            nc.scalar.activation(hid_col[:, c, :], ps[2 + c % 4][:, :], ACT.Silu).then_inc(y.da, 1)

            entry(0)
            route_exp(0)
            exponentials()
            routed(0)
            dense(0)
            entry(1)
            route_exp(1)
            dense(1)
            routed(1)

        @block.vector
        def _(dve):
            V = nc.vector

            def rows_at(buf, t):
                return buf[:, bass.ds(t, 1), :].rearrange("p a d -> p (a d)")

            def prepare():
                V.memset(zeros, 0.0).then_inc(s_zero, 1)
                V.memset(logits[:, :, :], -1e30).then_inc(s_prep, 1)
                V.memset(scan_on[:, :, :], 1.0).then_inc(s_prep, 1)
                dve.wait_ge(s_prep, 2)
                V.memset(scan_on[:, :, 0:1], 0.0).then_inc(s_prep, 1)
                dve.wait_ge(s_cond, 16 * (B + 3))
                V.tensor_scalar(c2[:, :], crep[:, :], 2.0, None, ALU.mult).then_inc(s_prep, 1)
                dve.wait_ge(s_prep, 4)
                for b in range(B):
                    V.tensor_scalar(bsw[:, b, :], bsT, c2[:, b:b + 1], None, ALU.mult).then_inc(s_bsw, 1)
                for b in range(B):
                    dve.wait_ge(s_weffmm, b + 1)
                    V.tensor_tensor(weff[:, b, :, :].rearrange("p k o -> p (k o)"), ps[b % 4][:, :], wbaseT,
                                    ALU.add).then_inc(s_weff, 1)
                dve.wait_ge(s_small, 96)

            def entry(l):
                y, q = L[l], ENTRY_LAG[l]
                stat = Chain(dve, y.stat, STAT_STEPS[l])
                norm = Chain(dve, y.norm, NORM_STEPS[l])
                mix = Chain(dve, s_mix, MIX_STEPS)
                dot = Chain(dve, s_dot, DOT_STEPS)
                x1 = Chain(dve, s_x1, X1_STEPS)
                E = EXPERTS[l]

                def step(st):
                    if st.has(q + 3):
                        s, t = st.slot(q + 3), st.tile(q + 3)
                        dve.wait_ge(y.lg, t + 1)
                        to = logits[:, bass.ds(t, 1), 0:E].rearrange("p a e -> p (a e)")
                        if l == 0:
                            V.tensor_tensor(to, ps[6][:, 0:E], r("gate_b")[:, 0:E], ALU.add).then_inc(y.lgc, 1)
                        else:
                            V.tensor_scalar(to, ps[6][:, 0:E], inv[:, s:s + 1], None, ALU.mult).then_inc(y.lgc, 1)
                    if st.has(q + 1):
                        s, t = st.slot(q + 1), st.tile(q + 1)
                        norm.start(t)
                        dve.wait_ge(y.pow, t + 1)
                        after(dve, y.zt, st, q + 1, 2)
                        after(dve, y.zcopy, st, q + 1, 2)
                        if l == 0:
                            norm.did(V.tensor_scalar(z_row[:, s, :], work[:, s, :], rstd[:, s:s + 1], None, ALU.mult))
                        else:
                            after(dve, y.lgc, st, q + 1, 2)
                            norm.did(V.tensor_tensor(inv[:, s:s + 1], var[:, s:s + 1], rstd[:, s:s + 1], ALU.mult))
                            norm.did(V.tensor_scalar(z_row[:, s, :], c_row[:, s, :], rstd[:, s:s + 1], None, ALU.mult))
                    if st.has(q):
                        s, t = st.slot(q), st.tile(q)
                        stat.start(t)
                        dve.wait_ge(y.cond_mm, t + 1)
                        if l == 0:
                            after(dve, y.rescopy, st, q, 2)
                        bias = r("b_base") if l == 0 else r("bias1")
                        after(dve, y.norm, st, q, 2, NORM_STEPS[l])
                        if l == 0:
                            stat.then(V.scalar_tensor_tensor(c_row[:, s, :], ps[3 + s][:, 0:D], 1.0, bias,
                                                             ALU.mult, ALU.add, accum_out=stats[:, s, 0:1]))
                            stat.then(V.tensor_scalar(stats[:, s, 1:2], stats[:, s, 0:1], 1.0 / D, None, ALU.mult))
                            stat.then(V.tensor_scalar(work[:, s, :], c_row[:, s, :], stats[:, s, 1:2], None, ALU.subtract))
                            stat.then(V.scalar_tensor_tensor(junk, work[:, s, :], 1.0, work[:, s, :],
                                                             ALU.mult, ALU.mult, accum_out=stats[:, s, 2:3]))
                            stat.did(V.tensor_scalar(var[:, s:s + 1], stats[:, s, 2:3], 1.0 / D, 1e-5, ALU.mult, ALU.add))
                        else:
                            stat.then(V.tensor_tensor(c_row[:, s, :], ps[3 + s][:, 0:D], bias, ALU.add))
                            stat.then(V.scalar_tensor_tensor(work[:, s, :], c_row[:, s, :], 1.0, c_row[:, s, :],
                                                             ALU.mult, ALU.mult, accum_out=stats[:, s, 0:1]))
                            stat.did(V.tensor_scalar(var[:, s:s + 1], stats[:, s, 0:1], 1.0 / D, 1.1920929e-07,
                                                     ALU.mult, ALU.add))
                    if l == 1 and st.has(3):
                        s, t = st.slot(3), st.tile(3)
                        x1.start(t)
                        dve.wait_ge(s_sig, t + 1)
                        x1.then(V.tensor_tensor(work[:, s, :], ps[(1, 7)[s]][:, 0:D], rows_at(abel, t), ALU.subtract))
                        x1.then(V.scalar_tensor_tensor(work[:, s, :], work[:, s, :], gdot[:, s, 3:4], rows_at(abel, t),
                                                       ALU.mult, ALU.add))
                        after(dve, s_xtr, st, 3, 2)
                        x1.then(V.tensor_tensor(x_in[:, s, :], work[:, s, :], rows_at(res, t), ALU.add))
                        x1.did(V.tensor_scalar(rows_at(res, t), x_in[:, s, :], 1.0, None, ALU.mult))
                    if l == 1 and st.has(2):
                        s, t = st.slot(2), st.tile(2)
                        dot.start(t)
                        dve.wait_ge(s_rot, t + 1)
                        dot.then(V.scalar_tensor_tensor(work[:, s, :], rows_at(abel, t), 1.0, r("gate_abel"),
                                                        ALU.mult, ALU.mult, accum_out=gdot[:, s, 0:1]))
                        dot.then(V.scalar_tensor_tensor(work[:, s, :], ps[(1, 7)[s]][:, 0:D], 1.0, r("gate_nonabel"),
                                                        ALU.mult, ALU.mult, accum_out=gdot[:, s, 1:2]))
                        dot.then(V.tensor_tensor(gdot[:, s, 2:3], gdot[:, s, 0:1], gdot[:, s, 1:2], ALU.add))
                        dot.did(V.tensor_tensor(gdot[:, s, 2:3], gdot[:, s, 2:3], r("gate_c")[:, 0:1], ALU.add))
                    if l == 1 and st.has(0):
                        s, t = st.slot(0), st.tile(0)
                        mix.start(t)
                        after(dve, s_mt, st, 0, 2)
                        mix.then(V.tensor_scalar(m_row[:, s, :], rows_at(z_all, t),
                                                 gate_w8[:, 0, bass.ds(t, 1)], None, ALU.mult))
                        mix.did(V.scalar_tensor_tensor(m_row[:, s, :], rows_at(second[0], t), gate_w8[:, 1, bass.ds(t, 1)],
                                                       m_row[:, s, :], ALU.mult, ALU.add))

                if l == 1:
                    dve.wait_ge(L[0].gather, 16 * TOPK * NT)
                pipeline(dve, NT, q + 3, step)

            def route(l):
                y, E, NQ = L[l], EXPERTS[l], TILES[l]
                ch = Chain(dve, y.route, ROUTE_STEPS[l])
                ch.start(0)

                def te(v):
                    return v.rearrange("p (t e) -> p t e", e=E)

                def et(v):
                    return v.rearrange("p (e t) -> p e t", t=NT)

                both, tot = (scratch[l][:, a, 0:NT * E] for a in range(2))
                first, other = (onehot[:, k, 0:NT * E] for k in range(TOPK))
                cum = scratch[l][:, 3, 0:NT * E]
                e2, den, w_a, w_b = (scratch[l][:, 2, a * NT:(a + 1) * NT] for a in range(4))
                dve.wait_ge(y.lgc, NT)
                wide = 8 if l == 0 else 16
                for t in range(NT):
                    i = V.max(top[:, t, :], logits[:, t, 0:wide])
                ch.then(i)
                for t in range(NT):
                    i = V.max_index(top_i[:, t, :], top[:, t, :], logits[:, t, 0:wide])
                ch.then(i)
                if l == 1:
                    V.tensor_tensor(te(tot), logits[:, :, 0:E], top[:, :, 0:1].broadcast_to([P, NT, E]), ALU.subtract)
                ch.then(V.tensor_tensor(e2.unsqueeze(2), top[:, :, 1:2], top[:, :, 0:1], ALU.subtract))
                ch.then(V.tensor_copy(picked[:, :, :], top_i[:, :, 0:TOPK]))
                for k, v in enumerate((first, other)):
                    ch.did(V.tensor_tensor(te(v), iota_e[:, 0:E].unsqueeze(1).broadcast_to([P, NT, E]),
                                           picked[:, :, k:k + 1].broadcast_to([P, NT, E]), ALU.is_equal))
                ch.wait()
                ch.then(V.tensor_tensor(both, first, other, ALU.add))
                assert ch.k == BOTH_STEP
                dve.wait_ge(y.expd, 1 + l)
                if l == 0:
                    ch.then(V.tensor_scalar(den, e2, 1.0, None, ALU.add))
                    ch.then(V.reciprocal(gate_w8[:, 0, :], den))
                    ch.then(V.tensor_tensor(gate_w8[:, 1, :], e2, gate_w8[:, 0, :], ALU.mult))
                else:
                    ch.then(V.tensor_reduce(den, te(tot), AX.X, ALU.add))
                    ch.then(V.reciprocal(w_a, den))
                    ch.then(V.tensor_tensor(w_b, e2, w_a, ALU.mult))
                    ch.then(V.tensor_tensor(den, w_a, w_b, ALU.add))
                    ch.then(V.tensor_scalar(den, den, 1e-9, None, ALU.add))
                    ch.then(V.reciprocal(e2, den))
                    ch.then(V.tensor_tensor(gate_w8[:, 0, :], w_a, e2, ALU.mult))
                    ch.then(V.tensor_tensor(gate_w8[:, 1, :], w_b, e2, ALU.mult))
                dve.wait_ge(y.rank, 2)
                ch.then(V.tensor_copy(et(tot), ps[7][:, 0:NT * E].rearrange("p (t e) -> p e t", e=E)))
                ch.then(V.tensor_tensor_scan(cum, scan_on[:, 0:E, :].rearrange("p e t -> p (e t)"), tot, 0.0,
                                             ALU.mult, ALU.add))
                count = et(cum)[:, :, NT - 1:NT].rearrange("p e a -> p (e a)")
                tiles_i, tiles, ends, start = (small_e[:, a, 0:E] for a in range(4))
                tiles_i = tiles_i.bitcast(I32)
                ch.then(V.tensor_scalar(tiles_i, count, float(P - 1), None, ALU.add))
                ch.then(V.tensor_scalar(tiles_i, tiles_i, 7, None, ALU.logical_shift_right))
                ch.then(V.tensor_copy(tiles, tiles_i))
                ch.then(V.tensor_tensor_scan(ends, scan_on[:, 0, 1:2].broadcast_to([P, E]), tiles, 0.0, ALU.mult, ALU.add))
                ch.then(V.tensor_tensor(start, ends, tiles, ALU.subtract))
                ch.then(V.tensor_scalar(start, start, float(P), None, ALU.mult))
                ch.then(V.tensor_tensor(cum, cum, tot, ALU.subtract))
                ch.then(V.tensor_tensor(et(cum), et(cum), start.unsqueeze(2).broadcast_to([P, E, NT]), ALU.add))
                ch.then(V.tensor_tensor(te(tot), te(ps[6][:, 0:NT * E]), cum.rearrange("p (e t) -> p t e", t=NT), ALU.add))
                for k, v in enumerate((first, other)):
                    ch.then(V.tensor_tensor(te(v), te(v), te(tot), ALU.mult))
                    ch.then(V.tensor_reduce(cum[:, k * NT:(k + 1) * NT], te(v), AX.X, ALU.add))
                    ch.then(V.tensor_copy(pos_i[:, k, :], cum[:, k * NT:(k + 1) * NT]))
                at_or_before = scratch[l][:, 0:3, :].rearrange("p a n -> p (a n)")[:, 0:NQ * E].rearrange("p (q e) -> p q e", e=E)
                ch.then(V.tensor_tensor(at_or_before, iota_t[:, 0:NQ].unsqueeze(2).broadcast_to([P, NQ, E]),
                                        ends.unsqueeze(1).broadcast_to([P, NQ, E]), ALU.is_ge))
                which = scratch[l][:, 3, 64:64 + NQ]
                ch.then(V.tensor_reduce(which, at_or_before, AX.X, ALU.add))
                ch.then(V.tensor_scalar(which, which, float(E - 1), None, ALU.min))
                ch.then(V.tensor_scalar(table[:, 0, 0:NQ], which, float(UNIT), float(EXPERT_SLOT[l] * UNIT), ALU.mult, ALU.add))
                ch.then(V.tensor_scalar(table[:, 1, 0:NQ], which, float(D), None, ALU.mult))
                assert ch.k == ROUTE_STEPS[l], ch.k

            def exponentials():
                steps = Chain(dve, s_poly, 64)
                steps.start(0)
                dve.wait_ge(s_gens, 32)
                V.tensor_reduce(small[:, 4:4 + GENS * KC], A_.rearrange("p g k c -> p (g k) c"), AX.X, ALU.add,
                                apply_absolute_value=True).then_inc(s_norm, 1)
                dve.wait_ge(s_norm, 1)
                V.tensor_reduce(small[:, 0:1], small[:, 4:4 + GENS * KC], AX.X, ALU.max).then_inc(s_norm, 1)
                dve.wait_ge(s_allmax, 1)
                n = Chain(dve, s_norm, 16)
                n.start(0)
                n.k = 2
                n.then(V.tensor_scalar(small_i[:, 0:1], small[:, 1:2].bitcast(I32), 23, None, ALU.logical_shift_right))
                n.then(V.tensor_scalar(small_i[:, 1:2], small_i[:, 0:1], -126.0, 1.0, ALU.add, ALU.max))
                n.then(V.tensor_scalar(small_i[:, 1:2], small_i[:, 1:2], 100.0, None, ALU.min))
                n.then(V.tensor_scalar(small_i[:, 2:3], small_i[:, 1:2], -1.0, 127.0, ALU.mult, ALU.add))
                n.then(V.tensor_scalar(small_i[:, 3:4], small_i[:, 2:3], 23, None, ALU.logical_shift_left))
                scale = small_i[:, 3:4].bitcast(F32)
                for v in (A_, AT_):
                    w = v.rearrange("p g k c -> p (g k c)")
                    V.tensor_scalar(w, w, scale, None, ALU.mult).then_inc(s_scaled, 1)
                dve.wait_ge(s_scaled, 2)

                def m(v, g):
                    return v[:, g, :, :].rearrange("p k c -> p (k c)")

                def stt(o, a, c, b):
                    return V.scalar_tensor_tensor(o, a, c, b, ALU.mult, ALU.add)

                for g in range(GENS):
                    dve.wait_ge(s_prod, g + 1)
                    steps.then(V.tensor_copy(m(A2_, g), ps[g][:, :]))
                for g in range(GENS):
                    steps.did(stt(m(PR_, g), m(A_, g), X1 / X2, m(A2_, g)))
                dve.wait_ge(s_id2, 16)
                for g in range(GENS):
                    dve.wait_ge(s_prod, GENS + g + 1)
                    steps.did(stt(m(U_, g), m(A2_, g), X3 / X2, ps[g][:, :]))
                    steps.then(stt(m(PR_, g), m(A_, g), X5 / X6, m(A2_, g)))
                    steps.then(stt(m(PR_, g), ident2, X4 / X6, m(PR_, g)))
                    steps.did(stt(m(PR_, g), ps[g][:, :], X7 * X2 / X6, m(PR_, g)))
                    steps.then(stt(m(A_, g), m(A2_, g), Y2, m(A_, g)))
                    steps.then(V.tensor_tensor(m(A_, g), m(A_, g), ident2, ALU.add))
                for g in range(GENS):
                    dve.wait_ge(s_prod, 2 * GENS + g + 1)
                    steps.then(stt(m(A_, g), ps[g][:, :], X2 * X6, m(A_, g)))
                turns = dve.value_load(small_i[0:1, 1:2], min_val=1, max_val=100)
                with dve.Fori(0, turns) as i:
                    for g in range(GENS):
                        dve.wait_ge(s_sqp, GENS * i + g + 1)
                        V.tensor_copy(m(A_, g), ps[g][:, :]).then_inc(s_sqc, 1)
                for j, (to, bank) in enumerate(((m(A2_, 0), 0), (m(A2_, 1), 1), (rot[:, :, :].rearrange("p k c -> p (k c)"), 2))):
                    dve.wait_ge(s_rp, j + 1)
                    V.tensor_copy(to, ps[bank][:, :]).then_inc(s_rc, 1)

            def masked_weights():
                dve.wait_ge(s_rc, 3)
                V.tensor_tensor(kron.rearrange("p (b t) -> p b t", t=LANES),
                                lane_mask[:, :].unsqueeze(1).broadcast_to([P, B, LANES]),
                                crep[:, :].unsqueeze(2).broadcast_to([P, B, LANES]), ALU.mult).then_inc(s_kron, 1)
                dve.wait_ge(s_wc, 16 * (B + 1))
                for q in range(NWCHUNK):
                    V.tensor_tensor(wch[q], wch[q], mch[q], ALU.mult).then_inc(s_wmul, 1)
                for q in range(NWCHUNK):
                    for a in range(2):
                        dve.wait_ge(s_wmm, 2 * q + a + 1)
                        V.tensor_copy(mch[q][:, a * 512:(a + 1) * 512], ps[2 * q + a][:, :]).then_inc(s_wev, 1)

            def routed(l):
                y = L[l]
                if l == 0:
                    dve.wait_ge(s_eb, 32)

                def step(st):
                    if l == 0 and st.has(1):
                        s, t = st.slot(1), st.tile(1)
                        at = dve.value_load(table[0:1, 1, bass.ds(t, 1)], min_val=0, max_val=(EXPERTS[0] - 1) * D)
                        dve.wait_ge(y.h, t + 1)
                        after(dve, y.ht, st, 1, 2)
                        V.tensor_tensor(q_hid[:, s, :], ps[2 + s][:, :], eb1_sb[:, bass.ds(at * 2, HID)], ALU.add).then_inc(y.hb, 1)
                    if st.has(2):
                        s, t = st.slot(2), st.tile(2)
                        dve.wait_ge(y.ht, t + 1)
                        after(dve, y.o, st, 2, 2)
                        V.tensor_copy(q_hidc[:, s, :, :].rearrange("p c t -> p (c t)"), ps[4 + s][:, :]).then_inc(y.htc, 1)
                    if st.has(0):
                        s, t = st.slot(0), st.tile(0)
                        dve.wait_ge(y.qt, t + 1)
                        after(dve, y.h, st, 0, 2)
                        if l == 0:
                            for k in range(KC):
                                V.tensor_scalar(q_col[:, s, k, :], ps[s][:, k * P:(k + 1) * P], ln_g[:, k:k + 1],
                                                ln_b[:, k:k + 1], ALU.mult, ALU.add).then_inc(y.qtc, 1)
                        else:
                            V.tensor_copy(q_col[:, s, :, :].rearrange("p k t -> p (k t)"), ps[s][:, 0:D]).then_inc(y.qtc, 1)
                    if st.has(3):
                        s, t = st.slot(3), st.tile(3)
                        if l == 0:
                            at = dve.value_load(table[0:1, 1, bass.ds(t, 1)], min_val=0, max_val=(EXPERTS[0] - 1) * D)
                        dve.wait_ge(y.o, t + 1)
                        if st.i is not None or st.k - 3 >= 2:
                            dve.wait_ge(y.ostore[s], 16 * st.turn(3))
                        if l == 0:
                            V.tensor_tensor(q_out[:, s, :], ps[6 + s][:, 0:D], eb2_sb[:, bass.ds(at, D)], ALU.add).then_inc(y.oc, 1)
                        else:
                            V.tensor_copy(q_out[:, s, :], ps[6 + s][:, 0:D]).then_inc(y.oc, 1)

                pipeline(dve, TILES[l], 4, step)

            def scale_unit(u):
                dve.wait_ge(s_unit1[u], 16)
                for k in range(KC):
                    w = units[:, u, k * HID:(k + 1) * HID]
                    V.tensor_scalar(w, w, rms[:, u, k:k + 1], None, ALU.mult).then_inc(s_rms, 1)

            def dense(l):
                y = L[l]
                dve.sem_inc(y.doc, 1)
                for i in range(NBLK):
                    for u in range(8 * l + 2 * i, 8 * l + 2 * i + 2):
                        scale_unit(u)
                    for j in range(4):
                        t = 4 * i + j
                        dve.wait_ge(y.do, t + 1)
                        if l == 0:
                            V.tensor_tensor(abel[:, t, :], ps[6 + j % 2][:, 0:D], r("ab2"), ALU.add).then_inc(y.doc, 1)
                        else:
                            V.tensor_tensor(res[:, t, :], ps[6 + j % 2][:, 0:D], res[:, t, :], ALU.add).then_inc(y.doc, 1)

            def final():
                fin = Chain(dve, s_fin, FINAL_STEPS)

                def step(st):
                    if st.has(0):
                        t = st.tile(0)
                        fin.start(t)
                        dve.wait_ge(L[1].gather, 16 * TOPK * NT)
                        fin.then(V.scalar_tensor_tensor(rows_at(res, t), rows_at(z_all, t), gate_w8[:, 0, bass.ds(t, 1)],
                                                        rows_at(res, t), ALU.mult, ALU.add))
                        fin.did(V.scalar_tensor_tensor(rows_at(res, t), rows_at(second[1], t), gate_w8[:, 1, bass.ds(t, 1)],
                                                       rows_at(res, t), ALU.mult, ALU.add))

                pipeline(dve, NT, 0, step)

            prepare()
            entry(0)
            route(0)
            exponentials()
            routed(0)
            masked_weights()
            dense(0)
            entry(1)
            route(1)
            dense(1)
            routed(1)
            final()

        @block.tensor
        def _(pe):
            mm = nc.tensor.matmul

            def layer0_weights():
                pe.wait_ge(s_cond, 16 * (B + 3))
                for b in range(B):
                    pe.wait_ge(s_bsw, b + 1)
                    if b >= 4:
                        pe.wait_ge(s_weff, b - 3)
                    for k in range(KC):
                        i = mm(ps[b % 4][:, k * D:(k + 1) * D], asT[:, k * P:(k + 1) * P], bsw[:, b, :], start=True, stop=True)
                    i.then_inc(s_weffmm, 1)

            def transpose2(bank, rows2, done):
                for k in range(KC):
                    i = nc.tensor.transpose(bank[:, k * P:(k + 1) * P], rows2[:, k * P:(k + 1) * P], ident)
                i.then_inc(done, 1)

            def entry(l):
                y, q = L[l], ENTRY_LAG[l]
                E = EXPERTS[l]

                def step(st):
                    if st.has(q + 3):
                        s, t = st.slot(q + 3), st.tile(q + 3)
                        pe.wait_ge(y.ztc, (t + 1) * ZTC_STEPS[l])
                        after(pe, y.lgc, st, q + 3, 1)
                        for k in range(KC):
                            i = mm(ps[6][:, 0:E], z_col[:, s, k, :], router[l][:, k, :], start=(k == 0), stop=(k == KC - 1))
                        i.then_inc(y.lg, 1)
                    if st.has(q + 2):
                        s, t = st.slot(q + 2), st.tile(q + 2)
                        pe.wait_ge(y.norm, (t + 1) * NORM_STEPS[l])
                        after(pe, y.ztc, st, q + 2, 1, ZTC_STEPS[l])
                        transpose2(ps[5], z_row[:, s, :], y.zt)
                    if st.has(q):
                        s, t = st.slot(q), st.tile(q)
                        if l == 0:
                            pe.wait_ge(s_xt[s], 16 * (st.turn(q) + 1))
                        else:
                            pe.wait_ge(s_xtc, t + 1)
                        after(pe, y.stat, st, q, 2, STAT_STEPS[l])
                        for k in range(KC):
                            i = mm(ps[3 + s][:, 0:D], x_t[:, s, k, :],
                                   cond_w[l][:, bass.ds(st.turn(q), 1), k, :].rearrange("p a o -> p (a o)"),
                                   start=(k == 0), stop=(k == KC - 1))
                        i.then_inc(y.cond_mm, 1)
                    if l == 1 and st.has(4):
                        s, t = st.slot(4), st.tile(4)
                        pe.wait_ge(s_x1, (t + 1) * X1_STEPS)
                        after(pe, s_xtc, st, 4, 1)
                        transpose2(ps[2], x_in[:, s, :], s_xtr)
                    if l == 1 and st.has(2):
                        s, t = st.slot(2), st.tile(2)
                        pe.wait_ge(s_mtc, t + 1)
                        after(pe, s_x1, st, 2, 2, X1_STEPS)
                        for k in range(KC):
                            i = mm(ps[(1, 7)[s]][:, 0:D], m_col[:, s, k, :], rot[:, k, :], start=(k == 0), stop=(k == KC - 1))
                        i.then_inc(s_rot, 1)
                    if l == 1 and st.has(1):
                        s, t = st.slot(1), st.tile(1)
                        pe.wait_ge(s_mix, (t + 1) * MIX_STEPS)
                        after(pe, s_mtc, st, 1, 1)
                        transpose2(ps[0], m_row[:, s, :], s_mt)

                pipeline(pe, NT, q + 3, step)

            def rank(l):
                y, n = L[l], NT * EXPERTS[l]
                pe.wait_ge(y.route, BOTH_STEP)
                both = scratch[l][:, 0, 0:n]
                mm(ps[6][:, 0:n], upper, both, start=True, stop=True).then_inc(y.rank, 1)
                mm(ps[7][:, 0:n], ones, both, start=True, stop=True).then_inc(y.rank, 1)

            def product(bank, xt, y):
                for mc in range(KC):
                    for k in range(KC):
                        i = mm(bank[:, mc * D:(mc + 1) * D], xt[:, k, mc * P:(mc + 1) * P], y[:, k, :],
                               start=(k == 0), stop=(k == KC - 1))
                return i

            def turned(bank, x):
                for k in range(KC):
                    for mc in range(KC):
                        i = nc.tensor.transpose(bank[:, k * D + mc * P:k * D + (mc + 1) * P],
                                                x[:, mc, k * P:(k + 1) * P], ident)
                return i

            def exponentials():
                pe.wait_ge(s_scaled, 2)
                for g in range(GENS):
                    product(ps[g], AT_[:, g], A_[:, g]).then_inc(s_prod, 1)
                for g in range(GENS):
                    pe.wait_ge(s_poly, g + 1)
                    turned(ps[4 + g], A2_[:, g]).then_inc(s_tr, 1)
                for g in range(GENS):
                    pe.wait_ge(s_poly, GENS + g + 1)
                    pe.wait_ge(s_trc, g + 1)
                    product(ps[g], TR_[:, g], PR_[:, g]).then_inc(s_prod, 1)
                for g in range(GENS):
                    pe.wait_ge(s_poly, 2 * GENS + 6 * g + 1)
                    turned(ps[4 + g], U_[:, g]).then_inc(s_tr, 1)
                for g in range(GENS):
                    pe.wait_ge(s_poly, 2 * GENS + 6 * g + 4)
                    pe.wait_ge(s_trc, GENS + g + 1)
                    product(ps[g], TR_[:, g], PR_[:, g]).then_inc(s_prod, 1)
                for g in range(GENS):
                    pe.wait_ge(s_poly, 8 * GENS + g + 1)
                    turned(ps[4 + g], A_[:, g]).then_inc(s_tr, 1)
                turns = pe.value_load(small_i[0:1, 1:2], min_val=1, max_val=100)
                with pe.Fori(0, turns) as i:
                    for g in range(GENS):
                        pe.wait_ge(s_sqtc, GENS * i + g + 1)
                        product(ps[g], AT_[:, g], A_[:, g]).then_inc(s_sqp, 1)
                    for g in range(GENS):
                        pe.wait_ge(s_sqc, GENS * i + g + 1)
                        turned(ps[4 + g], A_[:, g]).then_inc(s_sqt, 1)
                pe.wait_ge(s_sqtc, GENS * turns + GENS)
                product(ps[0], A_[:, 1], AT_[:, 0]).then_inc(s_rp, 1)
                product(ps[1], AT_[:, 2], A_[:, 3]).then_inc(s_rp, 1)
                pe.wait_ge(s_rc, 2)
                product(ps[2], A2_[:, 0], A2_[:, 1]).then_inc(s_rp, 1)
                pe.wait_ge(s_rc, 3)

            def masked_weights():
                pe.wait_ge(s_kron, 1)
                pe.wait_ge(L[0].oc, TILES[0])
                for q in range(NWCHUNK):
                    pe.wait_ge(s_wmul, q + 1)
                    for a in range(2):
                        mm(ps[2 * q + a][:, :], kron, wch[q][:, a * 512:(a + 1) * 512], start=True, stop=True
                           ).then_inc(s_wmm, 1)
                pe.wait_ge(s_wev, 2 * NWCHUNK)

            def routed(l):
                y = L[l]
                top_at = (EXPERT_SLOT[l] + EXPERTS[l] - 1) * UNIT

                def unit_of(t):
                    return pe.value_load(table[0:1, 0, bass.ds(t, 1)], min_val=EXPERT_SLOT[l] * UNIT, max_val=top_at)

                def step(st):
                    if st.has(1):
                        s, t = st.slot(1), st.tile(1)
                        pe.wait_ge(y.qtc, (t + 1) * (KC if l == 0 else 1))
                        after(pe, y.hb if l == 0 else y.ha, st, 1, 2)
                        at = unit_of(t)
                        for k in range(KC):
                            i = mm(ps[2 + s][:, :], q_col[:, s, k, :], flat[:, bass.ds(at + k * HID, HID)],
                                   start=(k == 0), stop=(k == KC - 1))
                        i.then_inc(y.h, 1)
                    if st.has(2):
                        s, t = st.slot(2), st.tile(2)
                        pe.wait_ge(y.ha, t + 1)
                        after(pe, y.htc, st, 2, 2)
                        for c in range(HC):
                            i = nc.tensor.transpose(ps[4 + s][:, c * P:(c + 1) * P], q_hid[:, s, c * P:(c + 1) * P], ident)
                        i.then_inc(y.ht, 1)
                    if st.has(0):
                        s, t = st.slot(0), st.tile(0)
                        pe.wait_ge(y.qload[s], 16 * (st.turn(0) + 1))
                        after(pe, y.qtc, st, 0, 2, KC if l == 0 else 1)
                        transpose2(ps[s], q_row[:, s, :], y.qt)
                    if st.has(3):
                        s, t = st.slot(3), st.tile(3)
                        pe.wait_ge(y.htc, t + 1)
                        after(pe, y.oc, st, 3, 2)
                        at = unit_of(t)
                        for c in range(HC):
                            i = mm(ps[6 + s][:, 0:D], q_hidc[:, s, c, :], flat[:, bass.ds(at + W2_AT + c * D, D)],
                                   start=(c == 0), stop=(c == HC - 1))
                        i.then_inc(y.o, 1)

                if l == 0:
                    pe.wait_ge(s_units0, 128)
                else:
                    pe.wait_ge(s_rms, SLOTS * KC)
                pipeline(pe, TILES[l], 4, step)
                pe.wait_ge(y.oc, TILES[l])

            def dense(l):
                y = L[l]
                if l == 0:
                    pe.wait_ge(s_units0, 128)
                else:
                    pe.wait_ge(s_rms, 2 * KC)
                pe.wait_ge(y.ztcopy, NT)
                with pe.Fori(0, NBLK) as i:
                    for c in range(2 * HC):
                        u = DENSE_SLOT[l] + c // HC
                        if c >= 4:
                            pe.wait_ge(y.da, 2 * HC * i + c - 3)
                        for k in range(KC):
                            at = k * HID + (c % HC) * P
                            m = mm(ps[2 + c % 4][:, :], units[:, u, at:at + P], znt[:, k, bass.ds(i * BLK, BLK)],
                                   start=(k == 0), stop=(k == KC - 1))
                        m.then_inc(y.dh, 1)
                    pe.wait_ge(y.route, ROUTE_STEPS[l])
                    for j in range(4):
                        pe.wait_ge(y.doc, 1 + 4 * i + max(j - 1, 0))
                        for c in range(2 * HC):
                            u = DENSE_SLOT[l] + c // HC
                            if j == 0:
                                pe.wait_ge(y.da, 2 * HC * i + c + 1)
                            at = W2_AT + (c % HC) * D
                            m = mm(ps[6 + j % 2][:, 0:D], hid_col[:, c, j * P:(j + 1) * P], units[:, u, at:at + D],
                                   start=(c == 0), stop=(c == 2 * HC - 1))
                        m.then_inc(y.do, 1)
                pe.wait_ge(y.doc, 1 + NT)

            layer0_weights()
            pe.wait_ge(s_weff, B)
            pe.wait_ge(s_small, 96)
            entry(0)
            rank(0)
            pe.wait_ge(L[0].lgc, NT)
            exponentials()
            routed(0)
            masked_weights()
            dense(0)
            pe.wait_ge(s_wbot, 16 * B)
            entry(1)
            rank(1)
            dense(1)
            routed(1)


def constants():
    c = np.zeros((P, 3 * P + LANES + 16 + max(TILES)), np.float32)
    c[:, 0:P] = np.eye(P)
    c[:, P:2 * P] = np.triu(np.ones((P, P)), 1)
    c[:, 2 * P:3 * P] = 1.0
    at = 3 * P
    c[:, at:at + LANES] = np.arange(P)[:, None] % LANES == np.arange(LANES)[None, :]
    at += LANES
    c[:, at:at + 16] = np.arange(16)
    at += 16
    c[:, at:] = np.arange(max(TILES))
    identity2 = np.zeros((P, KC, D), np.float32)
    for k in range(KC):
        identity2[:, k, k * P:(k + 1) * P] = np.eye(P)
    return c, identity2.reshape(P, KC * D)


def kernel(**inputs):
    import concourse.bacc as bacc
    from concourse.bass_utils import run_bass_kernel_spmd

    a = {k: np.asarray(v) for k, v in inputs.items()}

    def chunks(m):
        return m.reshape(-1, P, m.shape[1]).transpose(1, 0, 2).reshape(P, -1)

    def unit(w1, w2):
        return np.concatenate([chunks(w1), chunks(w2)], axis=1)

    x = a["x"]
    aw1, aw2 = a["L0_ffn_aw1"], a["L0_ffn_aw2"]
    units0 = [unit(aw1[:, h * HID:(h + 1) * HID], aw2[h * HID:(h + 1) * HID]) for h in range(2)]
    units0 += [unit(a["L0_ffn_ew1"][e], a["L0_ffn_ew2"][e]) for e in range(EXPERTS[0])]
    units1 = [unit(a["L1_ffn_w1_s"][e], a["L1_ffn_w2_s"][e]) for e in range(2)]
    units1 += [unit(a["L1_ffn_w1"][e], a["L1_ffn_w2"][e]) for e in range(EXPERTS[1])]
    rms = np.concatenate([a["L1_ffn_rms_w_s"], a["L1_ffn_rms_w"]])
    parts = {"b_base": a["L0_cond_b_base"], "ab2": a["L0_ffn_ab2"], "gate_abel": a["L0_ffn_gc_w"][0:D, 0],
             "gate_nonabel": a["L0_ffn_gc_w"][D:2 * D, 0], "bias1": a["L1_cond_bias"], "gate_b": a["L0_ffn_gate_b"],
             "gate_c": a["L0_ffn_gc_b"]}
    rows = np.zeros((1, NROWS), np.float32)
    for name, v in parts.items():
        rows[0, ROWS[name][0]:ROWS[name][0] + v.size] = v
    parts = {"ln_g": chunks(a["L0_ffn_ln_g"][:, None]), "ln_b": chunks(a["L0_ffn_ln_b"][:, None]),
             "ab1": chunks(a["L0_ffn_ab1"][:, None]), "gate_w": chunks(a["L0_ffn_gate_w"]),
             "router_w": chunks(a["L1_ffn_router_w"]), "rms": rms.reshape(SLOTS, KC, P).transpose(2, 0, 1).reshape(P, -1)}
    cols = np.zeros((P, NCOLS), np.float32)
    for name, v in parts.items():
        cols[:, COLS[name][0]:COLS[name][0] + v.shape[1]] = v
    gens = a["L0_ffn_gens"]
    con, identity2 = constants()
    arrays = {
        "x_rows": x.reshape(T, D),
        "x_cols": x.reshape(NT, P, KC, P).transpose(0, 3, 2, 1),
        "cond": a["cond_8"].T,
        "wbase": chunks(a["L0_cond_W_base"].T),
        "as_t": a["L0_cond_As"].reshape(P, D),
        "bs_t": a["L0_cond_Bs"].transpose(0, 2, 1).reshape(P, D),
        "rows": rows,
        "cols": cols,
        "units0": np.stack(units0),
        "units1": np.stack(units1),
        "eb1": a["L0_ffn_eb1"].reshape(1, -1),
        "eb2": a["L0_ffn_eb2"].reshape(1, -1),
        "gens": gens.reshape(GENS, KC, P, D).transpose(2, 0, 1, 3),
        "gens_t": gens.transpose(0, 2, 1).reshape(GENS, KC, P, D).transpose(2, 0, 1, 3),
        "w1c": a["L1_cond_weight"].transpose(0, 2, 1).reshape(B, TBLOCKS, LANES, D).transpose(0, 2, 1, 3).reshape(P, -1),
        "mask1c": a["L1_cond_mask"].T.reshape(TBLOCKS, LANES, D).transpose(1, 0, 2).reshape(LANES, -1),
        "consts": con,
        "identity2": identity2,
    }
    nc = bacc.Bacc("TRN2", target_bir_lowering=False, num_devices=1)
    feeds, args = {}, []
    for name, v in arrays.items():
        feeds[f"in_{name}"] = np.ascontiguousarray(v)
        args.append(nc.dram_tensor(f"in_{name}", v.shape, F32, kind="ExternalInput").ap())
    out = nc.dram_tensor("out_rows", (T, D), F32, kind="ExternalOutput").ap()
    two_layers(nc, *args, out)
    result = run_bass_kernel_spmd(nc, [feeds], core_ids=[0])
    return result.results[0]["out_rows"].reshape(B, TOK, D)
```

```python
import math
from contextlib import ExitStack

import concourse.bass as bass
import numpy as np
from concourse import mybir

F32 = mybir.dt.float32
I32 = mybir.dt.int32
U32 = mybir.dt.uint32
ALU = mybir.AluOpType
ACT = mybir.ActivationFunctionType
AX = mybir.AxisListType
RMAX = bass.bass_isa.ReduceOp.max

P = 128
B, TOK, D = 8, 256, 256
T = B * TOK
NT = T // P
PER_BATCH = TOK // P
KC = D // P
HID = 512
HC = HID // P
UNIT = KC * HID + HC * D
W2_AT = KC * HID
SLOTS = 16
TOPK = 2
BLK = 512
NBLK = T // BLK
GENS = 4
LANES = 16
TBLOCKS = D // LANES
WCHUNK = 1024
RWIDE = NT * 14
NWCHUNK = TBLOCKS * D // WCHUNK
GROUP = 4
NGROUPS = NT // GROUP
DENSE_BEFORE = (0, 3)

EXPERTS = (6, 14)
DENSE_SLOT = (8, 0)
EXPERT_SLOT = (10, 2)


def routed_tiles(n_experts):
    n = (TOPK * T + n_experts * (P - 1)) // P
    return n + n % 2


TILES = tuple(routed_tiles(e) for e in EXPERTS)

_Q = math.sqrt(177.0)
X3 = 2.0 / 3.0
X1 = X3 * (1 + _Q) / 88
X2 = X3 * (1 + _Q) / 352
X4 = (-271 + 29 * _Q) / (315 * X3)
X5 = 11 * (-1 + _Q) / (1260 * X3)
X6 = 11 * (-9 + _Q) / (5040 * X3)
X7 = (89 - _Q) / (5040 * X3 * X3)
Y2 = (857 - 58 * _Q) / 630

CONSTS = {}
for _name, _n in (("ident", P), ("upper", P), ("ones", P), ("lanes", LANES), ("iota_e", 16), ("iota_t", max(TILES))):
    _at = sum(n for _, n in CONSTS.values())
    CONSTS[_name] = (_at, _n)
NCONSTS = sum(n for _, n in CONSTS.values())

ROWS = {}
for _name, _n in (("b_base", D), ("ln_g", D), ("ln_b", D), ("ab2", D), ("gate_abel", D), ("gate_nonabel", D), ("bias1", D),
                  ("gate_b", 8), ("gate_c", 8)):
    _at = sum(n for _, n in ROWS.values())
    ROWS[_name] = (_at, _n)
NROWS = sum(n for _, n in ROWS.values())

COLS = {}
for _name, _n in (("ab1", 2 * HC), ("gate_w", KC * EXPERTS[0]),
                  ("router_w", KC * EXPERTS[1]), ("rms", SLOTS * KC)):
    _at = sum(n for _, n in COLS.values())
    COLS[_name] = (_at, _n)
NCOLS = sum(n for _, n in COLS.values())


class Step:

    def __init__(self, n, k, i=None):
        self.n, self.k, self.i = n, k, i

    def has(self, lag):
        return self.i is not None or 0 <= self.k - lag < self.n

    def tile(self, lag):
        return self.k - lag + (0 if self.i is None else self.i * 2)

    def slot(self, lag):
        return (self.k - lag) % 2

    def turn(self, lag):
        return (self.k - lag) // 2 + (0 if self.i is None else self.i)


def unrolled(n, lags, step):
    for k in range(n + lags):
        step(Step(n, k))


def pipeline(eng, n, lags, step):
    lead = lags + 2 + lags % 2
    for k in range(lead):
        step(Step(n, k))
    with eng.Fori(0, (n - lead) // 2) as i:
        for k in range(2):
            step(Step(n, lead + k, i))
    for k in range(n, n + lags):
        step(Step(n, k))


class Chain:

    def __init__(self, eng, sem, per):
        self.eng, self.sem, self.per = eng, sem, per
        self.base, self.k = 0, 0

    def start(self, item):
        self.base, self.k = item * self.per, 0

    def did(self, instruction):
        self.k += 1
        assert self.k <= self.per
        instruction.then_inc(self.sem, 1)

    def wait(self):
        self.eng.wait_ge(self.sem, self.base + self.k)

    def then(self, instruction):
        self.did(instruction)
        self.wait()


def after(eng, sem, step, lag, back, per=1):
    if step.i is None and step.k - lag - back < 0:
        return
    eng.wait_ge(sem, (step.tile(lag) - back + 1) * per)


def two_layers(nc, x_rows, x_cols, cond, lora, rows, cols, units0, units1, eb1, eb2, gens, gens_t,
               w1c, mask1c, consts, identity2, out):
    ctx = ExitStack()
    with ctx:
        def sb(name, shape, dt=F32):
            return ctx.enter_context(nc.sbuf_tensor(name, shape, dt))

        def sem(name):
            return ctx.enter_context(nc.semaphore(name))

        queue = [nc.dram_tensor(f"queue{l}", (TILES[l] * P, D), F32, kind="Internal").ap() for l in range(2)]
        answer = [nc.dram_tensor(f"answer{l}", (TILES[l] * P, D), F32, kind="Internal").ap() for l in range(2)]
        wbot_dram = nc.dram_tensor("wbot", (B, D, D), F32, kind="Internal").ap()

        units = sb("units", [P, SLOTS, UNIT])
        z_all = sb("z_all", [P, NT, D])
        znt = sb("znt", [P, KC, T])
        res = sb("res", [P, NT, D])
        rot = sb("rot", [P, KC, D])
        con = sb("con", [P, NCONSTS])
        scan_on = sb("scan_on", [P, max(EXPERTS), NT])
        row = sb("row", [P, NROWS])
        col = sb("col", [P, NCOLS])
        crep = sb("crep", [P, B])
        c2 = sb("c2", [P, B])
        ring = sb("ring", [P, 4096])
        half = sb("half", [P, 1])
        abel_dot = sb("abel_dot", [P, NT])
        logits = sb("logits", [P, NT, 16])
        top = sb("top", [P, NT, 8])
        top_i = sb("top_i", [P, NT, 8], U32)
        gate_w8 = sb("gate_w8", [P, TOPK, NT])
        pos_i = sb("pos_i", [P, TOPK, NT], I32)
        table = sb("table", [P, 2, max(TILES)], I32)
        small = sb("small", [P, 32])
        small_i = sb("small_i", [P, 4], I32)
        row_sum = sb("row_sum", [P, 2])
        neg_mean = sb("neg_mean", [P, 2])
        sq_sum = sb("sq_sum", [P, 2])
        var = sb("var", [P, 2])
        rstd = sb("rstd", [P, 2])
        inv = sb("inv", [P, 2])
        rot_dot = sb("rot_dot", [P, 2])
        gate = sb("gate", [P, 2])

        def cn(name):
            at, n = CONSTS[name]
            return con[:, at:at + n]

        ident, upper, ones, lane_mask, iota_e, iota_t = (
            cn(n) for n in ("ident", "upper", "ones", "lanes", "iota_e", "iota_t"))

        def r(name):
            at, n = ROWS[name]
            return row[:, at:at + n]

        def cl(name):
            at, n = COLS[name]
            return col[:, at:at + n]

        ab1 = cl("ab1")
        dense_junk = r("ln_g")
        router = [cl("gate_w").rearrange("p (k e) -> p k e", k=KC),
                  cl("router_w").rearrange("p (k e) -> p k e", k=KC)]
        rms = cl("rms").rearrange("p (s k) -> p s k", k=KC)

        def cut(at, n):
            return ring[:, at:at + n], at + n

        at = 0
        v, at = cut(at, 2 * D)
        c_row = v.rearrange("p (s d) -> p s d", s=2)
        v, at = cut(at, 2 * D)
        g_row = v.rearrange("p (s d) -> p s d", s=2)
        v, at = cut(at, 2 * D)
        x_t = v.rearrange("p (s k t) -> p s k t", s=2, k=KC)
        v, at = cut(at, 2 * D)
        m_row = v.rearrange("p (s d) -> p s d", s=2)
        v, at = cut(at, 2 * D)
        m_col = v.rearrange("p (s k t) -> p s k t", s=2, k=KC)
        v, at = cut(at, 2 * D)
        less = v.rearrange("p (s d) -> p s d", s=2)
        v, at = cut(at, 2 * D)
        act_junk, dve_junk = v[:, 0:D], v[:, D:2 * D]
        assert at + D <= 4096
        zeros = ring[:, 4096 - D:4096]
        hid_col = ring[:, :].rearrange("p (c t) -> p c t", c=2 * HC)
        at = 0
        q_row = z_all[:, NT - 2:NT, :]
        v, at = cut(at, 2 * D)
        q_col = v.rearrange("p (s k t) -> p s k t", s=2, k=KC)
        v, at = cut(at, 2 * HID)
        q_hid = v.rearrange("p (s h) -> p s h", s=2)
        v, at = cut(at, 2 * HID)
        q_hidc = v.rearrange("p (s c t) -> p s c t", s=2, c=HC)
        v, at = cut(at, 2 * D)
        q_out = v.rearrange("p (s d) -> p s d", s=2)
        assert at <= 4096

        flat = units[:, :, :].rearrange("p s n -> p (s n)")

        def mats(slot):
            return units[:, slot, :].rearrange("p (g k c) -> p g k c", g=GENS, k=KC)

        A_, AT_, A2_, TR_, PR_, U_ = (mats(s) for s in range(6))
        weff = units[:, 6:8, :].rearrange("p s n -> p (s n)").rearrange("p (b k o) -> p b k o", b=B, k=KC)
        eb1_sb = units[:, 6:8, :].rearrange("p s n -> p (s n)")[:, 0:EXPERTS[0] * HID]
        eb2_sb = z_all[:, 0:EXPERTS[0], :].rearrange("p e d -> p (e d)")
        wbot = units[:, 14:16, :].rearrange("p s n -> p (s n)").rearrange("p (b k o) -> p b k o", b=B, k=KC)
        cond_w = [weff, wbot]
        abel = units[:, 12:14, :].rearrange("p s n -> p (s n)").rearrange("p (t d) -> p t d", t=NT)
        second = units[:, 10:12, :].rearrange("p s n -> p (s n)").rearrange("p (t d) -> p t d", t=NT)
        x_all_t = units[:, 14:16, :].rearrange("p s n -> p (s n)").rearrange("p (t k j) -> p t k j", t=NT, k=KC)
        setup = units[:, 4, :]
        asT = setup[:, 0:D]
        bsT = setup[:, D:2 * D]
        wbaseT = setup[:, 2 * D:4 * D]
        bsw = units[:, 5, :].rearrange("p (b o) -> p b o", b=B)
        masks = units[:, 0:2, :].rearrange("p s n -> p (s n)")
        wfull = units[:, 2:4, :].rearrange("p s n -> p (s n)")
        wch = [wfull[:, q * WCHUNK:(q + 1) * WCHUNK] for q in range(NWCHUNK)]
        mch = [masks[:, q * WCHUNK:(q + 1) * WCHUNK] for q in range(NWCHUNK)]
        kron = units[:, 5, 0:P]
        ident2 = ring[:, 4 * D:6 * D]
        onehot = rot[:, :, :]
        scratch = [units[:, (5, 15)[l], 0:4 * RWIDE].rearrange("p (a n) -> p a n", a=4) for l in range(2)]
        picked = sb("picked", [P, NT, TOPK])
        small_e = sb("small_e", [P, 4, 16])

        ps = [ctx.enter_context(nc.psum_tensor(f"ps{i}", [P, 512], F32)) for i in range(8)]

        s_small = sem("small_loaded")
        s_cond = sem("cond_loaded")
        s_gens = sem("gens_loaded")
        s_units0 = sem("units0_loaded")
        s_eb = sem("expert_biases_loaded")
        s_zero = sem("zeros_made")
        s_qzero = [sem(f"queue_zeroed{l}") for l in range(2)]
        s_rows = sem("rows_loaded")
        s_xt = [sem(f"x_cols_loaded{i}") for i in range(NGROUPS)]
        s_x = [sem(f"x_rows_loaded{i}") for i in range(NGROUPS)]
        s_unit1 = [sem(f"unit1_{i}_loaded") for i in range(SLOTS)]
        s_wc = sem("masked_weights_loaded")
        s_wst = sem("wbot_stored")
        s_id2 = sem("identity2_loaded")
        s_wbot = sem("wbot_loaded")
        s_out = [sem(f"out_stored{i}") for i in range(2)]
        s_prep = sem("prep_steps")
        s_bsw = sem("lora_b_scaled")
        s_weffmm = sem("weff_product")
        s_weff = sem("weff_added")
        s_norm = sem("norm_steps")
        s_allmax = sem("norm_maximum")
        s_scaled = sem("gens_scaled")
        s_prod = sem("exp_products")
        s_tr = sem("exp_transposes")
        s_poly = sem("exp_polynomial_steps")
        s_trc = sem("exp_transposes_copied")
        s_sqp = sem("square_products")
        s_sqc = sem("square_copied")
        s_sqt = sem("square_transposes")
        s_sqtc = sem("square_transposes_copied")
        s_rp = sem("rotation_products")
        s_rc = sem("rotation_copied")
        s_kron = sem("kron_made")
        s_wmul = sem("chunk_masked")
        s_wmm = sem("chunk_product")
        s_wev = sem("chunk_copied")
        s_rms = sem("unit_scaled")

        class Layer:
            pass

        L = []
        for l in range(2):
            y = Layer()
            y.cond_mm = sem(f"cond_product{l}")
            y.stat = sem(f"row_steps{l}")
            y.sq = sem(f"squares_summed{l}")
            y.pow = sem(f"rstd_steps{l}")
            y.norm = sem(f"normalised{l}")
            y.zt = sem(f"z_transposed{l}")
            y.ztc = sem(f"z_transpose_copied{l}")
            y.lg = sem(f"logits_product{l}")
            y.lgc = sem(f"logits_copied{l}")
            y.route = sem(f"route_steps{l}")
            y.expd = sem(f"route_exp{l}")
            y.rank = sem(f"rank_products{l}")
            y.scat = [sem(f"rows_scattered{l}_{i}") for i in range(2)]
            y.qload = [sem(f"queue_tile_loaded{l}_{i}") for i in range(2)]
            y.qt = sem(f"queue_transposed{l}")
            y.qtc = sem(f"queue_transpose_copied{l}")
            y.h = sem(f"hidden_product{l}")
            y.hb = sem(f"hidden_biased{l}")
            y.ha = sem(f"hidden_activated{l}")
            y.ht = sem(f"hidden_transposed{l}")
            y.htc = sem(f"hidden_transpose_copied{l}")
            y.o = sem(f"answer_product{l}")
            y.oc = sem(f"answer_copied{l}")
            y.ostore = [sem(f"answer_stored{l}_{i}") for i in range(2)]
            y.gather = [sem(f"answers_gathered{l}_{g}") for g in range(NGROUPS)]
            y.dh = sem(f"dense_hidden_product{l}")
            y.da = sem(f"dense_hidden_activated{l}")
            y.do = sem(f"dense_product{l}")
            y.doc = sem(f"dense_copied{l}")
            L.append(y)
        s_res = sem("residual_added")
        s_dabel = sem("dense_output_steps")
        s_mixa = sem("mix_first")
        s_mix = sem("mix_both")
        s_mt = sem("mix_transposed")
        s_mtc = sem("mix_transpose_copied")
        s_rot = sem("rotated")
        s_dot = sem("gate_dot")
        s_sig = sem("gate_made")
        s_less = sem("mix_less_dense")
        s_x1 = sem("x1_made")
        s_xtr = sem("x1_transposed")
        s_xtc = sem("x1_transpose_copied")
        s_fin = sem("final_steps")

        FINAL_STEPS = 2
        DABEL_STEPS = 3
        ROW_STEPS = (3, 1)
        POW_STEPS = (2, 3)
        ENTRY_LAG = (0, 5)
        ROUTE_STEPS = (32, 37)
        HID_LAG, HT_LAG, OUT_LAG, STORE_LAG = 2, 3, 4, 5
        BOTH_STEP = 7
        EARLY = EXPERTS[0]

        def all_scattered(eng, y):
            eng.wait_ge(y.scat[0], 16 * TOPK * EARLY)
            eng.wait_ge(y.scat[1], 16 * TOPK * (NT - EARLY))

        block = ctx.enter_context(nc.Block())

        @block.sync
        def _(sp):
            sp.dma_start(crep[:, :], cond).then_inc(s_cond, 16)
            sp.dma_start(setup[:, 0:4 * D], lora).then_inc(s_cond, 16)
            sp.dma_start(row[:, :], rows).then_inc(s_rows, 16)

            def load_x(g):
                at = slice(g * GROUP, (g + 1) * GROUP)
                sp.dma_start(x_all_t[:, at, :, :].rearrange("p t k j -> p t (k j)"),
                             x_cols[at, :, :].rearrange("t p n -> p t n")).then_inc(s_xt[g], 16)
                sp.dma_start(res[:, at, :], x_rows.rearrange("(t p) d -> p t d", p=P)[:, at, :]).then_inc(s_x[g], 16)

            load_x(0)
            sp.dma_start(con[:, :], consts).then_inc(s_small, 16)
            sp.dma_start(col[:, :], cols).then_inc(s_small, 16)
            for g in range(1, NGROUPS):
                load_x(g)
            sp.dma_start(ident2, identity2).then_inc(s_id2, 16)
            sp.dma_start(A_, gens).then_inc(s_gens, 16)
            sp.dma_start(AT_, gens_t).then_inc(s_gens, 16)
            for s in range(6):
                sp.dma_start(units[:, 8 + s, :], units0[s]).then_inc(s_units0, 16)

            def zero_queue(l):
                sp.dma_start(queue[l].rearrange("(n p) d -> p n d", p=P),
                             zeros.unsqueeze(1).broadcast_to([P, TILES[l], D])).then_inc(s_qzero[l], 16)

            sp.wait_ge(s_zero, 2)
            zero_queue(0)
            sp.wait_ge(L[0].cond_mm, NT)
            for s in range(6, 8):
                sp.dma_start(units[:, 8 + s, :], units0[s]).then_inc(s_units0, 16)
            sp.dma_start(eb1_sb, eb1).then_inc(s_eb, 16)
            zero_queue(1)
            sp.wait_ge(L[0].scat[0], 16 * TOPK * EARLY)
            sp.dma_start(eb2_sb, eb2).then_inc(s_eb, 16)

            def routed(l):
                y = L[l]
                all_scattered(sp, y)

                def step(st):
                    if st.has(0):
                        s, t = st.slot(0), st.tile(0)
                        after(sp, y.qt, st, 0, 2)
                        sp.dma_start(q_row[:, s, :], queue[l][bass.ds(t * P, P), :]).then_inc(y.qload[s], 16)
                    if st.has(STORE_LAG):
                        s, t = st.slot(STORE_LAG), st.tile(STORE_LAG)
                        sp.wait_ge(y.oc, t + 1)
                        sp.dma_start(answer[l][bass.ds(t * P, P), :], q_out[:, s, :]).then_inc(y.ostore[s], 16)

                pipeline(sp, TILES[l], STORE_LAG, step)

            sp.wait_ge(s_rc, 3)
            sp.dma_start(wfull, w1c).then_inc(s_wc, 16)
            for g in range(B):
                sp.dma_start(masks[g * LANES:(g + 1) * LANES, :], mask1c).then_inc(s_wc, 16)
            routed(0)
            tb = WCHUNK // D
            for q in range(NWCHUNK):
                sp.wait_ge(s_wev, 2 * q + 2)
                for b in range(B):
                    sp.dma_start(
                        wbot_dram[b].rearrange("(tb tl) o -> tl tb o", tl=LANES)[:, q * tb:(q + 1) * tb, :],
                        mch[q][b * LANES:(b + 1) * LANES, :].rearrange("p (tb o) -> p tb o", tb=tb)
                    ).then_inc(s_wst, 16)

            sp.wait_ge(L[0].o, TILES[0])
            sp.wait_ge(L[0].oc, TILES[0])
            sp.wait_ge(s_wst, 16 * B * NWCHUNK)
            for s in range(8):
                sp.dma_start(units[:, s, :], units1[s]).then_inc(s_unit1[s], 16)
                if s == 1:
                    for b in range(B):
                        sp.dma_start(wbot[:, b, :, :], wbot_dram[b].rearrange("(k p) o -> p k o", p=P)).then_inc(s_wbot, 16)
            sp.wait_ge(L[0].do, NT)
            for s in (8, 9):
                sp.dma_start(units[:, s, :], units1[s]).then_inc(s_unit1[s], 16)
            sp.wait_ge(s_mix, NT)
            sp.wait_ge(s_x1, NT)
            sp.wait_ge(L[1].cond_mm, NT)
            for s in range(10, SLOTS):
                if s == SLOTS - 1:
                    sp.wait_ge(L[1].route, ROUTE_STEPS[1])
                sp.dma_start(units[:, s, :], units1[s]).then_inc(s_unit1[s], 16)
            routed(1)
            out_v = out.rearrange("(n p) d -> n p d", p=P)

            def store(st):
                if st.has(0):
                    s, t = st.slot(0), st.tile(0)
                    sp.wait_ge(s_fin, (t + 1) * FINAL_STEPS)
                    sp.dma_start(out_v[bass.ds(t, 1), :, :].rearrange("a p d -> (a p) d"),
                                 res[:, bass.ds(t, 1), :].rearrange("p a d -> p (a d)")).then_inc(s_out[s], 16)

            pipeline(sp, NT, 0, store)
            for s in range(2):
                sp.wait_ge(s_out[s], 16 * NT // 2)

        @block.gpsimd
        def _(pool):
            nc.gpsimd.memset(half[:, :], -0.5).then_inc(s_zero, 1)
            pool.wait_ge(s_zero, 2)

            def entry(l):
                y, q = L[l], ENTRY_LAG[l]
                powers = Chain(pool, y.pow, POW_STEPS[l])

                def step(st):
                    if not st.has(q):
                        return
                    s, t = st.slot(q), st.tile(q)
                    powers.start(t)
                    pool.wait_ge(y.sq, t + 1)
                    after(pool, y.norm, st, q, 2)
                    if l == 1:
                        after(pool, y.lgc, st, q, 2)
                    powers.then(nc.gpsimd.tensor_scalar(var[:, s:s + 1], sq_sum[:, s:s + 1], 1.0 / D,
                                                        (1e-5, 1.1920929e-07)[l], ALU.mult, ALU.add))
                    powers.did(nc.gpsimd.tensor_tensor(rstd[:, s:s + 1], var[:, s:s + 1], half[:, :], ALU.pow))
                    if l == 1:
                        powers.wait()
                        powers.did(nc.gpsimd.tensor_tensor(inv[:, s:s + 1], var[:, s:s + 1], rstd[:, s:s + 1], ALU.mult))
                    if l == 0:
                        pool.wait_ge(s_x[t // GROUP], 16)
                        nc.gpsimd.tensor_tensor(res[:, t, :], c_row[:, s, :], res[:, t, :], ALU.add).then_inc(s_res, 1)

                unrolled(NT, q, step)

            def scatter(l):
                y = L[l]
                pool.wait_ge(y.route, ROUTE_STEPS[l])
                pool.wait_ge(y.norm, NT)
                pool.wait_ge(s_qzero[l], 16)
                for t in range(NT):
                    for k in range(TOPK):
                        nc.gpsimd.indirect_dma_start(
                            queue[l], bass.IndirectOffsetOnAxis(pos_i[:, k, t:t + 1].bitcast(U32), 0),
                            z_all[:, t, :], None).then_inc(y.scat[t >= EARLY], 16)

            def gather(l):
                y = L[l]
                for s in range(2):
                    pool.wait_ge(y.ostore[s], 16 * TILES[l] // 2)
                if l == 0:
                    pool.wait_ge(y.oc, TILES[0])
                if l == 1:
                    all_scattered(pool, y)
                for t in range(NT):
                    for k in range(TOPK):
                        to = z_all[:, t, :] if k == 0 else second[:, t, :]
                        nc.gpsimd.indirect_dma_start(
                            to, None, answer[l],
                            bass.IndirectOffsetOnAxis(pos_i[:, k, t:t + 1].bitcast(U32), 0)).then_inc(y.gather[t // GROUP], 16)

            entry(0)
            pool.wait_ge(s_norm, 2)
            nc.gpsimd.partition_all_reduce(small[:, 1:2], small[:, 0:1], P, RMAX).then_inc(s_allmax, 1)
            scatter(0)
            gather(0)
            entry(1)
            scatter(1)
            gather(1)

        @block.scalar
        def _(act):
            def entry(l):
                y, q = L[l], ENTRY_LAG[l]

                def step(st):
                    if st.has(q + 2):
                        t = st.tile(q + 2)
                        act.wait_ge(y.zt, t + 1)
                        nc.scalar.copy(znt[:, :, t * P:(t + 1) * P],
                                       ps[(6, 5)[l]][:, 0:D].rearrange("p (k j) -> p k j", k=KC)).then_inc(y.ztc, 1)
                    if l == 1 and st.has(4):
                        s, t = st.slot(4), st.tile(4)
                        act.wait_ge(s_xtr, t + 1)
                        after(act, y.cond_mm, st, 4, 2)
                        nc.scalar.copy(x_t[:, s, :, :].rearrange("p k t -> p (k t)"), ps[2][:, 0:D]).then_inc(s_xtc, 1)
                    if l == 1 and st.has(2):
                        s, t = st.slot(2), st.tile(2)
                        act.wait_ge(s_dot, t + 1)
                        after(act, s_x1, st, 2, 2)
                        nc.scalar.activation(gate[:, s:s + 1], rot_dot[:, s:s + 1], ACT.Sigmoid,
                                             bias=abel_dot[:, t:t + 1]).then_inc(s_sig, 1)
                    if l == 1 and st.has(1):
                        s, t = st.slot(1), st.tile(1)
                        act.wait_ge(s_mt, t + 1)
                        after(act, s_rot, st, 1, 2)
                        nc.scalar.copy(m_col[:, s, :, :].rearrange("p k t -> p (k t)"), ps[0][:, 0:D]).then_inc(s_mtc, 1)
                    if st.has(q):
                        s, t = st.slot(q), st.tile(q)
                        act.wait_ge(y.stat, t * ROW_STEPS[l] + (2, 1)[l])
                        after(act, y.pow, st, q, 2, POW_STEPS[l])
                        after(act, y.sq, st, q, 1)
                        if l == 0:
                            nc.scalar.activation(act_junk, c_row[:, s, :], ACT.Square, bias=neg_mean[:, s:s + 1],
                                                 accum_out=sq_sum[:, s:s + 1]).then_inc(y.sq, 1)
                        else:
                            nc.scalar.activation(act_junk, c_row[:, s, :], ACT.Square,
                                                 accum_out=sq_sum[:, s:s + 1]).then_inc(y.sq, 1)
                    if l == 1 and st.has(0):
                        s, t = st.slot(0), st.tile(0)
                        act.wait_ge(L[0].gather[t // GROUP], 16 * TOPK * GROUP)
                        after(act, s_mt, st, 0, 2)
                        nc.scalar.activation(m_row[:, s, :], z_all[:, t, :], ACT.Identity,
                                             scale=gate_w8[:, 0, t:t + 1]).then_inc(s_mixa, 1)

                if l == 1:
                    act.wait_ge(L[0].do, NT)
                    act.wait_ge(s_dabel, NT * DABEL_STEPS)
                unrolled(NT, q + 2, step)

            def route_exp(l):
                y = L[l]
                act.wait_ge(y.route, 3)
                e2 = scratch[l][:, 2, 0:NT]
                nc.scalar.activation(e2, e2, ACT.Exp).then_inc(y.expd, 1)
                if l == 1:
                    e = scratch[l][:, 1, 0:NT * EXPERTS[1]]
                    nc.scalar.activation(e, e, ACT.Exp).then_inc(y.expd, 1)

            def exponentials():
                for stage in range(3):
                    dst, done = ((TR_, s_trc), (TR_, s_trc), (AT_, s_sqtc))[stage]
                    for g in range(GENS):
                        act.wait_ge(s_tr, stage * GENS + g + 1)
                        if stage == 1:
                            act.wait_ge(s_prod, GENS + g + 1)
                        nc.scalar.copy(dst[:, g, :, :].rearrange("p k c -> p (k c)"), ps[4 + g][:, :]).then_inc(done, 1)
                turns = act.value_load(small_i[0:1, 1:2], min_val=1, max_val=100)
                with act.Fori(0, turns) as i:
                    for g in range(GENS):
                        act.wait_ge(s_sqt, GENS * i + g + 1)
                        nc.scalar.copy(AT_[:, g, :, :].rearrange("p k c -> p (k c)"), ps[4 + g][:, :]).then_inc(s_sqtc, 1)

            def routed(l):
                y = L[l]

                def step(st):
                    if st.has(HID_LAG):
                        s, t = st.slot(HID_LAG), st.tile(HID_LAG)
                        if l == 0:
                            act.wait_ge(y.hb, t + 1)
                            nc.scalar.activation(q_hid[:, s, :], q_hid[:, s, :], ACT.Gelu).then_inc(y.ha, 1)
                        else:
                            act.wait_ge(y.h, t + 1)
                            after(act, y.ht, st, HID_LAG, 2)
                            nc.scalar.activation(q_hid[:, s, :], ps[2 + s][:, :], ACT.Silu).then_inc(y.ha, 1)
                    if l == 0 and st.has(HT_LAG):
                        s, t = st.slot(HT_LAG), st.tile(HT_LAG)
                        act.wait_ge(y.ht, t + 1)
                        after(act, y.o, st, HT_LAG, 2)
                        nc.scalar.copy(q_hidc[:, s, :, :].rearrange("p c t -> p (c t)"), ps[4 + s][:, :]).then_inc(y.htc, 1)
                    if l == 0 and st.has(0):
                        s, t = st.slot(0), st.tile(0)
                        act.wait_ge(y.qt, t + 1)
                        after(act, y.h, st, 0, 2)
                        nc.scalar.copy(q_col[:, s, :, :].rearrange("p k t -> p (k t)"), ps[s][:, 0:D]).then_inc(y.qtc, 1)

                pipeline(act, TILES[l], STORE_LAG, step)

            def dense(l, blocks, after_routed):
                y = L[l]
                if after_routed:
                    for s in range(2):
                        act.wait_ge(y.ostore[s], 16 * TILES[l] // 2)

                def one(i):
                    for c in range(2 * HC):
                        act.wait_ge(y.dh, 2 * HC * i + c + 1)
                        if l == 0:
                            nc.scalar.activation(hid_col[:, c, :], ps[2 + c % 4][:, :], ACT.Gelu,
                                                 bias=ab1[:, c:c + 1]).then_inc(y.da, 1)
                        else:
                            nc.scalar.activation(hid_col[:, c, :], ps[2 + c % 4][:, :], ACT.Silu).then_inc(y.da, 1)

                if len(blocks) == 1:
                    one(blocks[0])
                else:
                    with act.Fori(blocks[0], blocks[-1] + 1) as i:
                        one(i)

            entry(0)
            route_exp(0)
            exponentials()
            routed(0)
            dense(0, range(NBLK), True)
            entry(1)
            route_exp(1)
            dense(1, range(DENSE_BEFORE[1]), False)
            routed(1)
            dense(1, range(DENSE_BEFORE[1], NBLK), True)

        @block.vector
        def _(dve):
            V = nc.vector

            def rows_at(buf, t):
                return buf[:, bass.ds(t, 1), :].rearrange("p a d -> p (a d)")

            def prepare():
                V.memset(zeros, 0.0).then_inc(s_zero, 1)
                V.memset(logits[:, :, :], -1e30).then_inc(s_prep, 1)
                V.memset(scan_on[:, :, :], 1.0).then_inc(s_prep, 1)
                dve.wait_ge(s_prep, 2)
                V.memset(scan_on[:, :, 0:1], 0.0).then_inc(s_prep, 1)
                dve.wait_ge(s_cond, 32)
                V.tensor_scalar(c2[:, :], crep[:, :], 2.0, None, ALU.mult).then_inc(s_prep, 1)
                dve.wait_ge(s_prep, 4)
                for b in range(B):
                    V.tensor_scalar(bsw[:, b, :], bsT, c2[:, b:b + 1], None, ALU.mult).then_inc(s_bsw, 1)
                for b in range(B):
                    dve.wait_ge(s_weffmm, b + 1)
                    V.tensor_tensor(weff[:, b, :, :].rearrange("p k o -> p (k o)"), ps[b % 4][:, :], wbaseT,
                                    ALU.add).then_inc(s_weff, 1)
                dve.wait_ge(s_rows, 16)

            def entry(l):
                y, q = L[l], ENTRY_LAG[l]
                stat = Chain(dve, y.stat, ROW_STEPS[l])
                E = EXPERTS[l]

                def step(st):
                    if st.has(q + 3):
                        s, t = st.slot(q + 3), st.tile(q + 3)
                        dve.wait_ge(y.lg, t + 1)
                        if l == 0:
                            V.tensor_tensor(logits[:, t, 0:E], ps[7][:, 0:E], r("gate_b")[:, 0:E], ALU.add).then_inc(y.lgc, 1)
                        else:
                            dve.wait_ge(y.pow, (t + 1) * POW_STEPS[1])
                            V.tensor_scalar(logits[:, t, 0:E], ps[6][:, 0:E], inv[:, s:s + 1], None, ALU.mult).then_inc(y.lgc, 1)
                    if st.has(q + 1):
                        s, t = st.slot(q + 1), st.tile(q + 1)
                        dve.wait_ge(y.pow, t * POW_STEPS[l] + 2)
                        dve.wait_ge(y.stat, (t + 1) * ROW_STEPS[l])
                        if l == 0:
                            V.scalar_tensor_tensor(z_all[:, t, :], g_row[:, s, :], rstd[:, s:s + 1], r("ln_b"),
                                                   ALU.mult, ALU.add).then_inc(y.norm, 1)
                        else:
                            V.tensor_scalar(z_all[:, t, :], c_row[:, s, :], rstd[:, s:s + 1], None, ALU.mult
                                            ).then_inc(y.norm, 1)
                    if st.has(q):
                        s, t = st.slot(q), st.tile(q)
                        stat.start(t)
                        dve.wait_ge(y.cond_mm, t + 1)
                        after(dve, y.sq, st, q, 2)
                        after(dve, y.norm, st, q, 2)
                        if l == 0:
                            after(dve, s_res, st, q, 2)
                            stat.then(V.scalar_tensor_tensor(c_row[:, s, :], ps[t % 4][:, 0:D], 1.0, r("b_base"),
                                                             ALU.mult, ALU.add, accum_out=row_sum[:, s:s + 1]))
                            stat.then(V.tensor_scalar(neg_mean[:, s:s + 1], row_sum[:, s:s + 1], -1.0 / D, None, ALU.mult))
                            stat.did(V.scalar_tensor_tensor(g_row[:, s, :], c_row[:, s, :], neg_mean[:, s:s + 1], r("ln_g"),
                                                            ALU.add, ALU.mult))
                        else:
                            stat.did(V.tensor_tensor(c_row[:, s, :], ps[3 + s][:, 0:D], r("bias1"), ALU.add))
                    if l == 1 and st.has(2):
                        s, t = st.slot(2), st.tile(2)
                        dve.wait_ge(s_rot, t + 1)
                        after(dve, s_sig, st, 2, 2)
                        after(dve, s_dot, st, 2, 1)
                        V.scalar_tensor_tensor(dve_junk, ps[(1, 7)[s]][:, 0:D], 1.0, r("gate_nonabel"),
                                               ALU.mult, ALU.mult, accum_out=rot_dot[:, s:s + 1]).then_inc(s_dot, 1)
                        after(dve, s_x1, st, 2, 2)
                        V.tensor_tensor(less[:, s, :], ps[(1, 7)[s]][:, 0:D], abel[:, t, :], ALU.subtract).then_inc(s_less, 1)
                    if l == 1 and st.has(0):
                        s, t = st.slot(0), st.tile(0)
                        dve.wait_ge(s_mixa, t + 1)
                        V.scalar_tensor_tensor(m_row[:, s, :], second[:, t, :], gate_w8[:, 1, t:t + 1],
                                               m_row[:, s, :], ALU.mult, ALU.add).then_inc(s_mix, 1)
                    if l == 1 and st.has(2):
                        s, t = st.slot(2), st.tile(2)
                        dve.wait_ge(s_sig, t + 1)
                        dve.wait_ge(s_less, t + 1)
                        V.scalar_tensor_tensor(res[:, t, :], less[:, s, :], gate[:, s:s + 1], res[:, t, :],
                                               ALU.mult, ALU.add).then_inc(s_x1, 1)

                unrolled(NT, q + 3, step)

            def route(l):
                y, E, NQ = L[l], EXPERTS[l], TILES[l]
                ch = Chain(dve, y.route, ROUTE_STEPS[l])
                ch.start(0)

                def te(v):
                    return v.rearrange("p (t e) -> p t e", e=E)

                def et(v):
                    return v.rearrange("p (e t) -> p e t", t=NT)

                both, tot = (scratch[l][:, a, 0:NT * E] for a in range(2))
                first, other = (onehot[:, k, 0:NT * E] for k in range(TOPK))
                cum = scratch[l][:, 3, 0:NT * E]
                e2, den, w_a, w_b = (scratch[l][:, 2, a * NT:(a + 1) * NT] for a in range(4))
                dve.wait_ge(y.lgc, NT)
                wide = 8 if l == 0 else 16
                for t in range(NT):
                    i = V.max(top[:, t, :], logits[:, t, 0:wide])
                ch.then(i)
                for t in range(NT):
                    i = V.max_index(top_i[:, t, :], top[:, t, :], logits[:, t, 0:wide])
                ch.then(i)
                if l == 1:
                    V.tensor_tensor(te(tot), logits[:, :, 0:E], top[:, :, 0:1].broadcast_to([P, NT, E]), ALU.subtract)
                ch.then(V.tensor_tensor(e2.unsqueeze(2), top[:, :, 1:2], top[:, :, 0:1], ALU.subtract))
                ch.then(V.tensor_copy(picked[:, :, :], top_i[:, :, 0:TOPK]))
                for k, v in enumerate((first, other)):
                    ch.did(V.tensor_tensor(te(v), iota_e[:, 0:E].unsqueeze(1).broadcast_to([P, NT, E]),
                                           picked[:, :, k:k + 1].broadcast_to([P, NT, E]), ALU.is_equal))
                ch.wait()
                ch.then(V.tensor_tensor(both, first, other, ALU.add))
                assert ch.k == BOTH_STEP
                dve.wait_ge(y.expd, 1 + l)
                if l == 0:
                    ch.then(V.tensor_scalar(den, e2, 1.0, None, ALU.add))
                    ch.then(V.reciprocal(gate_w8[:, 0, :], den))
                    ch.then(V.tensor_tensor(gate_w8[:, 1, :], e2, gate_w8[:, 0, :], ALU.mult))
                else:
                    ch.then(V.tensor_reduce(den, te(tot), AX.X, ALU.add))
                    ch.then(V.reciprocal(w_a, den))
                    ch.then(V.tensor_tensor(w_b, e2, w_a, ALU.mult))
                    ch.then(V.tensor_tensor(den, w_a, w_b, ALU.add))
                    ch.then(V.tensor_scalar(den, den, 1e-9, None, ALU.add))
                    ch.then(V.reciprocal(e2, den))
                    ch.then(V.tensor_tensor(gate_w8[:, 0, :], w_a, e2, ALU.mult))
                    ch.then(V.tensor_tensor(gate_w8[:, 1, :], w_b, e2, ALU.mult))
                dve.wait_ge(y.rank, 2)
                ch.then(V.tensor_copy(et(tot), ps[7][:, 0:NT * E].rearrange("p (t e) -> p e t", e=E)))
                ch.then(V.tensor_tensor_scan(cum, scan_on[:, 0:E, :].rearrange("p e t -> p (e t)"), tot, 0.0,
                                             ALU.mult, ALU.add))
                count = et(cum)[:, :, NT - 1:NT].rearrange("p e a -> p (e a)")
                tiles_i, tiles, ends, start = (small_e[:, a, 0:E] for a in range(4))
                tiles_i = tiles_i.bitcast(I32)
                ch.then(V.tensor_scalar(tiles_i, count, float(P - 1), None, ALU.add))
                ch.then(V.tensor_scalar(tiles_i, tiles_i, 7, None, ALU.logical_shift_right))
                ch.then(V.tensor_copy(tiles, tiles_i))
                ch.then(V.tensor_tensor_scan(ends, scan_on[:, 0, 1:2].broadcast_to([P, E]), tiles, 0.0, ALU.mult, ALU.add))
                ch.then(V.tensor_tensor(start, ends, tiles, ALU.subtract))
                ch.then(V.tensor_scalar(start, start, float(P), None, ALU.mult))
                ch.then(V.tensor_tensor(cum, cum, tot, ALU.subtract))
                ch.then(V.tensor_tensor(et(cum), et(cum), start.unsqueeze(2).broadcast_to([P, E, NT]), ALU.add))
                ch.then(V.tensor_tensor(te(tot), te(ps[6][:, 0:NT * E]), cum.rearrange("p (e t) -> p t e", t=NT), ALU.add))
                for k, v in enumerate((first, other)):
                    ch.then(V.tensor_tensor(te(v), te(v), te(tot), ALU.mult))
                    ch.then(V.tensor_reduce(cum[:, k * NT:(k + 1) * NT], te(v), AX.X, ALU.add))
                    ch.then(V.tensor_copy(pos_i[:, k, :], cum[:, k * NT:(k + 1) * NT]))
                at_or_before = scratch[l][:, 0:3, :].rearrange("p a n -> p (a n)")[:, 0:NQ * E].rearrange("p (q e) -> p q e", e=E)
                ch.then(V.tensor_tensor(at_or_before, iota_t[:, 0:NQ].unsqueeze(2).broadcast_to([P, NQ, E]),
                                        ends.unsqueeze(1).broadcast_to([P, NQ, E]), ALU.is_ge))
                which = scratch[l][:, 3, 64:64 + NQ]
                ch.then(V.tensor_reduce(which, at_or_before, AX.X, ALU.add))
                ch.then(V.tensor_scalar(which, which, float(E - 1), None, ALU.min))
                ch.then(V.tensor_scalar(table[:, 0, 0:NQ], which, float(UNIT), float(EXPERT_SLOT[l] * UNIT), ALU.mult, ALU.add))
                ch.then(V.tensor_scalar(table[:, 1, 0:NQ], which, float(D), None, ALU.mult))
                assert ch.k == ROUTE_STEPS[l], ch.k

            def exponentials():
                steps = Chain(dve, s_poly, 64)
                steps.start(0)
                dve.wait_ge(s_gens, 32)
                V.tensor_reduce(small[:, 4:4 + GENS * KC], A_.rearrange("p g k c -> p (g k) c"), AX.X, ALU.add,
                                apply_absolute_value=True).then_inc(s_norm, 1)
                dve.wait_ge(s_norm, 1)
                V.tensor_reduce(small[:, 0:1], small[:, 4:4 + GENS * KC], AX.X, ALU.max).then_inc(s_norm, 1)
                dve.wait_ge(s_allmax, 1)
                n = Chain(dve, s_norm, 16)
                n.start(0)
                n.k = 2
                n.then(V.tensor_scalar(small_i[:, 0:1], small[:, 1:2].bitcast(I32), 23, None, ALU.logical_shift_right))
                n.then(V.tensor_scalar(small_i[:, 1:2], small_i[:, 0:1], -126.0, 1.0, ALU.add, ALU.max))
                n.then(V.tensor_scalar(small_i[:, 1:2], small_i[:, 1:2], 100.0, None, ALU.min))
                n.then(V.tensor_scalar(small_i[:, 2:3], small_i[:, 1:2], -1.0, 127.0, ALU.mult, ALU.add))
                n.then(V.tensor_scalar(small_i[:, 3:4], small_i[:, 2:3], 23, None, ALU.logical_shift_left))
                scale = small_i[:, 3:4].bitcast(F32)
                for v in (A_, AT_):
                    w = v.rearrange("p g k c -> p (g k c)")
                    V.tensor_scalar(w, w, scale, None, ALU.mult).then_inc(s_scaled, 1)
                dve.wait_ge(s_scaled, 2)

                def m(v, g):
                    return v[:, g, :, :].rearrange("p k c -> p (k c)")

                def stt(o, a, c, b):
                    return V.scalar_tensor_tensor(o, a, c, b, ALU.mult, ALU.add)

                for g in range(GENS):
                    dve.wait_ge(s_prod, g + 1)
                    steps.then(V.tensor_copy(m(A2_, g), ps[g][:, :]))
                for g in range(GENS):
                    steps.did(stt(m(PR_, g), m(A_, g), X1 / X2, m(A2_, g)))
                dve.wait_ge(s_id2, 16)
                for g in range(GENS):
                    dve.wait_ge(s_prod, GENS + g + 1)
                    steps.did(stt(m(U_, g), m(A2_, g), X3 / X2, ps[g][:, :]))
                    steps.then(stt(m(PR_, g), m(A_, g), X5 / X6, m(A2_, g)))
                    steps.then(stt(m(PR_, g), ident2, X4 / X6, m(PR_, g)))
                    steps.did(stt(m(PR_, g), ps[g][:, :], X7 * X2 / X6, m(PR_, g)))
                    steps.then(stt(m(A_, g), m(A2_, g), Y2, m(A_, g)))
                    steps.then(V.tensor_tensor(m(A_, g), m(A_, g), ident2, ALU.add))
                for g in range(GENS):
                    dve.wait_ge(s_prod, 2 * GENS + g + 1)
                    steps.then(stt(m(A_, g), ps[g][:, :], X2 * X6, m(A_, g)))
                turns = dve.value_load(small_i[0:1, 1:2], min_val=1, max_val=100)
                with dve.Fori(0, turns) as i:
                    for g in range(GENS):
                        dve.wait_ge(s_sqp, GENS * i + g + 1)
                        V.tensor_copy(m(A_, g), ps[g][:, :]).then_inc(s_sqc, 1)
                for j, (to, bank) in enumerate(((m(A2_, 0), 0), (m(A2_, 1), 1), (rot[:, :, :].rearrange("p k c -> p (k c)"), 2))):
                    dve.wait_ge(s_rp, j + 1)
                    V.tensor_copy(to, ps[bank][:, :]).then_inc(s_rc, 1)

            def masked_weights():
                dve.wait_ge(s_rc, 3)
                V.tensor_tensor(kron.rearrange("p (b t) -> p b t", t=LANES),
                                lane_mask.unsqueeze(1).broadcast_to([P, B, LANES]),
                                crep[:, :].unsqueeze(2).broadcast_to([P, B, LANES]), ALU.mult).then_inc(s_kron, 1)
                dve.wait_ge(s_wc, 16 * (B + 1))
                for q in range(NWCHUNK):
                    V.tensor_tensor(wch[q], wch[q], mch[q], ALU.mult).then_inc(s_wmul, 1)
                for q in range(NWCHUNK):
                    for a in range(2):
                        dve.wait_ge(s_wmm, 2 * q + a + 1)
                        V.tensor_copy(mch[q][:, a * 512:(a + 1) * 512], ps[2 * q + a][:, :]).then_inc(s_wev, 1)

            def routed(l):
                y = L[l]
                if l == 0:
                    dve.wait_ge(s_eb, 32)

                def step(st):
                    if l == 0 and st.has(HID_LAG):
                        s, t = st.slot(HID_LAG), st.tile(HID_LAG)
                        at = dve.value_load(table[0:1, 1, bass.ds(t, 1)], min_val=0, max_val=(EXPERTS[0] - 1) * D)
                        dve.wait_ge(y.h, t + 1)
                        after(dve, y.ht, st, HID_LAG, 2)
                        V.tensor_tensor(q_hid[:, s, :], ps[2 + s][:, :], eb1_sb[:, bass.ds(at * 2, HID)], ALU.add).then_inc(y.hb, 1)
                    if l == 1 and st.has(HT_LAG):
                        s, t = st.slot(HT_LAG), st.tile(HT_LAG)
                        dve.wait_ge(y.ht, t + 1)
                        after(dve, y.o, st, HT_LAG, 2)
                        V.tensor_copy(q_hidc[:, s, :, :].rearrange("p c t -> p (c t)"), ps[4 + s][:, :]).then_inc(y.htc, 1)
                    if l == 1 and st.has(0):
                        s, t = st.slot(0), st.tile(0)
                        dve.wait_ge(y.qt, t + 1)
                        after(dve, y.h, st, 0, 2)
                        V.tensor_copy(q_col[:, s, :, :].rearrange("p k t -> p (k t)"), ps[s][:, 0:D]).then_inc(y.qtc, 1)
                    if st.has(OUT_LAG):
                        s, t = st.slot(OUT_LAG), st.tile(OUT_LAG)
                        if l == 0:
                            at = dve.value_load(table[0:1, 1, bass.ds(t, 1)], min_val=0, max_val=(EXPERTS[0] - 1) * D)
                        dve.wait_ge(y.o, t + 1)
                        if st.i is not None or st.k - OUT_LAG >= 2:
                            dve.wait_ge(y.ostore[s], 16 * st.turn(OUT_LAG))
                        if l == 0:
                            V.tensor_tensor(q_out[:, s, :], ps[6 + s][:, 0:D], eb2_sb[:, bass.ds(at, D)], ALU.add).then_inc(y.oc, 1)
                        else:
                            V.tensor_copy(q_out[:, s, :], ps[6 + s][:, 0:D]).then_inc(y.oc, 1)

                pipeline(dve, TILES[l], STORE_LAG, step)

            def scale_unit(u):
                dve.wait_ge(s_unit1[u], 16)
                for k in range(KC):
                    w = units[:, u, k * HID:(k + 1) * HID]
                    V.tensor_scalar(w, w, rms[:, u, k:k + 1], None, ALU.mult).then_inc(s_rms, 1)

            def dense(l, blocks, scaled):
                y = L[l]
                if blocks[0] == 0:
                    dve.sem_inc(y.doc, 1)
                    dabel = Chain(dve, s_dabel, DABEL_STEPS)
                    if l == 0:
                        dve.wait_ge(s_res, NT)
                for i in blocks:
                    for u in scaled[i - blocks[0]]:
                        scale_unit(u)
                    for t in range(4 * i, 4 * i + 4):
                        dve.wait_ge(y.do, t + 1)
                        if l == 1:
                            V.tensor_tensor(res[:, t, :], ps[6 + t % 2][:, 0:D], res[:, t, :], ALU.add).then_inc(y.doc, 1)
                            continue
                        V.tensor_tensor(abel[:, t, :], ps[6 + t % 2][:, 0:D], r("ab2"), ALU.add).then_inc(y.doc, 1)
                        dve.wait_ge(y.doc, t + 2)
                        dabel.start(t)
                        dabel.then(V.scalar_tensor_tensor(dense_junk, abel[:, t, :], 1.0, r("gate_abel"),
                                                          ALU.mult, ALU.mult, accum_out=abel_dot[:, t:t + 1]))
                        dabel.did(V.tensor_scalar(abel_dot[:, t:t + 1], abel_dot[:, t:t + 1], r("gate_c")[:, 0:1], None, ALU.add))
                        dabel.did(V.tensor_tensor(res[:, t, :], abel[:, t, :], res[:, t, :], ALU.add))

            def final(tiles):
                fin = Chain(dve, s_fin, FINAL_STEPS)
                for t in tiles:
                    fin.start(t)
                    dve.wait_ge(L[1].gather[t // GROUP], 16 * TOPK * GROUP)
                    dve.wait_ge(L[1].doc, t + 2)
                    fin.then(V.scalar_tensor_tensor(res[:, t, :], z_all[:, t, :], gate_w8[:, 0, t:t + 1],
                                                    res[:, t, :], ALU.mult, ALU.add))
                    fin.did(V.scalar_tensor_tensor(res[:, t, :], second[:, t, :], gate_w8[:, 1, t:t + 1],
                                                   res[:, t, :], ALU.mult, ALU.add))

            prepare()
            entry(0)
            route(0)
            exponentials()
            routed(0)
            masked_weights()
            dense(0, range(NBLK), [(2 * i, 2 * i + 1) for i in range(NBLK)])
            entry(1)
            route(1)
            dense(1, range(DENSE_BEFORE[1]), [(8, 9), (10, 11, 12), (13, 14, 15)])
            routed(1)
            ready = GROUP * 2
            final(range(0, ready))
            dense(1, range(DENSE_BEFORE[1], NBLK), [()])
            final(range(ready, NT))

        @block.tensor
        def _(pe):
            mm = nc.tensor.matmul

            def layer0_weights():
                pe.wait_ge(s_cond, 32)
                for b in range(B):
                    pe.wait_ge(s_bsw, b + 1)
                    if b >= 4:
                        pe.wait_ge(s_weff, b - 3)
                    for k in range(KC):
                        i = mm(ps[b % 4][:, k * D:(k + 1) * D], asT[:, k * P:(k + 1) * P], bsw[:, b, :], start=True, stop=True)
                    i.then_inc(s_weffmm, 1)

            def transpose2(bank, rows2, done):
                for k in range(KC):
                    i = nc.tensor.transpose(bank[:, k * P:(k + 1) * P], rows2[:, k * P:(k + 1) * P], ident)
                i.then_inc(done, 1)

            def entry(l):
                y, q = L[l], ENTRY_LAG[l]
                E = EXPERTS[l]

                def step(st):
                    if st.has(q + 3):
                        t = st.tile(q + 3)
                        pe.wait_ge(y.ztc, t + 1)
                        after(pe, y.lgc, st, q + 3, 1)
                        for k in range(KC):
                            i = mm(ps[(7, 6)[l]][:, 0:E], znt[:, k, t * P:(t + 1) * P], router[l][:, k, :],
                                   start=(k == 0), stop=(k == KC - 1))
                        i.then_inc(y.lg, 1)
                    if st.has(q + 2):
                        t = st.tile(q + 2)
                        pe.wait_ge(y.norm, t + 1)
                        after(pe, y.ztc, st, q + 2, 1)
                        transpose2(ps[(6, 5)[l]], z_all[:, t, :], y.zt)
                    if st.has(q):
                        s, t = st.slot(q), st.tile(q)
                        if l == 0:
                            pe.wait_ge(s_xt[t // GROUP], 16)
                            pe.wait_ge(s_weff, B)
                            after(pe, y.stat, st, q, 4, ROW_STEPS[l])
                            bank = ps[t % 4]
                        else:
                            pe.wait_ge(s_xtc, t + 1)
                            after(pe, y.stat, st, q, 2, ROW_STEPS[l])
                            bank = ps[3 + s]
                        for k in range(KC):
                            lhs = x_all_t[:, t, k, :] if l == 0 else x_t[:, s, k, :]
                            i = mm(bank[:, 0:D], lhs, cond_w[l][:, t // PER_BATCH, k, :], start=(k == 0), stop=(k == KC - 1))
                        i.then_inc(y.cond_mm, 1)
                    if l == 1 and st.has(4):
                        t = st.tile(4)
                        pe.wait_ge(s_x1, t + 1)
                        after(pe, s_xtc, st, 4, 1)
                        transpose2(ps[2], res[:, t, :], s_xtr)
                    if l == 1 and st.has(2):
                        s, t = st.slot(2), st.tile(2)
                        pe.wait_ge(s_mtc, t + 1)
                        after(pe, s_less, st, 2, 2)
                        for k in range(KC):
                            i = mm(ps[(1, 7)[s]][:, 0:D], m_col[:, s, k, :], rot[:, k, :], start=(k == 0), stop=(k == KC - 1))
                        i.then_inc(s_rot, 1)
                    if l == 1 and st.has(1):
                        s, t = st.slot(1), st.tile(1)
                        pe.wait_ge(s_mix, t + 1)
                        after(pe, s_mtc, st, 1, 1)
                        transpose2(ps[0], m_row[:, s, :], s_mt)

                unrolled(NT, q + 3, step)

            def rank(l):
                y, n = L[l], NT * EXPERTS[l]
                pe.wait_ge(y.route, BOTH_STEP)
                both = scratch[l][:, 0, 0:n]
                mm(ps[6][:, 0:n], upper, both, start=True, stop=True).then_inc(y.rank, 1)
                mm(ps[7][:, 0:n], ones, both, start=True, stop=True).then_inc(y.rank, 1)

            def product(bank, xt, y):
                for mc in range(KC):
                    for k in range(KC):
                        i = mm(bank[:, mc * D:(mc + 1) * D], xt[:, k, mc * P:(mc + 1) * P], y[:, k, :],
                               start=(k == 0), stop=(k == KC - 1))
                return i

            def turned(bank, x):
                for k in range(KC):
                    for mc in range(KC):
                        i = nc.tensor.transpose(bank[:, k * D + mc * P:k * D + (mc + 1) * P],
                                                x[:, mc, k * P:(k + 1) * P], ident)
                return i

            def exponentials():
                pe.wait_ge(s_scaled, 2)
                for g in range(GENS):
                    product(ps[g], AT_[:, g], A_[:, g]).then_inc(s_prod, 1)
                for g in range(GENS):
                    pe.wait_ge(s_poly, g + 1)
                    turned(ps[4 + g], A2_[:, g]).then_inc(s_tr, 1)
                for g in range(GENS):
                    pe.wait_ge(s_poly, GENS + g + 1)
                    pe.wait_ge(s_trc, g + 1)
                    product(ps[g], TR_[:, g], PR_[:, g]).then_inc(s_prod, 1)
                for g in range(GENS):
                    pe.wait_ge(s_poly, 2 * GENS + 6 * g + 1)
                    turned(ps[4 + g], U_[:, g]).then_inc(s_tr, 1)
                for g in range(GENS):
                    pe.wait_ge(s_poly, 2 * GENS + 6 * g + 4)
                    pe.wait_ge(s_trc, GENS + g + 1)
                    product(ps[g], TR_[:, g], PR_[:, g]).then_inc(s_prod, 1)
                for g in range(GENS):
                    pe.wait_ge(s_poly, 8 * GENS + g + 1)
                    turned(ps[4 + g], A_[:, g]).then_inc(s_tr, 1)
                turns = pe.value_load(small_i[0:1, 1:2], min_val=1, max_val=100)
                with pe.Fori(0, turns) as i:
                    for g in range(GENS):
                        pe.wait_ge(s_sqtc, GENS * i + g + 1)
                        product(ps[g], AT_[:, g], A_[:, g]).then_inc(s_sqp, 1)
                    for g in range(GENS):
                        pe.wait_ge(s_sqc, GENS * i + g + 1)
                        turned(ps[4 + g], A_[:, g]).then_inc(s_sqt, 1)
                pe.wait_ge(s_sqtc, GENS * turns + GENS)
                product(ps[0], A_[:, 1], AT_[:, 0]).then_inc(s_rp, 1)
                product(ps[1], AT_[:, 2], A_[:, 3]).then_inc(s_rp, 1)
                pe.wait_ge(s_rc, 2)
                product(ps[2], A2_[:, 0], A2_[:, 1]).then_inc(s_rp, 1)
                pe.wait_ge(s_rc, 3)

            def masked_weights():
                pe.wait_ge(s_kron, 1)
                pe.wait_ge(L[0].oc, TILES[0])
                for q in range(NWCHUNK):
                    pe.wait_ge(s_wmul, q + 1)
                    for a in range(2):
                        mm(ps[2 * q + a][:, :], kron, wch[q][:, a * 512:(a + 1) * 512], start=True, stop=True
                           ).then_inc(s_wmm, 1)
                pe.wait_ge(s_wev, 2 * NWCHUNK)

            def routed(l):
                y = L[l]
                top_at = (EXPERT_SLOT[l] + EXPERTS[l] - 1) * UNIT

                def unit_of(t):
                    return pe.value_load(table[0:1, 0, bass.ds(t, 1)], min_val=EXPERT_SLOT[l] * UNIT, max_val=top_at)

                def step(st):
                    if st.has(HID_LAG):
                        s, t = st.slot(HID_LAG), st.tile(HID_LAG)
                        at = unit_of(t)
                        pe.wait_ge(y.qtc, t + 1)
                        after(pe, y.hb if l == 0 else y.ha, st, HID_LAG, 2)
                        for k in range(KC):
                            i = mm(ps[2 + s][:, :], q_col[:, s, k, :], flat[:, bass.ds(at + k * HID, HID)],
                                   start=(k == 0), stop=(k == KC - 1))
                        i.then_inc(y.h, 1)
                    if st.has(HT_LAG):
                        s, t = st.slot(HT_LAG), st.tile(HT_LAG)
                        pe.wait_ge(y.ha, t + 1)
                        after(pe, y.htc, st, HT_LAG, 2)
                        for c in range(HC):
                            i = nc.tensor.transpose(ps[4 + s][:, c * P:(c + 1) * P], q_hid[:, s, c * P:(c + 1) * P], ident)
                        i.then_inc(y.ht, 1)
                    if st.has(0):
                        s, t = st.slot(0), st.tile(0)
                        pe.wait_ge(y.qload[s], 16 * (st.turn(0) + 1))
                        after(pe, y.qtc, st, 0, 2)
                        transpose2(ps[s], q_row[:, s, :], y.qt)
                    if st.has(OUT_LAG):
                        s, t = st.slot(OUT_LAG), st.tile(OUT_LAG)
                        at = unit_of(t)
                        pe.wait_ge(y.htc, t + 1)
                        after(pe, y.oc, st, OUT_LAG, 2)
                        for c in range(HC):
                            i = mm(ps[6 + s][:, 0:D], q_hidc[:, s, c, :], flat[:, bass.ds(at + W2_AT + c * D, D)],
                                   start=(c == 0), stop=(c == HC - 1))
                        i.then_inc(y.o, 1)

                if l == 0:
                    pe.wait_ge(s_units0, 128)
                else:
                    pe.wait_ge(s_rms, SLOTS * KC)
                pipeline(pe, TILES[l], STORE_LAG, step)
                pe.wait_ge(y.oc, TILES[l])

            def dense(l, blocks):
                y = L[l]
                if l == 1:
                    pe.wait_ge(s_rms, 2 * KC)
                pe.wait_ge(y.ztc, NT)

                def one(i):
                    for c in range(2 * HC):
                        u = DENSE_SLOT[l] + c // HC
                        if c >= 4:
                            pe.wait_ge(y.da, 2 * HC * i + c - 3)
                        for k in range(KC):
                            at = k * HID + (c % HC) * P
                            m = mm(ps[2 + c % 4][:, :], units[:, u, at:at + P], znt[:, k, bass.ds(i * BLK, BLK)],
                                   start=(k == 0), stop=(k == KC - 1))
                        m.then_inc(y.dh, 1)
                    pe.wait_ge(y.route, ROUTE_STEPS[l])
                    for j in range(4):
                        pe.wait_ge(y.doc, 1 + 4 * i + max(j - 1, 0))
                        for c in range(2 * HC):
                            u = DENSE_SLOT[l] + c // HC
                            if j == 0:
                                pe.wait_ge(y.da, 2 * HC * i + c + 1)
                            at = W2_AT + (c % HC) * D
                            m = mm(ps[6 + j % 2][:, 0:D], hid_col[:, c, j * P:(j + 1) * P], units[:, u, at:at + D],
                                   start=(c == 0), stop=(c == 2 * HC - 1))
                        m.then_inc(y.do, 1)

                if len(blocks) == 1:
                    one(blocks[0])
                else:
                    with pe.Fori(blocks[0], blocks[-1] + 1) as i:
                        one(i)
                pe.wait_ge(y.doc, 1 + 4 * (blocks[-1] + 1))

            layer0_weights()
            pe.wait_ge(s_weff, B)
            pe.wait_ge(s_small, 32)
            entry(0)
            rank(0)
            pe.wait_ge(L[0].lgc, NT)
            exponentials()
            routed(0)
            masked_weights()
            dense(0, range(NBLK))
            pe.wait_ge(s_wbot, 16 * B)
            entry(1)
            rank(1)
            dense(1, range(DENSE_BEFORE[1]))
            routed(1)
            dense(1, range(DENSE_BEFORE[1], NBLK))


def constants():
    parts = {"ident": np.eye(P), "upper": np.triu(np.ones((P, P)), 1), "ones": 1.0,
             "lanes": np.arange(P)[:, None] % LANES == np.arange(LANES)[None, :],
             "iota_e": np.arange(16), "iota_t": np.arange(max(TILES))}
    c = np.zeros((P, NCONSTS), np.float32)
    for name, v in parts.items():
        at, n = CONSTS[name]
        c[:, at:at + n] = v
    identity2 = np.zeros((P, KC, D), np.float32)
    for k in range(KC):
        identity2[:, k, k * P:(k + 1) * P] = np.eye(P)
    return c, identity2.reshape(P, KC * D)


def kernel(**inputs):
    import concourse.bacc as bacc
    from concourse.bass_utils import run_bass_kernel_spmd

    a = {k: np.asarray(v) for k, v in inputs.items()}

    def chunks(m):
        return m.reshape(-1, P, m.shape[1]).transpose(1, 0, 2).reshape(P, -1)

    def unit(w1, w2):
        return np.concatenate([chunks(w1), chunks(w2)], axis=1)

    x = a["x"]
    aw1, aw2 = a["L0_ffn_aw1"], a["L0_ffn_aw2"]
    units0 = [unit(aw1[:, h * HID:(h + 1) * HID], aw2[h * HID:(h + 1) * HID]) for h in range(2)]
    units0 += [unit(a["L0_ffn_ew1"][e], a["L0_ffn_ew2"][e]) for e in range(EXPERTS[0])]
    units1 = [unit(a["L1_ffn_w1_s"][e], a["L1_ffn_w2_s"][e]) for e in range(2)]
    units1 += [unit(a["L1_ffn_w1"][e], a["L1_ffn_w2"][e]) for e in range(EXPERTS[1])]
    rms = np.concatenate([a["L1_ffn_rms_w_s"], a["L1_ffn_rms_w"]])
    parts = {"b_base": a["L0_cond_b_base"], "ln_g": a["L0_ffn_ln_g"], "ln_b": a["L0_ffn_ln_b"], "ab2": a["L0_ffn_ab2"], "gate_abel": a["L0_ffn_gc_w"][0:D, 0],
             "gate_nonabel": a["L0_ffn_gc_w"][D:2 * D, 0], "bias1": a["L1_cond_bias"], "gate_b": a["L0_ffn_gate_b"],
             "gate_c": a["L0_ffn_gc_b"]}
    rows = np.zeros((1, NROWS), np.float32)
    for name, v in parts.items():
        rows[0, ROWS[name][0]:ROWS[name][0] + v.size] = v
    parts = {"ab1": chunks(a["L0_ffn_ab1"][:, None]), "gate_w": chunks(a["L0_ffn_gate_w"]),
             "router_w": chunks(a["L1_ffn_router_w"]), "rms": rms.reshape(SLOTS, KC, P).transpose(2, 0, 1).reshape(P, -1)}
    cols = np.zeros((P, NCOLS), np.float32)
    for name, v in parts.items():
        cols[:, COLS[name][0]:COLS[name][0] + v.shape[1]] = v
    gens = a["L0_ffn_gens"]
    con, identity2 = constants()
    arrays = {
        "x_rows": x.reshape(T, D),
        "x_cols": x.reshape(NT, P, KC, P).transpose(0, 3, 2, 1).reshape(NT, P, D),
        "cond": np.repeat(a["cond_8"].T, LANES, axis=0),
        "lora": np.concatenate([a["L0_cond_As"].reshape(P, D), a["L0_cond_Bs"].transpose(0, 2, 1).reshape(P, D),
                                chunks(a["L0_cond_W_base"].T)], axis=1),
        "rows": np.repeat(rows, P, axis=0),
        "cols": cols,
        "units0": np.stack(units0),
        "units1": np.stack(units1),
        "eb1": np.repeat(a["L0_ffn_eb1"].reshape(1, -1), P, axis=0),
        "eb2": np.repeat(a["L0_ffn_eb2"].reshape(1, -1), P, axis=0),
        "gens": gens.reshape(GENS, KC, P, D).transpose(2, 0, 1, 3),
        "gens_t": gens.transpose(0, 2, 1).reshape(GENS, KC, P, D).transpose(2, 0, 1, 3),
        "w1c": a["L1_cond_weight"].transpose(0, 2, 1).reshape(B, TBLOCKS, LANES, D).transpose(0, 2, 1, 3).reshape(P, -1),
        "mask1c": a["L1_cond_mask"].T.reshape(TBLOCKS, LANES, D).transpose(1, 0, 2).reshape(LANES, -1),
        "consts": con,
        "identity2": identity2,
    }
    nc = bacc.Bacc("TRN2", target_bir_lowering=False, num_devices=1)
    feeds, args = {}, []
    for name, v in arrays.items():
        feeds[f"in_{name}"] = np.ascontiguousarray(v)
        args.append(nc.dram_tensor(f"in_{name}", v.shape, F32, kind="ExternalInput").ap())
    out = nc.dram_tensor("out_rows", (T, D), F32, kind="ExternalOutput").ap()
    two_layers(nc, *args, out)
    result = run_bass_kernel_spmd(nc, [feeds], core_ids=[0])
    return result.results[0]["out_rows"].reshape(B, TOK, D)
```

```python
import math
from contextlib import ExitStack

import concourse.bass as bass
import numpy as np
from concourse import mybir

F32 = mybir.dt.float32
I32 = mybir.dt.int32
U32 = mybir.dt.uint32
ALU = mybir.AluOpType
ACT = mybir.ActivationFunctionType
AX = mybir.AxisListType
RMAX = bass.bass_isa.ReduceOp.max

P = 128
B, TOK, D = 8, 256, 256
T = B * TOK
NT = T // P
PER_BATCH = TOK // P
KC = D // P
HID = 512
HC = HID // P
UNIT = KC * HID + HC * D
W2_AT = KC * HID
SLOTS = 16
TOPK = 2
BLK = 512
NBLK = T // BLK
GENS = 4
LANES = 16
TBLOCKS = D // LANES
WCHUNK = 1024
RWIDE = (NT * 7, NT * 14)
NWCHUNK = TBLOCKS * D // WCHUNK
GROUP = 4
NGROUPS = NT // GROUP
WARM_UP = 4
DENSE_BEFORE = (0, 2)

EXPERTS = (6, 14)
DENSE_SLOT = (8, 0)
EXPERT_SLOT = (10, 2)


def routed_tiles(n_experts):
    n = (TOPK * T + n_experts * (P - 1)) // P
    return n + n % 2


TILES = tuple(routed_tiles(e) for e in EXPERTS)

_Q = math.sqrt(177.0)
X3 = 2.0 / 3.0
X1 = X3 * (1 + _Q) / 88
X2 = X3 * (1 + _Q) / 352
X4 = (-271 + 29 * _Q) / (315 * X3)
X5 = 11 * (-1 + _Q) / (1260 * X3)
X6 = 11 * (-9 + _Q) / (5040 * X3)
X7 = (89 - _Q) / (5040 * X3 * X3)
Y2 = (857 - 58 * _Q) / 630

CONSTS = {}
for _name, _n in (("ident", P), ("upper", P), ("ones", P), ("lanes", LANES), ("iota_e", 16), ("iota_t", max(TILES))):
    _at = sum(n for _, n in CONSTS.values())
    CONSTS[_name] = (_at, _n)
NCONSTS = sum(n for _, n in CONSTS.values())

ROWS = {}
for _name, _n in (("b_base", D), ("ln_g", D), ("ln_b", D), ("ab2", D), ("gate_abel", D), ("gate_nonabel", D), ("bias1", D),
                  ("gate_b", 8), ("gate_c", 8)):
    _at = sum(n for _, n in ROWS.values())
    ROWS[_name] = (_at, _n)
NROWS = sum(n for _, n in ROWS.values())

COLS = {}
for _name, _n in (("ab1", 2 * HC), ("gate_w", KC * EXPERTS[0]),
                  ("router_w", KC * EXPERTS[1]), ("rms", SLOTS * KC)):
    _at = sum(n for _, n in COLS.values())
    COLS[_name] = (_at, _n)
NCOLS = sum(n for _, n in COLS.values())


class Step:

    def __init__(self, n, k, i=None):
        self.n, self.k, self.i = n, k, i

    def has(self, lag):
        return self.i is not None or 0 <= self.k - lag < self.n

    def tile(self, lag):
        return self.k - lag + (0 if self.i is None else self.i * 2)

    def slot(self, lag):
        return (self.k - lag) % 2

    def turn(self, lag):
        return (self.k - lag) // 2 + (0 if self.i is None else self.i)


def unrolled(n, lags, step):
    for k in range(n + lags):
        step(Step(n, k))


def pipeline(eng, n, lags, step):
    lead = lags + 2 + lags % 2
    for k in range(lead):
        step(Step(n, k))
    with eng.Fori(0, (n - lead) // 2) as i:
        for k in range(2):
            step(Step(n, lead + k, i))
    for k in range(n, n + lags):
        step(Step(n, k))


class Chain:

    def __init__(self, eng, sem, per):
        self.eng, self.sem, self.per = eng, sem, per
        self.base, self.k = 0, 0

    def start(self, item):
        self.base, self.k = item * self.per, 0

    def did(self, instruction):
        self.k += 1
        assert self.k <= self.per
        instruction.then_inc(self.sem, 1)

    def wait(self):
        self.eng.wait_ge(self.sem, self.base + self.k)

    def then(self, instruction):
        self.did(instruction)
        self.wait()


def after(eng, sem, step, lag, back, per=1):
    if step.i is None and step.k - lag - back < 0:
        return
    eng.wait_ge(sem, (step.tile(lag) - back + 1) * per)


def two_layers(nc, x_rows, x_cols, cond, lora, rows, cols, units0, units1, eb1, eb2, gens, gens_t,
               w1c, mask1c, consts, identity2, out):
    ctx = ExitStack()
    with ctx:
        def sb(name, shape, dt=F32):
            return ctx.enter_context(nc.sbuf_tensor(name, shape, dt))

        def sem(name):
            return ctx.enter_context(nc.semaphore(name))

        queue = [nc.dram_tensor(f"queue{l}", (TILES[l] * P, D), F32, kind="Internal").ap() for l in range(2)]
        answer = [nc.dram_tensor(f"answer{l}", (TILES[l] * P, D), F32, kind="Internal").ap() for l in range(2)]
        wbot_dram = nc.dram_tensor("wbot", (B, D, D), F32, kind="Internal").ap()

        units = sb("units", [P, SLOTS, UNIT])
        z_all = sb("z_all", [P, NT, D])
        znt = sb("znt", [P, KC, T])
        res = sb("res", [P, NT, D])
        rot = sb("rot", [P, KC, D])
        con = sb("con", [P, NCONSTS])
        scan_on = sb("scan_on", [P, max(EXPERTS), NT])
        row = sb("row", [P, NROWS])
        col = sb("col", [P, NCOLS])
        crep = sb("crep", [P, B])
        c2 = sb("c2", [P, B])
        ring = sb("ring", [P, 4096])
        half = sb("half", [P, 1])
        abel_dot = sb("abel_dot", [P, NT])
        logits = sb("logits", [P, NT, 16])
        top = sb("top", [P, NT, 8])
        top_i = sb("top_i", [P, NT, 8], U32)
        gate_w8 = sb("gate_w8", [P, TOPK, NT])
        pos_i = sb("pos_i", [P, TOPK, NT], I32)
        table = sb("table", [P, 2, max(TILES)], I32)
        small = sb("small", [P, 32])
        small_i = sb("small_i", [P, 4], I32)
        row_sum = sb("row_sum", [P, 2])
        neg_mean = sb("neg_mean", [P, 2])
        sq_sum = sb("sq_sum", [P, 2])
        var = sb("var", [P, 2])
        rstd = sb("rstd", [P, 2])
        inv = sb("inv", [P, NT])
        rot_dot = sb("rot_dot", [P, 2])
        gate = sb("gate", [P, 2])

        def cn(name):
            at, n = CONSTS[name]
            return con[:, at:at + n]

        ident, upper, ones, lane_mask, iota_e, iota_t = (
            cn(n) for n in ("ident", "upper", "ones", "lanes", "iota_e", "iota_t"))

        def r(name):
            at, n = ROWS[name]
            return row[:, at:at + n]

        def cl(name):
            at, n = COLS[name]
            return col[:, at:at + n]

        ab1 = cl("ab1")
        dense_junk = r("ln_g")
        router = [cl("gate_w").rearrange("p (k e) -> p k e", k=KC),
                  cl("router_w").rearrange("p (k e) -> p k e", k=KC)]
        rms = cl("rms").rearrange("p (s k) -> p s k", k=KC)

        def cut(at, n):
            return ring[:, at:at + n], at + n

        at = 0
        v, at = cut(at, 2 * D)
        c_row = v.rearrange("p (s d) -> p s d", s=2)
        v, at = cut(at, 2 * D)
        g_row = v.rearrange("p (s d) -> p s d", s=2)
        v, at = cut(at, 2 * D)
        x_t = v.rearrange("p (s k t) -> p s k t", s=2, k=KC)
        v, at = cut(at, 2 * D)
        m_col = v.rearrange("p (s k t) -> p s k t", s=2, k=KC)
        v, at = cut(at, 2 * D)
        less = v.rearrange("p (s d) -> p s d", s=2)
        v, at = cut(at, 2 * D)
        act_junk, dve_junk = v[:, 0:D], v[:, D:2 * D]
        assert at + D <= 4096
        zeros = ring[:, 4096 - D:4096]
        hid_col = ring[:, :].rearrange("p (c t) -> p c t", c=2 * HC)
        at = 0
        q_row = z_all[:, NT - 2:NT, :]
        v, at = cut(at, 2 * D)
        q_col = v.rearrange("p (s k t) -> p s k t", s=2, k=KC)
        v, at = cut(at, 2 * HID)
        q_hid = v.rearrange("p (s h) -> p s h", s=2)
        v, at = cut(at, 2 * HID)
        q_hidc = v.rearrange("p (s c t) -> p s c t", s=2, c=HC)
        v, at = cut(at, 2 * D)
        q_out = v.rearrange("p (s d) -> p s d", s=2)
        assert at <= 4096

        flat = units[:, :, :].rearrange("p s n -> p (s n)")

        def mats(slot):
            return units[:, slot, :].rearrange("p (g k c) -> p g k c", g=GENS, k=KC)

        A_, AT_, A2_, TR_, PU_, V_ = (mats(s) for s in range(6))
        weff = units[:, 6:8, :].rearrange("p s n -> p (s n)").rearrange("p (b k o) -> p b k o", b=B, k=KC)
        eb1_sb = units[:, 6:8, :].rearrange("p s n -> p (s n)")[:, 0:EXPERTS[0] * HID]
        eb2_sb = z_all[:, 0:EXPERTS[0], :].rearrange("p e d -> p (e d)")
        wbot = units[:, 14:16, :].rearrange("p s n -> p (s n)").rearrange("p (b k o) -> p b k o", b=B, k=KC)
        cond_w = [weff, wbot]
        abel = units[:, 12:14, :].rearrange("p s n -> p (s n)").rearrange("p (t d) -> p t d", t=NT)
        second = units[:, 10:12, :].rearrange("p s n -> p (s n)").rearrange("p (t d) -> p t d", t=NT)
        x_all_t = units[:, 14:16, :].rearrange("p s n -> p (s n)").rearrange("p (t k j) -> p t k j", t=NT, k=KC)
        setup = units[:, 4, :]
        asT = setup[:, 0:D]
        bsT = setup[:, D:2 * D]
        wbaseT = setup[:, 2 * D:4 * D]
        bsw = units[:, 5, :].rearrange("p (b o) -> p b o", b=B)
        masks = units[:, 0:2, :].rearrange("p s n -> p (s n)")
        wfull = units[:, 2:4, :].rearrange("p s n -> p (s n)")
        wch = [wfull[:, q * WCHUNK:(q + 1) * WCHUNK] for q in range(NWCHUNK)]
        mch = [masks[:, q * WCHUNK:(q + 1) * WCHUNK] for q in range(NWCHUNK)]
        kron = units[:, 5, 0:P]
        ident2 = ring[:, 6 * D:8 * D]
        y2_a2 = ring[:, 8 * D:10 * D]
        onehot = rot[:, :, :]
        scratch = []
        for l, (slot, at) in enumerate(((7, EXPERTS[0] * HID - UNIT), (15, 0))):
            scratch.append(units[:, slot, at:at + 6 * RWIDE[l]].rearrange("p (a n) -> p a n", a=6))
        picked = sb("picked", [P, NT, TOPK])
        small_e = sb("small_e", [P, 4, 16])

        ps = [ctx.enter_context(nc.psum_tensor(f"ps{i}", [P, 512], F32)) for i in range(8)]

        s_small = sem("small_loaded")
        s_cond = sem("cond_loaded")
        s_gens = sem("gens_loaded")
        s_gens_t = sem("transposed_gens_loaded")
        s_units0 = sem("units0_loaded")
        s_eb = sem("expert_biases_loaded")
        s_zero = sem("zeros_made")
        s_qzero = [sem(f"queue_zeroed{l}") for l in range(2)]
        s_rows = sem("rows_loaded")
        s_xt = [sem(f"x_cols_loaded{i}") for i in range(NGROUPS)]
        s_x = [sem(f"x_rows_loaded{i}") for i in range(NGROUPS)]
        s_unit1 = [sem(f"unit1_{i}_loaded") for i in range(SLOTS)]
        s_wc = sem("masked_weights_loaded")
        s_wst = sem("wbot_stored")
        s_id2 = sem("identity2_loaded")
        s_wbot = sem("wbot_loaded")
        s_out = [sem(f"out_stored{i}") for i in range(2)]
        s_prep = sem("prep_steps")
        s_bsw = sem("lora_b_scaled")
        s_weffmm = sem("weff_product")
        s_weff = sem("weff_added")
        s_norm = sem("norm_steps")
        s_allmax = sem("norm_maximum")
        s_scaled = sem("gens_scaled")
        s_prod = sem("exp_products")
        s_tr = sem("exp_transposes")
        s_poly = sem("exp_polynomial_steps")
        s_low = sem("exp_low_terms")
        s_trc = sem("exp_transposes_copied")
        s_sqp = sem("square_products")
        s_sqc = sem("square_copied")
        s_sqt = sem("square_transposes")
        s_sqtc = sem("square_transposes_copied")
        s_rp = sem("rotation_products")
        s_rc = sem("rotation_copied")
        s_kron = sem("kron_made")
        s_wmul = sem("chunk_masked")
        s_wmm = sem("chunk_product")
        s_wev = sem("chunk_copied")
        s_rms = sem("unit_scaled")

        class Layer:
            pass

        L = []
        for l in range(2):
            y = Layer()
            y.cond_mm = sem(f"cond_product{l}")
            y.stat = sem(f"row_steps{l}")
            y.sq = sem(f"squares_summed{l}")
            y.pow = sem(f"rstd_steps{l}")
            y.norm = sem(f"normalised{l}")
            y.zt = sem(f"z_transposed{l}")
            y.ztc = sem(f"z_transpose_copied{l}")
            y.lg = sem(f"logits_product{l}")
            y.lgc = sem(f"logits_copied{l}")
            y.route = sem(f"route_steps{l}")
            y.expd = sem(f"route_exp{l}")
            y.ranked = sem(f"ranks_copied{l}")
            y.rank = sem(f"rank_products{l}")
            y.scat = [sem(f"rows_scattered{l}_{i}") for i in range(2)]
            y.qload = [sem(f"queue_tile_loaded{l}_{i}") for i in range(2)]
            y.qt = sem(f"queue_transposed{l}")
            y.qtc = sem(f"queue_transpose_copied{l}")
            y.h = sem(f"hidden_product{l}")
            y.hb = sem(f"hidden_biased{l}")
            y.ha = sem(f"hidden_activated{l}")
            y.ht = sem(f"hidden_transposed{l}")
            y.htc = sem(f"hidden_transpose_copied{l}")
            y.o = sem(f"answer_product{l}")
            y.oc = sem(f"answer_copied{l}")
            y.ostore = [sem(f"answer_stored{l}_{i}") for i in range(2)]
            y.gather = [sem(f"answers_gathered{l}_{g}") for g in range(NGROUPS)]
            y.dh = sem(f"dense_hidden_product{l}")
            y.da = sem(f"dense_hidden_activated{l}")
            y.do = sem(f"dense_product{l}")
            y.doc = sem(f"dense_copied{l}")
            L.append(y)
        s_res = sem("residual_added")
        s_dabel = sem("dense_output_steps")
        s_mixa = sem("mix_first")
        s_mix = sem("mix_both")
        s_mt = sem("mix_transposed")
        s_mtc = sem("mix_transpose_copied")
        s_rot = sem("rotated")
        s_dot = sem("gate_dot")
        s_sig = sem("gate_made")
        s_less = sem("mix_less_dense")
        s_x1 = sem("x1_made")
        s_xtr = sem("x1_transposed")
        s_xtc = sem("x1_transpose_copied")
        s_fin = sem("final_steps")

        FINAL_STEPS = 2
        DABEL_STEPS = 3
        ROW_STEPS = (3, 1)
        POW_STEPS = (2, 3)
        ENTRY_LAG = (0, 4)
        ROUTE_STEPS = (32, 37)
        HID_LAG, HT_LAG, OUT_LAG, STORE_LAG = 2, 3, 4, 5
        BOTH_STEP = 7
        SCALE_AT = 5
        EARLY = EXPERTS[0]

        def all_scattered(eng, y):
            eng.wait_ge(y.scat[0], 16 * TOPK * EARLY)
            eng.wait_ge(y.scat[1], 16 * TOPK * (NT - EARLY))

        block = ctx.enter_context(nc.Block())

        @block.sync
        def _(sp):
            sp.dma_start(crep[:, :], cond).then_inc(s_cond, 16)
            sp.dma_start(setup[:, 0:4 * D], lora).then_inc(s_cond, 16)
            sp.dma_start(A_, gens).then_inc(s_gens, 16)
            sp.dma_start(row[:, :], rows).then_inc(s_rows, 16)

            def load_x(g):
                at = slice(g * GROUP, (g + 1) * GROUP)
                sp.dma_start(x_all_t[:, at, :, :].rearrange("p t k j -> p t (k j)"),
                             x_cols[at, :, :].rearrange("t p n -> p t n")).then_inc(s_xt[g], 16)
                sp.dma_start(res[:, at, :], x_rows.rearrange("(t p) d -> p t d", p=P)[:, at, :]).then_inc(s_x[g], 16)

            load_x(0)
            sp.dma_start(con[:, :], consts).then_inc(s_small, 16)
            sp.dma_start(col[:, :], cols).then_inc(s_small, 16)
            for g in range(1, NGROUPS):
                load_x(g)
            sp.dma_start(ident2, identity2).then_inc(s_id2, 16)
            sp.dma_start(AT_, gens_t).then_inc(s_gens_t, 16)
            for s in range(6):
                sp.dma_start(units[:, 8 + s, :], units0[s]).then_inc(s_units0, 16)

            def zero_queue(l):
                sp.dma_start(queue[l].rearrange("(n p) d -> p n d", p=P),
                             zeros.unsqueeze(1).broadcast_to([P, TILES[l], D])).then_inc(s_qzero[l], 16)

            sp.wait_ge(s_zero, 2)
            zero_queue(0)
            sp.wait_ge(L[0].cond_mm, NT)
            for s in range(6, 8):
                sp.dma_start(units[:, 8 + s, :], units0[s]).then_inc(s_units0, 16)
            sp.dma_start(eb1_sb, eb1).then_inc(s_eb, 16)
            zero_queue(1)
            sp.wait_ge(L[0].scat[0], 16 * TOPK * EARLY)
            sp.dma_start(eb2_sb, eb2).then_inc(s_eb, 16)

            def load_masked(q):
                if q == 0:
                    sp.wait_ge(s_rc, 2)
                at = slice(q * WCHUNK, (q + 1) * WCHUNK)
                sp.dma_start(wch[q], w1c[:, at]).then_inc(s_wc, 16)
                sp.dma_start(mch[q], mask1c[:, at]).then_inc(s_wc, 16)

            def routed(l):
                y = L[l]
                all_scattered(sp, y)

                def step(st):
                    if st.has(0):
                        s, t = st.slot(0), st.tile(0)
                        after(sp, y.qt, st, 0, 2)
                        sp.dma_start(q_row[:, s, :], queue[l][bass.ds(t * P, P), :]).then_inc(y.qload[s], 16)
                    if l == 0 and st.i is None and 2 <= st.k < 2 + NWCHUNK:
                        load_masked(st.k - 2)
                    if st.has(STORE_LAG):
                        s, t = st.slot(STORE_LAG), st.tile(STORE_LAG)
                        sp.wait_ge(y.oc, t + 1)
                        sp.dma_start(answer[l][bass.ds(t * P, P), :], q_out[:, s, :]).then_inc(y.ostore[s], 16)

                pipeline(sp, TILES[l], STORE_LAG, step)

            routed(0)
            tb = WCHUNK // D
            for q in range(NWCHUNK):
                sp.wait_ge(s_wev, 2 * q + 2)
                for b in range(B):
                    sp.dma_start(
                        wbot_dram[b].rearrange("(tb tl) o -> tl tb o", tl=LANES)[:, q * tb:(q + 1) * tb, :],
                        mch[q][b * LANES:(b + 1) * LANES, :].rearrange("p (tb o) -> p tb o", tb=tb)
                    ).then_inc(s_wst, 16)

            sp.wait_ge(L[0].o, TILES[0])
            sp.wait_ge(L[0].oc, TILES[0])
            sp.wait_ge(s_wst, 16 * B * NWCHUNK)
            sp.wait_ge(s_rc, 3)
            for s in range(8):
                sp.dma_start(units[:, s, :], units1[s]).then_inc(s_unit1[s], 16)
                if s == 1:
                    for b in range(B):
                        sp.dma_start(wbot[:, b, :, :], wbot_dram[b].rearrange("(k p) o -> p k o", p=P)).then_inc(s_wbot, 16)
            sp.wait_ge(L[0].do, NT)
            for s in (8, 9):
                sp.dma_start(units[:, s, :], units1[s]).then_inc(s_unit1[s], 16)
            sp.wait_ge(s_mix, NT)
            sp.wait_ge(s_x1, NT)
            sp.wait_ge(L[1].cond_mm, NT)
            for s in range(10, SLOTS):
                if s == SLOTS - 1:
                    sp.wait_ge(L[1].route, ROUTE_STEPS[1])
                sp.dma_start(units[:, s, :], units1[s]).then_inc(s_unit1[s], 16)
            routed(1)
            out_v = out.rearrange("(n p) d -> n p d", p=P)

            def store(st):
                if st.has(0):
                    s, t = st.slot(0), st.tile(0)
                    sp.wait_ge(s_fin, (t + 1) * FINAL_STEPS)
                    sp.dma_start(out_v[bass.ds(t, 1), :, :].rearrange("a p d -> (a p) d"),
                                 res[:, bass.ds(t, 1), :].rearrange("p a d -> p (a d)")).then_inc(s_out[s], 16)

            pipeline(sp, NT, 0, store)
            for s in range(2):
                sp.wait_ge(s_out[s], 16 * NT // 2)

        @block.gpsimd
        def _(pool):
            nc.gpsimd.memset(half[:, :], -0.5).then_inc(s_zero, 1)
            pool.wait_ge(s_zero, 2)

            def entry(l):
                y, q = L[l], ENTRY_LAG[l]
                powers = Chain(pool, y.pow, POW_STEPS[l])

                def step(st):
                    if l == 0 and st.k == 0:
                        pool.wait_ge(s_norm, 3)
                        nc.gpsimd.partition_all_reduce(small[:, 1:2], small[:, 0:1], P, RMAX).then_inc(s_allmax, 1)
                    if not st.has(q):
                        return
                    s, t = st.slot(q), st.tile(q)
                    powers.start(t)
                    pool.wait_ge(y.sq, t + 1)
                    after(pool, y.norm, st, q, 2)
                    powers.then(nc.gpsimd.tensor_scalar(var[:, s:s + 1], sq_sum[:, s:s + 1], 1.0 / D,
                                                        (1e-5, 1.1920929e-07)[l], ALU.mult, ALU.add))
                    powers.did(nc.gpsimd.tensor_tensor(rstd[:, s:s + 1], var[:, s:s + 1], half[:, :], ALU.pow))
                    if l == 1:
                        powers.wait()
                        powers.did(nc.gpsimd.tensor_tensor(inv[:, t:t + 1], var[:, s:s + 1], rstd[:, s:s + 1], ALU.mult))
                    if l == 0:
                        pool.wait_ge(s_x[t // GROUP], 16)
                        nc.gpsimd.tensor_tensor(res[:, t, :], c_row[:, s, :], res[:, t, :], ALU.add).then_inc(s_res, 1)

                unrolled(NT, q, step)

            def low_terms():
                pool.wait_ge(s_id2, 16)
                pool.wait_ge(s_poly, 3 * GENS)
                low = Chain(pool, s_low, 3 * GENS)
                for g in range(GENS):
                    a, a2 = (v[:, g, :, :].rearrange("p k c -> p (k c)") for v in (A_, A2_))
                    low.did(nc.gpsimd.tensor_scalar(y2_a2, a2, Y2, None, ALU.mult))
                    low.then(nc.gpsimd.tensor_tensor(a, a, ident2, ALU.add))
                    low.then(nc.gpsimd.tensor_tensor(a, a, y2_a2, ALU.add))

            def scatter(l):
                y = L[l]
                pool.wait_ge(y.route, ROUTE_STEPS[l])
                pool.wait_ge(y.norm, NT)
                pool.wait_ge(s_qzero[l], 16)
                for t in range(NT):
                    for k in range(TOPK):
                        nc.gpsimd.indirect_dma_start(
                            queue[l], bass.IndirectOffsetOnAxis(pos_i[:, k, t:t + 1].bitcast(U32), 0),
                            z_all[:, t, :], None).then_inc(y.scat[t >= EARLY], 16)

            def mask_weights():
                pool.wait_ge(s_rc, 2)
                nc.gpsimd.tensor_tensor(kron.rearrange("p (b t) -> p b t", t=LANES),
                                        lane_mask.unsqueeze(1).broadcast_to([P, B, LANES]),
                                        crep[:, :].unsqueeze(2).broadcast_to([P, B, LANES]), ALU.mult).then_inc(s_kron, 1)
                pool.wait_ge(s_wc, 32 * NWCHUNK)
                for q in range(NWCHUNK):
                    nc.gpsimd.tensor_tensor(wch[q], wch[q], mch[q], ALU.mult).then_inc(s_wmul, 1)

            def gather(l):
                y = L[l]
                for s in range(2):
                    pool.wait_ge(y.ostore[s], 16 * TILES[l] // 2)
                if l == 0:
                    pool.wait_ge(y.oc, TILES[0])
                if l == 1:
                    all_scattered(pool, y)
                for t in range(NT):
                    for k in range(TOPK):
                        to = z_all[:, t, :] if k == 0 else second[:, t, :]
                        nc.gpsimd.indirect_dma_start(
                            to, None, answer[l],
                            bass.IndirectOffsetOnAxis(pos_i[:, k, t:t + 1].bitcast(U32), 0)).then_inc(y.gather[t // GROUP], 16)

            entry(0)
            low_terms()
            scatter(0)
            mask_weights()
            gather(0)
            entry(1)
            scatter(1)
            gather(1)

        @block.scalar
        def _(act):
            def entry(l):
                y, q = L[l], ENTRY_LAG[l]

                def step(st):
                    if st.has(q + 3):
                        t = st.tile(q + 3)
                        act.wait_ge(y.zt, t + 1)
                        nc.scalar.copy(znt[:, :, t * P:(t + 1) * P],
                                       ps[(6, 5)[l]][:, 0:D].rearrange("p (k j) -> p k j", k=KC)).then_inc(y.ztc, 1)
                    if l == 1 and st.has(3):
                        s, t = st.slot(3), st.tile(3)
                        act.wait_ge(s_xtr, t + 1)
                        after(act, y.cond_mm, st, 3, 2)
                        nc.scalar.copy(x_t[:, s, :, :].rearrange("p k t -> p (k t)"), ps[2][:, 0:D]).then_inc(s_xtc, 1)
                    if st.has(q):
                        s, t = st.slot(q), st.tile(q)
                        act.wait_ge(y.stat, t * ROW_STEPS[l] + (2, 1)[l])
                        after(act, y.pow, st, q, 2, POW_STEPS[l])
                        after(act, y.sq, st, q, 1)
                        if l == 0:
                            nc.scalar.activation(act_junk, c_row[:, s, :], ACT.Square, bias=neg_mean[:, s:s + 1],
                                                 accum_out=sq_sum[:, s:s + 1]).then_inc(y.sq, 1)
                        else:
                            nc.scalar.activation(act_junk, c_row[:, s, :], ACT.Square,
                                                 accum_out=sq_sum[:, s:s + 1]).then_inc(y.sq, 1)
                    if l == 1 and st.has(0):
                        s, t = st.slot(0), st.tile(0)
                        act.wait_ge(s_mt, t + 1)
                        after(act, s_rot, st, 0, 2)
                        nc.scalar.copy(m_col[:, s, :, :].rearrange("p k t -> p (k t)"), ps[0][:, 0:D]).then_inc(s_mtc, 1)
                    if l == 1 and st.has(1):
                        s, t = st.slot(1), st.tile(1)
                        act.wait_ge(s_dot, t + 1)
                        after(act, s_x1, st, 1, 2)
                        nc.scalar.activation(gate[:, s:s + 1], rot_dot[:, s:s + 1], ACT.Sigmoid,
                                             bias=abel_dot[:, t:t + 1]).then_inc(s_sig, 1)

                    g, turned = divmod(st.k - SCALE_AT, 2)
                    if l == 0 and 0 <= g < GENS:
                        act.wait_ge(s_norm, 8)
                        if turned:
                            act.wait_ge(s_gens_t, 16)
                        w = (A_, AT_)[turned][:, g, :, :].rearrange("p k c -> p (k c)")
                        nc.scalar.activation(w, w, ACT.Identity, scale=small_i[:, 3:4].bitcast(F32)).then_inc(s_scaled, 1)

                if l == 1:
                    act.wait_ge(L[0].do, NT)
                    act.wait_ge(s_dabel, NT * DABEL_STEPS)
                unrolled(NT, q + 3, step)

            def route_exp(l):
                y = L[l]
                act.wait_ge(y.route, 3)
                e2 = scratch[l][:, 2, 0:NT]
                nc.scalar.activation(e2, e2, ACT.Exp).then_inc(y.expd, 1)
                if l == 1:
                    e = scratch[l][:, 1, 0:NT * EXPERTS[1]]
                    nc.scalar.activation(e, e, ACT.Exp).then_inc(y.expd, 1)

            def ranks(l):
                y = L[l]
                act.wait_ge(y.rank, 2)
                for a, bank in ((4, 7), (5, 6)):
                    n = NT * EXPERTS[l]
                    nc.scalar.copy(scratch[l][:, a, 0:n], ps[bank][:, 0:n]).then_inc(y.ranked, 1)

            def exponentials():
                for stage in range(3):
                    dst, done = ((TR_, s_trc), (TR_, s_trc), (AT_, s_sqtc))[stage]
                    for g in range(GENS):
                        act.wait_ge(s_tr, stage * GENS + g + 1)
                        if stage == 1:
                            act.wait_ge(s_prod, GENS + g + 1)
                        nc.scalar.copy(dst[:, g, :, :].rearrange("p k c -> p (k c)"), ps[4 + g][:, :]).then_inc(done, 1)
                turns = act.value_load(small_i[0:1, 1:2], min_val=1, max_val=100)
                with act.Fori(0, turns) as i:
                    for g in range(GENS):
                        act.wait_ge(s_sqt, GENS * i + g + 1)
                        nc.scalar.copy(AT_[:, g, :, :].rearrange("p k c -> p (k c)"), ps[4 + g][:, :]).then_inc(s_sqtc, 1)

            def routed(l):
                y = L[l]

                def step(st):
                    if st.has(HID_LAG):
                        s, t = st.slot(HID_LAG), st.tile(HID_LAG)
                        if l == 0:
                            act.wait_ge(y.hb, t + 1)
                            nc.scalar.activation(q_hid[:, s, :], q_hid[:, s, :], ACT.Gelu).then_inc(y.ha, 1)
                        else:
                            act.wait_ge(y.h, t + 1)
                            after(act, y.ht, st, HID_LAG, 2)
                            nc.scalar.activation(q_hid[:, s, :], ps[2 + s][:, :], ACT.Silu).then_inc(y.ha, 1)
                    if l == 0 and st.has(HT_LAG):
                        s, t = st.slot(HT_LAG), st.tile(HT_LAG)
                        act.wait_ge(y.ht, t + 1)
                        after(act, y.o, st, HT_LAG, 2)
                        nc.scalar.copy(q_hidc[:, s, :, :].rearrange("p c t -> p (c t)"), ps[4 + s][:, :]).then_inc(y.htc, 1)
                    if l == 0 and st.has(0):
                        s, t = st.slot(0), st.tile(0)
                        act.wait_ge(y.qt, t + 1)
                        after(act, y.h, st, 0, 2)
                        nc.scalar.copy(q_col[:, s, :, :].rearrange("p k t -> p (k t)"), ps[s][:, 0:D]).then_inc(y.qtc, 1)

                if l == 0:
                    act.wait_ge(s_res, NT)
                pipeline(act, TILES[l], STORE_LAG, step)

            def dense(l, blocks, after_routed, between=None):
                y = L[l]
                if after_routed:
                    for s in range(2):
                        act.wait_ge(y.ostore[s], 16 * TILES[l] // 2)

                def one(i):
                    for c in range(2 * HC):
                        if between and c == 4:
                            between(l)
                        act.wait_ge(y.dh, 2 * HC * i + c + 1)
                        if l == 0:
                            nc.scalar.activation(hid_col[:, c, :], ps[2 + c % 4][:, :], ACT.Gelu,
                                                 bias=ab1[:, c:c + 1]).then_inc(y.da, 1)
                        else:
                            nc.scalar.activation(hid_col[:, c, :], ps[2 + c % 4][:, :], ACT.Silu).then_inc(y.da, 1)

                if len(blocks) == 1:
                    one(blocks[0])
                else:
                    with act.Fori(blocks[0], blocks[-1] + 1) as i:
                        one(i)

            entry(0)
            route_exp(0)
            ranks(0)
            exponentials()
            routed(0)
            dense(0, range(NBLK), True)
            entry(1)
            route_exp(1)
            dense(1, [0], False, ranks)
            dense(1, range(1, DENSE_BEFORE[1]), False)
            routed(1)
            dense(1, range(DENSE_BEFORE[1], NBLK), True)

        @block.vector
        def _(dve):
            V = nc.vector

            def prepare():
                V.memset(zeros, 0.0).then_inc(s_zero, 1)
                V.memset(logits[:, :, :], -1e30).then_inc(s_prep, 1)
                V.memset(scan_on[:, :, :], 1.0).then_inc(s_prep, 1)
                dve.wait_ge(s_prep, 2)
                V.memset(scan_on[:, :, 0:1], 0.0).then_inc(s_prep, 1)
                dve.wait_ge(s_cond, 32)
                V.tensor_scalar(c2[:, :], crep[:, :], 2.0, None, ALU.mult).then_inc(s_prep, 1)
                dve.wait_ge(s_prep, 4)
                for b in range(B):
                    V.tensor_scalar(bsw[:, b, :], bsT, c2[:, b:b + 1], None, ALU.mult).then_inc(s_bsw, 1)
                for b in range(B):
                    dve.wait_ge(s_weffmm, b + 1)
                    V.tensor_tensor(weff[:, b, :, :].rearrange("p k o -> p (k o)"), ps[b % 4][:, :], wbaseT,
                                    ALU.add).then_inc(s_weff, 1)
                    if b in (B // 2 - 1, B - 2):
                        norms(b // (B // 2))
                dve.wait_ge(s_rows, 16)

            def entry(l):
                y, q = L[l], ENTRY_LAG[l]
                stat = Chain(dve, y.stat, ROW_STEPS[l])
                E = EXPERTS[l]

                def step(st):
                    if st.has(q + 2):
                        s, t = st.slot(q + 2), st.tile(q + 2)
                        dve.wait_ge(y.pow, t * POW_STEPS[l] + 2)
                        dve.wait_ge(y.stat, (t + 1) * ROW_STEPS[l])
                        if l == 0:
                            V.scalar_tensor_tensor(z_all[:, t, :], g_row[:, s, :], rstd[:, s:s + 1], r("ln_b"),
                                                   ALU.mult, ALU.add).then_inc(y.norm, 1)
                        else:
                            V.tensor_scalar(z_all[:, t, :], c_row[:, s, :], rstd[:, s:s + 1], None, ALU.mult
                                            ).then_inc(y.norm, 1)
                    if st.has(q + 4):
                        s, t = st.slot(q + 4), st.tile(q + 4)
                        dve.wait_ge(y.lg, t + 1)
                        if l == 0:
                            V.tensor_tensor(logits[:, t, 0:E], ps[7][:, 0:E], r("gate_b")[:, 0:E], ALU.add).then_inc(y.lgc, 1)
                        else:
                            dve.wait_ge(y.pow, (t + 1) * POW_STEPS[1])
                            V.tensor_scalar(logits[:, t, 0:E], ps[6][:, 0:E], inv[:, t:t + 1], None, ALU.mult).then_inc(y.lgc, 1)
                    if l == 1 and st.has(2):
                        s, t = st.slot(2), st.tile(2)
                        dve.wait_ge(s_sig, t + 1)
                        dve.wait_ge(s_less, t + 1)
                        V.scalar_tensor_tensor(res[:, t, :], less[:, s, :], gate[:, s:s + 1], res[:, t, :],
                                               ALU.mult, ALU.add).then_inc(s_x1, 1)
                    if st.has(q):
                        s, t = st.slot(q), st.tile(q)
                        stat.start(t)
                        dve.wait_ge(y.cond_mm, t + 1)
                        after(dve, y.sq, st, q, 2)
                        after(dve, y.norm, st, q, 2)
                        if l == 0:
                            after(dve, s_res, st, q, 2)
                            stat.then(V.scalar_tensor_tensor(c_row[:, s, :], ps[t % 4][:, 0:D], 1.0, r("b_base"),
                                                             ALU.mult, ALU.add, accum_out=row_sum[:, s:s + 1]))
                            stat.then(V.tensor_scalar(neg_mean[:, s:s + 1], row_sum[:, s:s + 1], -1.0 / D, None, ALU.mult))
                            stat.did(V.scalar_tensor_tensor(g_row[:, s, :], c_row[:, s, :], neg_mean[:, s:s + 1], r("ln_g"),
                                                            ALU.add, ALU.mult))
                        else:
                            stat.did(V.tensor_tensor(c_row[:, s, :], ps[3 + s][:, 0:D], r("bias1"), ALU.add))
                    if l == 0 and st.k == SCALE_AT - 2:
                        scaling()
                    if l == 1 and st.has(1):
                        s, t = st.slot(1), st.tile(1)
                        dve.wait_ge(s_rot, t + 1)
                        after(dve, s_sig, st, 1, 2)
                        after(dve, s_dot, st, 1, 1)
                        V.scalar_tensor_tensor(dve_junk, ps[(1, 7)[s]][:, 0:D], 1.0, r("gate_nonabel"),
                                               ALU.mult, ALU.mult, accum_out=rot_dot[:, s:s + 1]).then_inc(s_dot, 1)
                        after(dve, s_x1, st, 1, 2)
                        V.tensor_tensor(less[:, s, :], ps[(1, 7)[s]][:, 0:D], abel[:, t, :], ALU.subtract).then_inc(s_less, 1)

                unrolled(NT, q + 4, step)

            def route(l):
                y, E = L[l], EXPERTS[l]
                ch = Chain(dve, y.route, ROUTE_STEPS[l])
                ch.start(0)

                def te(v):
                    return v.rearrange("p (t e) -> p t e", e=E)

                def et(v):
                    return v.rearrange("p (e t) -> p e t", t=NT)

                both, tot = (scratch[l][:, a, 0:NT * E] for a in range(2))
                first, other = (onehot[:, k, 0:NT * E] for k in range(TOPK))
                cum = scratch[l][:, 3, 0:NT * E]
                e2, den, w_a, w_b = (scratch[l][:, 2, a * NT:(a + 1) * NT] for a in range(4))
                dve.wait_ge(y.lgc, NT)
                wide = 8 if l == 0 else 16
                for t in range(NT):
                    i = V.max(top[:, t, :], logits[:, t, 0:wide])
                ch.then(i)
                for t in range(NT):
                    i = V.max_index(top_i[:, t, :], top[:, t, :], logits[:, t, 0:wide])
                ch.then(i)
                if l == 1:
                    V.tensor_tensor(te(tot), logits[:, :, 0:E], top[:, :, 0:1].broadcast_to([P, NT, E]), ALU.subtract)
                ch.then(V.tensor_tensor(e2.unsqueeze(2), top[:, :, 1:2], top[:, :, 0:1], ALU.subtract))
                ch.then(V.tensor_copy(picked[:, :, :], top_i[:, :, 0:TOPK]))
                for k, v in enumerate((first, other)):
                    ch.did(V.tensor_tensor(te(v), iota_e[:, 0:E].unsqueeze(1).broadcast_to([P, NT, E]),
                                           picked[:, :, k:k + 1].broadcast_to([P, NT, E]), ALU.is_equal))
                ch.wait()
                ch.then(V.tensor_tensor(both, first, other, ALU.add))
                assert ch.k == BOTH_STEP
                return ch, te, et, both, tot, first, other, cum, e2, den, w_a, w_b

            def queues(l, begun):
                y, E, NQ = L[l], EXPERTS[l], TILES[l]
                ch, te, et, both, tot, first, other, cum, e2, den, w_a, w_b = begun
                dve.wait_ge(y.expd, 1 + l)
                if l == 0:
                    ch.then(V.tensor_scalar(den, e2, 1.0, None, ALU.add))
                    ch.then(V.reciprocal(gate_w8[:, 0, :], den))
                    ch.then(V.tensor_tensor(gate_w8[:, 1, :], e2, gate_w8[:, 0, :], ALU.mult))
                else:
                    ch.then(V.tensor_reduce(den, te(tot), AX.X, ALU.add))
                    ch.then(V.reciprocal(w_a, den))
                    ch.then(V.tensor_tensor(w_b, e2, w_a, ALU.mult))
                    ch.then(V.tensor_tensor(den, w_a, w_b, ALU.add))
                    ch.then(V.tensor_scalar(den, den, 1e-9, None, ALU.add))
                    ch.then(V.reciprocal(e2, den))
                    ch.then(V.tensor_tensor(gate_w8[:, 0, :], w_a, e2, ALU.mult))
                    ch.then(V.tensor_tensor(gate_w8[:, 1, :], w_b, e2, ALU.mult))
                dve.wait_ge(y.ranked, 2)
                in_tile, before = (scratch[l][:, a, 0:NT * E] for a in (4, 5))
                ch.then(V.tensor_copy(et(tot), in_tile.rearrange("p (t e) -> p e t", e=E)))
                ch.then(V.tensor_tensor_scan(cum, scan_on[:, 0:E, :].rearrange("p e t -> p (e t)"), tot, 0.0,
                                             ALU.mult, ALU.add))
                count = et(cum)[:, :, NT - 1:NT].rearrange("p e a -> p (e a)")
                tiles_i, tiles, ends, start = (small_e[:, a, 0:E] for a in range(4))
                tiles_i = tiles_i.bitcast(I32)
                ch.then(V.tensor_scalar(tiles_i, count, float(P - 1), None, ALU.add))
                ch.then(V.tensor_scalar(tiles_i, tiles_i, 7, None, ALU.logical_shift_right))
                ch.then(V.tensor_copy(tiles, tiles_i))
                ch.then(V.tensor_tensor_scan(ends, scan_on[:, 0, 1:2].broadcast_to([P, E]), tiles, 0.0, ALU.mult, ALU.add))
                ch.then(V.tensor_tensor(start, ends, tiles, ALU.subtract))
                ch.then(V.tensor_scalar(start, start, float(P), None, ALU.mult))
                ch.then(V.tensor_tensor(cum, cum, tot, ALU.subtract))
                ch.then(V.tensor_tensor(et(cum), et(cum), start.unsqueeze(2).broadcast_to([P, E, NT]), ALU.add))
                ch.then(V.tensor_tensor(te(tot), te(before), cum.rearrange("p (e t) -> p t e", t=NT), ALU.add))
                for k, v in enumerate((first, other)):
                    ch.then(V.tensor_tensor(te(v), te(v), te(tot), ALU.mult))
                    ch.then(V.tensor_reduce(cum[:, k * NT:(k + 1) * NT], te(v), AX.X, ALU.add))
                    ch.then(V.tensor_copy(pos_i[:, k, :], cum[:, k * NT:(k + 1) * NT]))
                at_or_before = scratch[l][:, 0:3, :].rearrange("p a n -> p (a n)")[:, 0:NQ * E].rearrange("p (q e) -> p q e", e=E)
                ch.then(V.tensor_tensor(at_or_before, iota_t[:, 0:NQ].unsqueeze(2).broadcast_to([P, NQ, E]),
                                        ends.unsqueeze(1).broadcast_to([P, NQ, E]), ALU.is_ge))
                which = scratch[l][:, 3, 64:64 + NQ]
                ch.then(V.tensor_reduce(which, at_or_before, AX.X, ALU.add))
                ch.then(V.tensor_scalar(which, which, float(E - 1), None, ALU.min))
                ch.then(V.tensor_scalar(table[:, 0, 0:NQ], which, float(UNIT), float(EXPERT_SLOT[l] * UNIT), ALU.mult, ALU.add))
                ch.then(V.tensor_scalar(table[:, 1, 0:NQ], which, float(D), None, ALU.mult))
                assert ch.k == ROUTE_STEPS[l], ch.k

            def norms(half):
                dve.wait_ge(s_gens, 16)
                n = GENS // 2
                V.tensor_reduce(small[:, 4 + half * n * KC:4 + (half + 1) * n * KC],
                                A_[:, half * n:(half + 1) * n].rearrange("p g k c -> p (g k) c"), AX.X, ALU.add,
                                apply_absolute_value=True).then_inc(s_norm, 1)

            def largest_norm():
                dve.wait_ge(s_norm, 2)
                V.tensor_reduce(small[:, 0:1], small[:, 4:4 + GENS * KC], AX.X, ALU.max).then_inc(s_norm, 1)

            def scaling():
                dve.wait_ge(s_allmax, 1)
                n = Chain(dve, s_norm, 16)
                n.start(0)
                n.k = 3
                n.then(V.tensor_scalar(small_i[:, 0:1], small[:, 1:2].bitcast(I32), 23, None, ALU.logical_shift_right))
                n.then(V.tensor_scalar(small_i[:, 1:2], small_i[:, 0:1], -126.0, 1.0, ALU.add, ALU.max))
                n.then(V.tensor_scalar(small_i[:, 1:2], small_i[:, 1:2], 100.0, None, ALU.min))
                n.then(V.tensor_scalar(small_i[:, 2:3], small_i[:, 1:2], -1.0, 127.0, ALU.mult, ALU.add))
                n.then(V.tensor_scalar(small_i[:, 3:4], small_i[:, 2:3], 23, None, ALU.logical_shift_left))

            def exponentials(routing):
                steps = Chain(dve, s_poly, 64)
                steps.start(0)
                dve.wait_ge(s_scaled, 2 * GENS)

                def m(v, g):
                    return v[:, g, :, :].rearrange("p k c -> p (k c)")

                def stt(o, a, c, b):
                    return V.scalar_tensor_tensor(o, a, c, b, ALU.mult, ALU.add)

                for g in range(GENS):
                    dve.wait_ge(s_prod, g + 1)
                    steps.then(V.tensor_copy(m(A2_, g), ps[g][:, :]))
                for g in range(GENS):
                    steps.did(stt(m(PU_, g), m(A_, g), X1 / X2, m(A2_, g)))
                dve.wait_ge(s_id2, 16)
                for g in range(GENS):
                    steps.did(stt(m(V_, g), m(A_, g), X5 / X6, m(A2_, g)))
                steps.wait()
                for g in range(GENS):
                    steps.did(stt(m(V_, g), ident2, X4 / X6, m(V_, g)))
                steps.wait()
                for g in range(GENS):
                    dve.wait_ge(s_prod, GENS + g + 1)
                    steps.did(stt(m(PU_, g), m(A2_, g), X3 / X2, ps[g][:, :]))
                    steps.did(stt(m(V_, g), ps[g][:, :], X7 * X2 / X6, m(V_, g)))
                queues(0, routing)
                for g in range(GENS):
                    dve.wait_ge(s_prod, 2 * GENS + g + 1)
                    dve.wait_ge(s_low, 3 * (g + 1))
                    steps.then(stt(m(A_, g), ps[g][:, :], X2 * X6, m(A_, g)))
                turns = dve.value_load(small_i[0:1, 1:2], min_val=1, max_val=100)
                with dve.Fori(0, turns) as i:
                    for g in range(GENS):
                        dve.wait_ge(s_sqp, GENS * i + g + 1)
                        V.tensor_copy(m(A_, g), ps[g][:, :]).then_inc(s_sqc, 1)
                for j in range(2):
                    dve.wait_ge(s_rp, j + 1)
                    V.tensor_copy(m(PU_, j), ps[6 + j][:, :]).then_inc(s_rc, 1)

            def masked_weights():
                for q in range(NWCHUNK):
                    for a in range(2):
                        dve.wait_ge(s_wmm, 2 * q + a + 1)
                        V.tensor_copy(mch[q][:, a * 512:(a + 1) * 512], ps[2 * q + a][:, :]).then_inc(s_wev, 1)

            def routed(l):
                y = L[l]
                if l == 0:
                    dve.wait_ge(s_eb, 32)

                def step(st):
                    if l == 0 and st.has(HID_LAG):
                        s, t = st.slot(HID_LAG), st.tile(HID_LAG)
                        at = dve.value_load(table[0:1, 1, bass.ds(t, 1)], min_val=0, max_val=(EXPERTS[0] - 1) * D)
                        dve.wait_ge(y.h, t + 1)
                        after(dve, y.ht, st, HID_LAG, 2)
                        V.tensor_tensor(q_hid[:, s, :], ps[2 + s][:, :], eb1_sb[:, bass.ds(at * 2, HID)], ALU.add).then_inc(y.hb, 1)
                    if l == 1 and st.has(HT_LAG):
                        s, t = st.slot(HT_LAG), st.tile(HT_LAG)
                        dve.wait_ge(y.ht, t + 1)
                        after(dve, y.o, st, HT_LAG, 2)
                        V.tensor_copy(q_hidc[:, s, :, :].rearrange("p c t -> p (c t)"), ps[4 + s][:, :]).then_inc(y.htc, 1)
                    if l == 1 and st.has(0):
                        s, t = st.slot(0), st.tile(0)
                        dve.wait_ge(y.qt, t + 1)
                        after(dve, y.h, st, 0, 2)
                        V.tensor_copy(q_col[:, s, :, :].rearrange("p k t -> p (k t)"), ps[s][:, 0:D]).then_inc(y.qtc, 1)
                    if st.has(OUT_LAG):
                        s, t = st.slot(OUT_LAG), st.tile(OUT_LAG)
                        if l == 0:
                            at = dve.value_load(table[0:1, 1, bass.ds(t, 1)], min_val=0, max_val=(EXPERTS[0] - 1) * D)
                        dve.wait_ge(y.o, t + 1)
                        if st.i is not None or st.k - OUT_LAG >= 2:
                            dve.wait_ge(y.ostore[s], 16 * st.turn(OUT_LAG))
                        if l == 0:
                            V.tensor_tensor(q_out[:, s, :], ps[6 + s][:, 0:D], eb2_sb[:, bass.ds(at, D)], ALU.add).then_inc(y.oc, 1)
                        else:
                            V.tensor_copy(q_out[:, s, :], ps[6 + s][:, 0:D]).then_inc(y.oc, 1)

                pipeline(dve, TILES[l], STORE_LAG, step)

            def rotation():
                dve.wait_ge(s_rp, 3)
                V.tensor_copy(rot[:, :, :].rearrange("p k c -> p (k c)"), ps[7][:, :]).then_inc(s_rc, 1)

            def scale_unit(u):
                dve.wait_ge(s_unit1[u], 16)
                for k in range(KC):
                    w = units[:, u, k * HID:(k + 1) * HID]
                    V.tensor_scalar(w, w, rms[:, u, k:k + 1], None, ALU.mult).then_inc(s_rms, 1)

            def add_dense(t):
                dve.wait_ge(L[1].do, t + 1)
                V.tensor_tensor(res[:, t, :], ps[6 + t % 2][:, 0:D], res[:, t, :], ALU.add).then_inc(L[1].doc, 1)

            def mix(t):
                dve.wait_ge(L[0].gather[t // GROUP], 16 * TOPK * GROUP)
                V.tensor_scalar(z_all[:, t, :], z_all[:, t, :], gate_w8[:, 0, t:t + 1], None, ALU.mult).then_inc(s_mixa, 1)
                dve.wait_ge(s_mixa, t + 1)
                V.scalar_tensor_tensor(z_all[:, t, :], second[:, t, :], gate_w8[:, 1, t:t + 1], z_all[:, t, :],
                                       ALU.mult, ALU.add).then_inc(s_mix, 1)

            def dense(l, blocks, scaled):
                y = L[l]
                if blocks[0] == 0:
                    dve.sem_inc(y.doc, 1)
                    dabel = Chain(dve, s_dabel, DABEL_STEPS)
                    if l == 0:
                        dve.wait_ge(s_res, NT)
                for i in blocks:
                    for u in scaled[i - blocks[0]]:
                        scale_unit(u)
                    for t in range(4 * i, 4 * i + 4):
                        if l == 1:
                            add_dense(t)
                            continue
                        dve.wait_ge(y.do, t + 1)
                        V.tensor_tensor(abel[:, t, :], ps[6 + t % 2][:, 0:D], r("ab2"), ALU.add).then_inc(y.doc, 1)
                        dve.wait_ge(y.doc, t + 2)
                        dabel.start(t)
                        dabel.then(V.scalar_tensor_tensor(dense_junk, abel[:, t, :], 1.0, r("gate_abel"),
                                                          ALU.mult, ALU.mult, accum_out=abel_dot[:, t:t + 1]))
                        dabel.did(V.tensor_scalar(abel_dot[:, t:t + 1], abel_dot[:, t:t + 1], r("gate_c")[:, 0:1], None, ALU.add))
                        dabel.did(V.tensor_tensor(res[:, t, :], abel[:, t, :], res[:, t, :], ALU.add))
                        if i >= NBLK // 2:
                            for m in range(2 * (t - NT // 2), 2 * (t - NT // 2) + 2):
                                mix(m)

            def final(tiles):
                fin = Chain(dve, s_fin, FINAL_STEPS)
                for t in tiles:
                    fin.start(t)
                    dve.wait_ge(L[1].gather[t // GROUP], 16 * TOPK * GROUP)
                    dve.wait_ge(L[1].doc, t + 2)
                    fin.then(V.scalar_tensor_tensor(res[:, t, :], z_all[:, t, :], gate_w8[:, 0, t:t + 1],
                                                    res[:, t, :], ALU.mult, ALU.add))
                    fin.did(V.scalar_tensor_tensor(res[:, t, :], second[:, t, :], gate_w8[:, 1, t:t + 1],
                                                   res[:, t, :], ALU.mult, ALU.add))

            prepare()
            largest_norm()
            entry(0)
            exponentials(route(0))
            routed(0)
            rotation()
            masked_weights()
            dense(0, range(NBLK), [(2 * i, 2 * i + 1) for i in range(NBLK)])
            entry(1)
            queues(1, route(1))
            dense(1, range(DENSE_BEFORE[1]), [(8, 9, 10, 11), (12, 13, 14, 15)])
            routed(1)
            for i in range(DENSE_BEFORE[1], NBLK - 1):
                dense(1, [i], [()])
            final(range(0, NT - GROUP))
            for t in range(NT - GROUP, NT):
                add_dense(t)
                final([t])

        @block.tensor
        def _(pe):
            mm = nc.tensor.matmul

            def transpose(to, block):
                return nc.tensor.transpose(to, block, ident)

            def keep_awake(n):
                for _ in range(n):
                    mm(ps[4][:, 0:D], zeros[:, 0:P], zeros, start=True, stop=True)

            def layer0_weights():
                pe.wait_ge(s_zero, 2)
                keep_awake(WARM_UP)
                pe.wait_ge(s_cond, 32)
                for b in range(B):
                    pe.wait_ge(s_bsw, b + 1)
                    if b >= 4:
                        pe.wait_ge(s_weff, b - 3)
                    for k in range(KC):
                        i = mm(ps[b % 4][:, k * D:(k + 1) * D], asT[:, k * P:(k + 1) * P], bsw[:, b, :], start=True, stop=True)
                    i.then_inc(s_weffmm, 1)

            def transpose2(bank, rows2, done):
                for k in range(KC):
                    i = transpose(bank[:, k * P:(k + 1) * P], rows2[:, k * P:(k + 1) * P])
                i.then_inc(done, 1)

            def entry(l):
                y, q = L[l], ENTRY_LAG[l]
                E = EXPERTS[l]

                def step(st):
                    if st.has(q + 4):
                        t = st.tile(q + 4)
                        pe.wait_ge(y.ztc, t + 1)
                        after(pe, y.lgc, st, q + 4, 1)
                        for k in range(KC):
                            i = mm(ps[(7, 6)[l]][:, 0:E], znt[:, k, t * P:(t + 1) * P], router[l][:, k, :],
                                   start=(k == 0), stop=(k == KC - 1))
                        i.then_inc(y.lg, 1)
                    if st.has(q + 3):
                        t = st.tile(q + 3)
                        pe.wait_ge(y.norm, t + 1)
                        after(pe, y.ztc, st, q + 3, 1)
                        transpose2(ps[(6, 5)[l]], z_all[:, t, :], y.zt)
                    if st.has(q):
                        s, t = st.slot(q), st.tile(q)
                        if l == 0:
                            pe.wait_ge(s_xt[t // GROUP], 16)
                            pe.wait_ge(s_weff, B)
                            after(pe, y.stat, st, q, 4, ROW_STEPS[l])
                            bank = ps[t % 4]
                        else:
                            pe.wait_ge(s_xtc, t + 1)
                            after(pe, y.stat, st, q, 2, ROW_STEPS[l])
                            bank = ps[3 + s]
                        for k in range(KC):
                            lhs = x_all_t[:, t, k, :] if l == 0 else x_t[:, s, k, :]
                            i = mm(bank[:, 0:D], lhs, cond_w[l][:, t // PER_BATCH, k, :], start=(k == 0), stop=(k == KC - 1))
                        i.then_inc(y.cond_mm, 1)
                    if l == 0:
                        keep_awake(1)
                    if l == 1 and st.has(3):
                        t = st.tile(3)
                        pe.wait_ge(s_x1, t + 1)
                        after(pe, s_xtc, st, 3, 1)
                        transpose2(ps[2], res[:, t, :], s_xtr)
                    if l == 1 and st.has(1):
                        s, t = st.slot(1), st.tile(1)
                        pe.wait_ge(s_mtc, t + 1)
                        after(pe, s_less, st, 1, 2)
                        for k in range(KC):
                            i = mm(ps[(1, 7)[s]][:, 0:D], m_col[:, s, k, :], rot[:, k, :], start=(k == 0), stop=(k == KC - 1))
                        i.then_inc(s_rot, 1)
                    if l == 1 and st.has(0):
                        t = st.tile(0)
                        pe.wait_ge(s_mix, t + 1)
                        after(pe, s_mtc, st, 0, 1)
                        transpose2(ps[0], z_all[:, t, :], s_mt)

                unrolled(NT, q + 4, step)

            def rank(l):
                y, n = L[l], NT * EXPERTS[l]
                pe.wait_ge(y.route, BOTH_STEP)
                pe.wait_ge(y.lgc, NT)
                both = scratch[l][:, 0, 0:n]
                mm(ps[6][:, 0:n], upper, both, start=True, stop=True).then_inc(y.rank, 1)
                mm(ps[7][:, 0:n], ones, both, start=True, stop=True).then_inc(y.rank, 1)

            def product(bank, xt, y):
                for mc in range(KC):
                    for k in range(KC):
                        i = mm(bank[:, mc * D:(mc + 1) * D], xt[:, k, mc * P:(mc + 1) * P], y[:, k, :],
                               start=(k == 0), stop=(k == KC - 1))
                return i

            def turned(bank, x):
                for k in range(KC):
                    for mc in range(KC):
                        i = transpose(bank[:, k * D + mc * P:k * D + (mc + 1) * P], x[:, mc, k * P:(k + 1) * P])
                return i

            def exponentials():
                for g in range(GENS):
                    pe.wait_ge(s_scaled, 2 * g + 2)
                    product(ps[g], AT_[:, g], A_[:, g]).then_inc(s_prod, 1)
                rank(0)
                for g in range(GENS):
                    pe.wait_ge(s_poly, g + 1)
                    if g == 2:
                        pe.wait_ge(L[0].ranked, 2)
                    turned(ps[4 + g], A2_[:, g]).then_inc(s_tr, 1)
                for g in range(GENS):
                    pe.wait_ge(s_poly, GENS + g + 1)
                    pe.wait_ge(s_trc, g + 1)
                    product(ps[g], TR_[:, g], PU_[:, g]).then_inc(s_prod, 1)
                for g in range(GENS):
                    pe.wait_ge(s_poly, 4 * GENS + 2 * g + 1)
                    turned(ps[4 + g], PU_[:, g]).then_inc(s_tr, 1)
                for g in range(GENS):
                    pe.wait_ge(s_poly, 4 * GENS + 2 * g + 2)
                    pe.wait_ge(s_trc, GENS + g + 1)
                    product(ps[g], TR_[:, g], V_[:, g]).then_inc(s_prod, 1)
                for g in range(GENS):
                    pe.wait_ge(s_poly, 6 * GENS + g + 1)
                    turned(ps[4 + g], A_[:, g]).then_inc(s_tr, 1)
                turns = pe.value_load(small_i[0:1, 1:2], min_val=1, max_val=100)
                with pe.Fori(0, turns) as i:
                    for g in range(GENS):
                        pe.wait_ge(s_sqtc, GENS * i + g + 1)
                        product(ps[g], AT_[:, g], A_[:, g]).then_inc(s_sqp, 1)
                    for g in range(GENS):
                        pe.wait_ge(s_sqc, GENS * i + g + 1)
                        turned(ps[4 + g], A_[:, g]).then_inc(s_sqt, 1)
                pe.wait_ge(s_sqtc, GENS * turns + GENS)
                product(ps[6], A_[:, 1], AT_[:, 0]).then_inc(s_rp, 1)
                product(ps[7], AT_[:, 2], A_[:, 3]).then_inc(s_rp, 1)

            def masked_weights():
                pe.wait_ge(s_kron, 1)
                pe.wait_ge(L[0].oc, TILES[0])
                product(ps[7], PU_[:, 0], PU_[:, 1]).then_inc(s_rp, 1)
                for q in range(NWCHUNK):
                    pe.wait_ge(s_wmul, q + 1)
                    for a in range(2):
                        if q == NWCHUNK - 1 and a == 1:
                            pe.wait_ge(s_rc, 3)
                        mm(ps[2 * q + a][:, :], kron, wch[q][:, a * 512:(a + 1) * 512], start=True, stop=True
                           ).then_inc(s_wmm, 1)
                pe.wait_ge(s_wev, 2 * NWCHUNK)

            def routed(l):
                y = L[l]
                top_at = (EXPERT_SLOT[l] + EXPERTS[l] - 1) * UNIT

                def unit_of(t):
                    return pe.value_load(table[0:1, 0, bass.ds(t, 1)], min_val=EXPERT_SLOT[l] * UNIT, max_val=top_at)

                def step(st):
                    if st.has(HID_LAG):
                        s, t = st.slot(HID_LAG), st.tile(HID_LAG)
                        at = unit_of(t)
                        pe.wait_ge(y.qtc, t + 1)
                        after(pe, y.hb if l == 0 else y.ha, st, HID_LAG, 2)
                        for k in range(KC):
                            i = mm(ps[2 + s][:, :], q_col[:, s, k, :], flat[:, bass.ds(at + k * HID, HID)],
                                   start=(k == 0), stop=(k == KC - 1))
                        i.then_inc(y.h, 1)
                    if st.has(HT_LAG):
                        s, t = st.slot(HT_LAG), st.tile(HT_LAG)
                        pe.wait_ge(y.ha, t + 1)
                        after(pe, y.htc, st, HT_LAG, 2)
                        for c in range(HC):
                            i = transpose(ps[4 + s][:, c * P:(c + 1) * P], q_hid[:, s, c * P:(c + 1) * P])
                        i.then_inc(y.ht, 1)
                    if st.has(0):
                        s, t = st.slot(0), st.tile(0)
                        pe.wait_ge(y.qload[s], 16 * (st.turn(0) + 1))
                        after(pe, y.qtc, st, 0, 2)
                        transpose2(ps[s], q_row[:, s, :], y.qt)
                    if st.has(OUT_LAG):
                        s, t = st.slot(OUT_LAG), st.tile(OUT_LAG)
                        at = unit_of(t)
                        if l == 0 and st.i is None and t == 0:
                            pe.wait_ge(s_rc, 2)
                        pe.wait_ge(y.htc, t + 1)
                        after(pe, y.oc, st, OUT_LAG, 2)
                        for c in range(HC):
                            i = mm(ps[6 + s][:, 0:D], q_hidc[:, s, c, :], flat[:, bass.ds(at + W2_AT + c * D, D)],
                                   start=(c == 0), stop=(c == HC - 1))
                        i.then_inc(y.o, 1)

                if l == 0:
                    pe.wait_ge(s_units0, 128)
                else:
                    pe.wait_ge(s_rms, SLOTS * KC)
                pipeline(pe, TILES[l], STORE_LAG, step)
                pe.wait_ge(y.oc, TILES[l])

            def dense(l, blocks, between=None):
                y = L[l]
                if l == 1:
                    pe.wait_ge(s_rms, 2 * KC)
                pe.wait_ge(y.ztc, NT)

                def one(i):
                    for c in range(2 * HC):
                        if between and c == 4:
                            between(l)
                        u = DENSE_SLOT[l] + c // HC
                        if c >= 4:
                            pe.wait_ge(y.da, 2 * HC * i + c - 3)
                        for k in range(KC):
                            at = k * HID + (c % HC) * P
                            m = mm(ps[2 + c % 4][:, :], units[:, u, at:at + P], znt[:, k, bass.ds(i * BLK, BLK)],
                                   start=(k == 0), stop=(k == KC - 1))
                        m.then_inc(y.dh, 1)
                    pe.wait_ge(y.ranked, 2)
                    for j in range(4):
                        pe.wait_ge(y.doc, 1 + 4 * i + max(j - 1, 0))
                        for c in range(2 * HC):
                            u = DENSE_SLOT[l] + c // HC
                            if j == 0:
                                pe.wait_ge(y.da, 2 * HC * i + c + 1)
                            at = W2_AT + (c % HC) * D
                            m = mm(ps[6 + j % 2][:, 0:D], hid_col[:, c, j * P:(j + 1) * P], units[:, u, at:at + D],
                                   start=(c == 0), stop=(c == 2 * HC - 1))
                        m.then_inc(y.do, 1)

                if len(blocks) == 1:
                    one(blocks[0])
                else:
                    with pe.Fori(blocks[0], blocks[-1] + 1) as i:
                        one(i)
                pe.wait_ge(y.doc, 1 + 4 * (blocks[-1] + 1))

            layer0_weights()
            pe.wait_ge(s_weff, B)
            pe.wait_ge(s_small, 32)
            entry(0)
            pe.wait_ge(L[0].lgc, NT)
            exponentials()
            routed(0)
            masked_weights()
            dense(0, range(NBLK))
            pe.wait_ge(s_wbot, 16 * B)
            entry(1)
            dense(1, [0], rank)
            dense(1, range(1, DENSE_BEFORE[1]))
            routed(1)
            dense(1, range(DENSE_BEFORE[1], NBLK))


def constants():
    parts = {"ident": np.eye(P), "upper": np.triu(np.ones((P, P)), 1), "ones": 1.0,
             "lanes": np.arange(P)[:, None] % LANES == np.arange(LANES)[None, :],
             "iota_e": np.arange(16), "iota_t": np.arange(max(TILES))}
    c = np.zeros((P, NCONSTS), np.float32)
    for name, v in parts.items():
        at, n = CONSTS[name]
        c[:, at:at + n] = v
    identity2 = np.zeros((P, KC, D), np.float32)
    for k in range(KC):
        identity2[:, k, k * P:(k + 1) * P] = np.eye(P)
    return c, identity2.reshape(P, KC * D)


def kernel(**inputs):
    import concourse.bacc as bacc
    from concourse.bass_utils import run_bass_kernel_spmd

    a = {k: np.asarray(v) for k, v in inputs.items()}

    def chunks(m):
        return m.reshape(-1, P, m.shape[1]).transpose(1, 0, 2).reshape(P, -1)

    def unit(w1, w2):
        return np.concatenate([chunks(w1), chunks(w2)], axis=1)

    x = a["x"]
    aw1, aw2 = a["L0_ffn_aw1"], a["L0_ffn_aw2"]
    units0 = [unit(aw1[:, h * HID:(h + 1) * HID], aw2[h * HID:(h + 1) * HID]) for h in range(2)]
    units0 += [unit(a["L0_ffn_ew1"][e], a["L0_ffn_ew2"][e]) for e in range(EXPERTS[0])]
    units1 = [unit(a["L1_ffn_w1_s"][e], a["L1_ffn_w2_s"][e]) for e in range(2)]
    units1 += [unit(a["L1_ffn_w1"][e], a["L1_ffn_w2"][e]) for e in range(EXPERTS[1])]
    rms = np.concatenate([a["L1_ffn_rms_w_s"], a["L1_ffn_rms_w"]])
    parts = {"b_base": a["L0_cond_b_base"], "ln_g": a["L0_ffn_ln_g"], "ln_b": a["L0_ffn_ln_b"], "ab2": a["L0_ffn_ab2"], "gate_abel": a["L0_ffn_gc_w"][0:D, 0],
             "gate_nonabel": a["L0_ffn_gc_w"][D:2 * D, 0], "bias1": a["L1_cond_bias"], "gate_b": a["L0_ffn_gate_b"],
             "gate_c": a["L0_ffn_gc_b"]}
    rows = np.zeros((1, NROWS), np.float32)
    for name, v in parts.items():
        rows[0, ROWS[name][0]:ROWS[name][0] + v.size] = v
    parts = {"ab1": chunks(a["L0_ffn_ab1"][:, None]), "gate_w": chunks(a["L0_ffn_gate_w"]),
             "router_w": chunks(a["L1_ffn_router_w"]), "rms": rms.reshape(SLOTS, KC, P).transpose(2, 0, 1).reshape(P, -1)}
    cols = np.zeros((P, NCOLS), np.float32)
    for name, v in parts.items():
        cols[:, COLS[name][0]:COLS[name][0] + v.shape[1]] = v
    gens = a["L0_ffn_gens"]
    con, identity2 = constants()
    arrays = {
        "x_rows": x.reshape(T, D),
        "x_cols": x.reshape(NT, P, KC, P).transpose(0, 3, 2, 1).reshape(NT, P, D),
        "cond": np.repeat(a["cond_8"].T, LANES, axis=0),
        "lora": np.concatenate([a["L0_cond_As"].reshape(P, D), a["L0_cond_Bs"].transpose(0, 2, 1).reshape(P, D),
                                chunks(a["L0_cond_W_base"].T)], axis=1),
        "rows": np.repeat(rows, P, axis=0),
        "cols": cols,
        "units0": np.stack(units0),
        "units1": np.stack(units1),
        "eb1": np.repeat(a["L0_ffn_eb1"].reshape(1, -1), P, axis=0),
        "eb2": np.repeat(a["L0_ffn_eb2"].reshape(1, -1), P, axis=0),
        "gens": gens.reshape(GENS, KC, P, D).transpose(2, 0, 1, 3),
        "gens_t": gens.transpose(0, 2, 1).reshape(GENS, KC, P, D).transpose(2, 0, 1, 3),
        "w1c": a["L1_cond_weight"].transpose(0, 2, 1).reshape(B, TBLOCKS, LANES, D).transpose(0, 2, 1, 3).reshape(P, -1),
        "mask1c": np.tile(a["L1_cond_mask"].T.reshape(TBLOCKS, LANES, D).transpose(1, 0, 2).reshape(LANES, -1), (B, 1)),
        "consts": con,
        "identity2": identity2,
    }
    nc = bacc.Bacc("TRN2", target_bir_lowering=False, num_devices=1)
    feeds, args = {}, []
    for name, v in arrays.items():
        feeds[f"in_{name}"] = np.ascontiguousarray(v)
        args.append(nc.dram_tensor(f"in_{name}", v.shape, F32, kind="ExternalInput").ap())
    out = nc.dram_tensor("out_rows", (T, D), F32, kind="ExternalOutput").ap()
    two_layers(nc, *args, out)
    result = run_bass_kernel_spmd(nc, [feeds], core_ids=[0])
    return result.results[0]["out_rows"].reshape(B, TOK, D)
```
